# Optimizing a Trainium2 kernel written in Bass

```python
import numpy as np
import jax
import jax.numpy as jnp

def _softmax(x, axis=-1):
    return jax.nn.softmax(x, axis=axis)

def _gelu(x):
    return jax.nn.gelu(x, approximate=True)

def _silu(x):
    return jax.nn.silu(x)

def _sigmoid(x):
    return jax.nn.sigmoid(x)

def _layernorm(x, axis=-1, eps=1e-05):
    m = jnp.mean(x, axis=axis, keepdims=True)
    v = jnp.var(x, axis=axis, keepdims=True)
    return (x - m) / jnp.sqrt(v + eps)

def _scatter_add(tgt, idx, src, axis=0):
    return tgt.at[idx].add(src)

def _segment_sum(src, seg, n):
    return jax.ops.segment_sum(src, seg, n)
kernel_name = 'mk_adaln_d1_jaxref_r4_26d60f'

def setup_inputs(seed: int=0):
    np.random.seed(seed)
    _w = jnp.asarray

    def _L0_attn_setup():
        import jax, jax.numpy as jnp
        import numpy as np
        B, S, D = (4, 1024, 512)
        IDENTITY_WEIGHT = 0.5
        ROT_DIM = D // 2

        def _layernorm(x, gamma, beta, eps=1e-05):
            mu = jnp.mean(x, axis=-1, keepdims=True)
            var = jnp.var(x, axis=-1, keepdims=True)
            return (x - mu) * jax.lax.rsqrt(var + eps) * gamma + beta

        def _rotary(t, rot_dim, theta=10000.0):
            seq = t.shape[-2]
            inv_freq = 1.0 / theta ** (jnp.arange(0, rot_dim, 2, dtype=jnp.float32) / rot_dim)
            freqs = jnp.arange(seq, dtype=jnp.float32)[:, None] * inv_freq[None, :]
            freqs = jnp.repeat(freqs, 2, axis=-1)
            cos, sin = (jnp.cos(freqs), jnp.sin(freqs))
            t_rot, t_pass = (t[..., :rot_dim], t[..., rot_dim:])
            x1, x2 = (t_rot[..., 0::2], t_rot[..., 1::2])
            rot_half = jnp.stack([-x2, x1], axis=-1).reshape(t_rot.shape)
            return jnp.concatenate([t_rot * cos + rot_half * sin, t_pass], axis=-1)

        def _cos_sim(x):
            return x / jnp.linalg.norm(x, axis=-1, keepdims=True)
        key = jax.random.key(seed)
        ks = jax.random.split(key, 3)
        scale = 0.02
        return {'X': jax.random.normal(ks[0], (B, S, D), jnp.float32), 'W_in': jax.random.normal(ks[1], (D, 3 * D), jnp.float32) * scale, 'b_in': jnp.zeros((3 * D,), jnp.float32), 'W_out': jax.random.normal(ks[2], (D, D), jnp.float32) * scale, 'b_out': jnp.zeros((D,), jnp.float32), 'gamma': jnp.ones((D,), jnp.float32), 'beta': jnp.zeros((D,), jnp.float32)}
    _L0_attn_in = _L0_attn_setup()

    def _L0_ffn_setup():
        import jax, jax.numpy as jnp
        import numpy as np
        B, S, D = (4, 128, 512)
        E, K, H = (8, 2, 352)
        HS = 2 * 352
        ALPHA = 0.001
        W_SCALE = 0.02

        def _moe_forward(hidden_states, gate_w, w_gate, w_up, w_down, sw_gate, sw_up, sw_down):
            b, s, d = hidden_states.shape
            x = hidden_states.reshape(-1, d)
            T = x.shape[0]
            logits = x @ gate_w
            scores = jax.nn.softmax(logits, axis=-1)
            topk_w, topk_idx = jax.lax.top_k(scores, K)
            mask = jax.nn.one_hot(topk_idx, E, dtype=scores.dtype).sum(axis=1)
            ce = mask.mean(axis=0)
            Pi = scores.mean(axis=0)
            aux_loss = (Pi * ce * E).sum() * ALPHA
            comb = jnp.zeros((T, E), dtype=x.dtype)
            comb = comb.at[jnp.arange(T)[:, None], topk_idx].add(topk_w)
            g = jax.nn.silu(jnp.einsum('td,edh->teh', x, w_gate)) * jnp.einsum('td,edh->teh', x, w_up)
            routed = jnp.einsum('teh,ehd,te->td', g, w_down, comb)
            shared = jax.nn.silu(x @ sw_gate) * (x @ sw_up) @ sw_down
            out = (routed + shared).reshape(b, s, d)
            return (out, aux_loss)
        key = jax.random.key(seed)
        ks = jax.random.split(key, 8)
        rn = lambda k, sh: jax.random.normal(k, sh, dtype=jnp.float32)
        return {'hidden_states': rn(ks[0], (B, S, D)), 'gate_w': rn(ks[1], (D, E)) * W_SCALE, 'w_gate': rn(ks[2], (E, D, H)) * W_SCALE, 'w_up': rn(ks[3], (E, D, H)) * W_SCALE, 'w_down': rn(ks[4], (E, H, D)) * W_SCALE, 'sw_gate': rn(ks[5], (D, HS)) * W_SCALE, 'sw_up': rn(ks[6], (D, HS)) * W_SCALE, 'sw_down': rn(ks[7], (HS, D)) * W_SCALE}
    _L0_ffn_in = _L0_ffn_setup()
    _L0_c = _w((lambda *s: np.random.randn(*s).astype(np.float32) * 0.05)(2, 512))
    _L0_wmod = _w((lambda *s: np.random.randn(*s).astype(np.float32) * 0.05)(512, 6 * 512) * 512 ** (-0.5))
    _d = {'L0_attn_X': _L0_attn_in['X'], 'L0_attn_W_in': _L0_attn_in['W_in'], 'L0_attn_b_in': _L0_attn_in['b_in'], 'L0_attn_W_out': _L0_attn_in['W_out'], 'L0_attn_b_out': _L0_attn_in['b_out'], 'L0_attn_gamma': _L0_attn_in['gamma'], 'L0_attn_beta': _L0_attn_in['beta'], 'L0_ffn_gate_w': _L0_ffn_in['gate_w'], 'L0_ffn_w_gate': _L0_ffn_in['w_gate'], 'L0_ffn_w_up': _L0_ffn_in['w_up'], 'L0_ffn_w_down': _L0_ffn_in['w_down'], 'L0_ffn_sw_gate': _L0_ffn_in['sw_gate'], 'L0_ffn_sw_up': _L0_ffn_in['sw_up'], 'L0_ffn_sw_down': _L0_ffn_in['sw_down'], 'L0_c': _L0_c, 'L0_wmod': _L0_wmod}
    _x0 = _d['L0_attn_X']
    _d['L0_attn_X'] = jax.random.normal(jax.random.fold_in(jax.random.key(seed), 1), (2, 1024, 512), dtype=_x0.dtype)
    del _x0
    return _d

def reference(L0_attn_X, L0_attn_W_in, L0_attn_b_in, L0_attn_W_out, L0_attn_b_out, L0_attn_gamma, L0_attn_beta, L0_ffn_gate_w, L0_ffn_w_gate, L0_ffn_w_up, L0_ffn_w_down, L0_ffn_sw_gate, L0_ffn_sw_up, L0_ffn_sw_down, L0_c, L0_wmod):

    def _L0_attn_ref(X, W_in, b_in, W_out, b_out, gamma, beta):
        import jax, jax.numpy as jnp
        import numpy as np
        B, S, D = (4, 1024, 512)
        IDENTITY_WEIGHT = 0.5
        ROT_DIM = D // 2

        def _layernorm(x, gamma, beta, eps=1e-05):
            mu = jnp.mean(x, axis=-1, keepdims=True)
            var = jnp.var(x, axis=-1, keepdims=True)
            return (x - mu) * jax.lax.rsqrt(var + eps) * gamma + beta

        def _rotary(t, rot_dim, theta=10000.0):
            seq = t.shape[-2]
            inv_freq = 1.0 / theta ** (jnp.arange(0, rot_dim, 2, dtype=jnp.float32) / rot_dim)
            freqs = jnp.arange(seq, dtype=jnp.float32)[:, None] * inv_freq[None, :]
            freqs = jnp.repeat(freqs, 2, axis=-1)
            cos, sin = (jnp.cos(freqs), jnp.sin(freqs))
            t_rot, t_pass = (t[..., :rot_dim], t[..., rot_dim:])
            x1, x2 = (t_rot[..., 0::2], t_rot[..., 1::2])
            rot_half = jnp.stack([-x2, x1], axis=-1).reshape(t_rot.shape)
            return jnp.concatenate([t_rot * cos + rot_half * sin, t_pass], axis=-1)

        def _cos_sim(x):
            return x / jnp.linalg.norm(x, axis=-1, keepdims=True)
        Xn = _layernorm(X, gamma, beta)
        QKV = Xn @ W_in + b_in
        Q, K, V = jnp.split(QKV, 3, axis=-1)
        K = _rotary(K, ROT_DIM)
        V = _rotary(V, ROT_DIM)
        A = jnp.sum(_cos_sim(K) * _cos_sim(V), axis=-2)
        A = (1.0 - IDENTITY_WEIGHT) * A + IDENTITY_WEIGHT
        Y = A[:, None, :] * Q
        Y = Y @ W_out + b_out
        return Y + X

    def _L0_ffn_ref(hidden_states, gate_w, w_gate, w_up, w_down, sw_gate, sw_up, sw_down):
        import jax, jax.numpy as jnp
        import numpy as np
        B, S, D = (4, 128, 512)
        E, K, H = (8, 2, 352)
        HS = 2 * 352
        ALPHA = 0.001
        W_SCALE = 0.02

        def _moe_forward(hidden_states, gate_w, w_gate, w_up, w_down, sw_gate, sw_up, sw_down):
            b, s, d = hidden_states.shape
            x = hidden_states.reshape(-1, d)
            T = x.shape[0]
            logits = x @ gate_w
            scores = jax.nn.softmax(logits, axis=-1)
            topk_w, topk_idx = jax.lax.top_k(scores, K)
            mask = jax.nn.one_hot(topk_idx, E, dtype=scores.dtype).sum(axis=1)
            ce = mask.mean(axis=0)
            Pi = scores.mean(axis=0)
            aux_loss = (Pi * ce * E).sum() * ALPHA
            comb = jnp.zeros((T, E), dtype=x.dtype)
            comb = comb.at[jnp.arange(T)[:, None], topk_idx].add(topk_w)
            g = jax.nn.silu(jnp.einsum('td,edh->teh', x, w_gate)) * jnp.einsum('td,edh->teh', x, w_up)
            routed = jnp.einsum('teh,ehd,te->td', g, w_down, comb)
            shared = jax.nn.silu(x @ sw_gate) * (x @ sw_up) @ sw_down
            out = (routed + shared).reshape(b, s, d)
            return (out, aux_loss)
        out, _aux = _moe_forward(hidden_states, gate_w, w_gate, w_up, w_down, sw_gate, sw_up, sw_down)
        return out
    x = L0_attn_X
    mod = (_silu(L0_c) @ L0_wmod).reshape(L0_c.shape[0], 6, 1, -1)
    sa, ca, ga, sb, cb, gb = (mod[:, 0], mod[:, 1], mod[:, 2], mod[:, 3], mod[:, 4], mod[:, 5])
    ga = (2 * (ga >= 0) - 1) * jnp.maximum(jnp.abs(ga), 0.25)
    gb = (2 * (gb >= 0) - 1) * jnp.maximum(jnp.abs(gb), 0.25)
    h = _layernorm(x, axis=-1) * (1 + ca) + sa
    x = x + ga * _L0_attn_ref(h, L0_attn_W_in, L0_attn_b_in, L0_attn_W_out, L0_attn_b_out, L0_attn_gamma, L0_attn_beta)
    h = _layernorm(x, axis=-1) * (1 + cb) + sb
    x = x + gb * _L0_ffn_ref(h, L0_ffn_gate_w, L0_ffn_w_gate, L0_ffn_w_up, L0_ffn_w_down, L0_ffn_sw_gate, L0_ffn_sw_up, L0_ffn_sw_down)
    return x

_drawn_inputs = setup_inputs


def setup_inputs(seed=0):
    import zlib

    import numpy as np

    out = dict(_drawn_inputs(seed))
    spreads = {'L0_attn_b_in': (0.0, 0.8),
     'L0_attn_b_out': (0.0, 0.345),
     'L0_attn_gamma': (1.0, 0.6),
     'L0_attn_beta': (0.0, 0.8)}
    factors = {'L0_ffn_gate_w': 8.0,
     'L0_ffn_w_gate': 8.0,
     'L0_ffn_w_up': 8.0,
     'L0_ffn_w_down': 8.0,
     'L0_ffn_sw_gate': 4.108,
     'L0_ffn_sw_up': 4.017,
     'L0_ffn_sw_down': 4.02}
    for name, (base, spread) in spreads.items():
        noise = np.random.default_rng([zlib.crc32(name.encode()), seed]).standard_normal(out[name].shape)
        drawn = base * np.exp(spread * noise) if base else spread * noise
        out[name] = jnp.asarray(drawn.astype(out[name].dtype))
    for name, factor in factors.items():
        out[name] = (out[name] * factor).astype(out[name].dtype)
    return out
```

```python
import numpy as np
import concourse.bass as bass
from concourse import mybir
from contextlib import ExitStack

F32, F32R, I32 = mybir.dt.float32, mybir.dt.float32r, mybir.dt.int32
ALU, ACT, AX = mybir.AluOpType, mybir.ActivationFunctionType, mybir.AxisListType

P = 128
B, S, D = 2, 1024, 512
T = B * S
NT = T // P
GT = 4
GN = GT * P
NG = T // GN
DC = D // P
ROT = D // 2
EPS = 1e-5
E, H, HS = 8, 352, 704
SM = [min(P, HS - P * m) for m in range(-(-HS // P))]
RM = [min(P, H - P * m) for m in range(-(-H // P))]
NS, NR = len(SM), len(RM)
CT = 5
CAP = CT * P
ROUNDS = -(-T // CAP)
COLS = ROUNDS * E * CT
TCOLS = COLS + CT
HALF = CAP // 2
EW = 2 * DC * H + NR * D

MOD = ["sa", "ca", "ga", "sb", "cb", "gb"]
WEIGHTS = ["sa", "ca", "K", "V", "ga", "sb", "cb", "Q", "O", "gb"]
PIECES = [(w, h) for w in WEIGHTS for h in range(2)]
PIECES += [(w, k) for k in range(DC) for w in ("sgate", "sup")]
PIECES += [("sdown", k) for k in range(NS // 2)]
MODS = [w for w in WEIGHTS if w in MOD]
SPLITS = [p for p in PIECES if p[0] not in MOD]


def build(nc, X, W_in, b_in, W_out, b_out, gamma, beta, gate_w, w_gate, w_up, w_down,
          sw_gate, sw_up, sw_down, c, wmod, cos_t, sin_t, out):
    def dram(name, shape, dt=F32):
        return nc.dram_tensor(name, shape, dt, kind="Internal").ap()

    mod_d = dram("mod_d", [B, 6 * D])
    base_d = dram("base_d", [T, D])
    x2_d = dram("x2_d", [T, D])
    h2_d = dram("h2_d", [T, D])
    slot_d = dram("slot_d", [P * COLS, 2], I32)

    ctx = ExitStack()
    with ctx:
        ctx.enter_context(nc.allow_non_contiguous_dma(reason="vectors of a few hundred values"))

        def sem(name):
            return ctx.enter_context(nc.semaphore(name))

        def region(stack):
            return lambda name, shape, dt=F32: stack.enter_context(nc.sbuf_tensor(name, shape, dt))

        sb = region(ctx)

        with ExitStack() as r_phase:
            al = region(r_phase)
            ew0 = al("ew0", [P, 2, EW], F32R)
            ht0 = al("ht0", [P, 2, DC, CAP], F32R)
            picked = al("picked", [P, CT, D])
        xt = sb("xt", [P, NG, 2, DC, GN], F32R)
        with ExitStack() as a1_phase:
            al = region(a1_phase)
            wkv = al("wkv", [P, 2, 2, DC, D], F32R)
            cos = al("cos", [P, S])
            sin = al("sin", [P, S])
            sq = al("sq", [P, 2, GN])
        with ExitStack() as r_phase:
            ew1 = region(r_phase)("ew1", [P, 2, EW], F32R)
        sgu = sb("sgu", [P, 2, 2, DC, HS], F32R)
        bc_s = sb("bc_s", [P, B, D])
        bc_c = sb("bc_c", [P, B, D])
        bc_ga = sb("bc_ga", [P, B, D])
        bc_gb = sb("bc_gb", [P, B, D])
        bout, mabs = bc_gb[:, 0, :], bc_gb[0:B, 1, :]
        ident = sb("ident", [P, P])
        ones = sb("ones", [P, P])
        upper = sb("upper", [P, P])
        nhalf = sb("nhalf", [P, 2 * GT])
        cT = sb("cT", [P, DC, B])
        scT = sb("scT", [P, DC, B])
        gb_col = sb("gb_col", [P, 2, DC])
        b_col = sb("b_col", [P, 3, DC])
        a_part = sb("a_part", [P, NG, DC])
        a_col = sb("a_col", [P, B, 2, DC])
        st6 = sb("st6", [P, GT, 6])
        mv = sb("mv", [P, GT, 2])
        ve = sb("ve", [P, GT])
        rs = sb("rs", [P, GT])
        nrm = sb("nrm", [P, GT, 2])
        rnm = sb("rnm", [P, GT, 2])
        wtok = sb("wtok", [P, GT])
        gw = sb("gw", [P, DC, E])
        lg = sb("lg", [P, NT, E])
        cntf = sb("cntf", [P, 2])
        loops = sb("loops", [P, 1], I32)
        gi = sb("gi", [P, 2, CT], I32)
        si = sb("si", [P, 2, CT], I32)
        wc = sb("wc", [P, 2, 2, CT])
        begin = sb("begin", [P, 5])
        with ExitStack() as a_phase:
            al = region(a_phase)
            wq = al("wq", [P, 2, DC, D], F32R)
            wo = al("wo", [P, 2, DC, D], F32R)
            with ExitStack() as a1_phase:
                al1 = region(a1_phase)
                atmp = al1("atmp", [P, 2, GN])
                kv = al1("kv", [P, 5, GN])
                rk = al1("rk", [P, 2, GN])
                rv = al1("rv", [P, 2, GN])
                mrow = al1("mrow", [B, D])
            qa = al("qa", [P, 2, DC, GN], F32R)
            tmp = al("tmp", [P, DC, GN])
            stage = al("stage", [P, 2, 2 * D])
            rows = al("rows", [P, GT, D])
            hx = al("hx", [P, GT, D])
        with ExitStack() as s_phase:
            al = region(s_phase)
            with ExitStack() as r_phase:
                al2 = region(r_phase)
                gtR = al2("gtR", [P, 2, NR, CAP], F32R)
                y = al2("y", [P, CT, D])
                gsel = al2("gsel", [P, CT, D])
                ht1 = al2("ht1", [P, 2, DC, CAP], F32R)
            sd = al("sd", [P, 2, NS, D], F32R)
            gtS = al("gtS", [P, 2, NS, GN], F32R)
            xrow = al("xrow", [P, 2, D])
            srow = al("srow", [P, 2, D])
            with ExitStack() as routing:
                al2 = region(routing)
                iota8 = al2("iota8", [P, NT, E])
                sc = al2("sc", [P, NT, E])
                eq = al2("eq", [P, NT, E])
                oh = al2("oh", [P, 2, NT, E])
                both = al2("both", [P, NT, E])
                within = al2("within", [P, NT, E])
                upto = al2("upto", [P, 3, NT, E])
                mx = al2("mx", [P, 2, NT, 1])
                wt = al2("wt", [P, 2, NT, 1])
                ix = al2("ix", [P, 2, NT, 1])
                rr = al2("rr", [P, 2, NT, 1])
                rd = al2("rd", [P, 2, NT, 1])
                qq = al2("qq", [P, 2, NT, 1])
                sl = al2("sl", [P, 2, NT, 1])
                sidx = al2("sidx", [P, 2 * NT], I32)
                rec = al2("rec", [P, 2, NT, 2], I32)
            ewst = al("ewst", [P, 2, NR * D])
            tab = al("tab", [P, TCOLS, 2], I32)
            w01 = al("w01", [P, 2, TCOLS])
            gidx = al("gidx", [P, TCOLS], I32)
        gbuf = [a[:, 0, :] for a in (bc_s, bc_c, bc_ga)]

        modrow = [mrow[:, :]] * 5 + [sq[0:B, 0, :]]

        bank = [ctx.enter_context(nc.psum_tensor(f"bank{i}", [P, GN], F32)) for i in range(8)]
        T_BANKS, KV_BANKS, NORM_BANK, W_BANK = (0, 1), (2, 3, 4, 5), 6, 7
        GATE_BANKS, UP_BANKS, DOWN_BANKS, RT_BANKS = (2, 4), (3, 5), (6, 7), (0, 1)
        Q_BANKS, Y_BANKS, T2_BANKS, LG_BANK = (2, 3, 4), (6, 7), (0, 5), 1

        consts = sem("consts")
        small_in = sem("small_in")
        c_in = sem("c_in")
        sc_ready = sem("sc_ready")
        piece_in = [sem(f"piece_in{i}") for i in range(2)]
        mod_mm, mod_row, mod_out, bc_in = sem("mod_mm"), sem("mod_row"), sem("mod_out"), sem("bc_in")
        bout_in = sem("bout_in")
        hi_done, lo_done = sem("hi_done"), sem("lo_done")
        x_in = [sem(f"x_in{j}") for j in range(GT)]
        dve_step, pool_step, act_step = sem("dve_step"), sem("pool_step"), sem("act_step")
        ve_ready, rs_ready = sem("ve_ready"), sem("rs_ready")
        h_ready, h_read, base_ready = sem("h_ready"), sem("h_read"), sem("base_ready")
        base_out = [sem(f"base_out{j}") for j in range(GT)]
        xn_ready, t_mm, t_hi, t_lo = sem("xn_ready"), sem("t_mm"), sem("t_hi"), sem("t_lo")
        kv_mm, kv_copied, sq_ready, sq_mm = sem("kv_mm"), sem("kv_copied"), sem("sq_ready"), sem("sq_mm")
        v_turned, prod, nrm_ready, w_ready = sem("v_turned"), sem("prod"), sem("nrm_ready"), sem("w_ready")
        w_mm, a_done, a_ready = sem("w_mm"), sem("a_done"), sem("a_ready")
        q_mm, qa_hi, qa_lo, y_mm = sem("q_mm"), sem("qa_hi"), sem("qa_lo"), sem("y_mm")
        base_in = [sem(f"base_in{j}") for j in range(GT)]
        x2_ready, h2_half, h2_ready = sem("x2_ready"), sem("h2_half"), sem("h2_ready")
        x2_out = [sem(f"x2_out{j}") for j in range(GT)]
        h2_out = [sem(f"h2_out{j}") for j in range(GT)]
        t2_mm, t2_hi, t2_lo, lg_mm = sem("t2_mm"), sem("t2_hi"), sem("t2_lo"), sem("lg_mm")

        slot0_out, slot_out, tab_in = sem("slot0_out"), sem("slot_out"), sem("tab_in")
        pad_in, tab_ready = sem("pad_in"), sem("tab_ready")
        lg_ready, exp_ready = sem("lg_ready"), sem("exp_ready")
        both_ready, rank_mm, rank_read = sem("both_ready"), sem("rank_mm"), sem("rank_read")
        slots_ready, loops_ready, cols_ready = sem("slots_ready"), sem("loops_ready"), sem("cols_ready")
        s_gu_mm, s_silu, s_mul, s_hi, s_lo = sem("s_gu_mm"), sem("s_silu"), sem("s_mul"), sem("s_hi"), sem("s_lo")
        s_down_mm, s_row = sem("s_down_mm"), sem("s_row")
        x2_in = [sem(f"x2_in{i}") for i in range(2)]
        s_out = [sem(f"s_out{i}") for i in range(2)]
        ew_in = [sem(f"ew_in{q}") for q in range(3)]
        ew_hi, ew_lo = sem("ew_hi"), sem("ew_lo")
        idx_ready, picked_in = sem("idx_ready"), sem("picked_in")
        wc_ready, gs_ready, gsel_ready = sem("wc_ready"), sem("gs_ready"), sem("gsel_ready")
        rt_mm, rt_hi, rt_lo = sem("rt_mm"), sem("rt_hi"), sem("rt_lo")
        gu_mm, r_silu, r_mul, r_hi, r_lo = sem("gu_mm"), sem("r_silu"), sem("r_mul"), sem("r_hi"), sem("r_lo")
        down_mm, y_ready, y_out, added = sem("down_mm"), sem("y_ready"), sem("y_out"), sem("added")

        ew, ht = (ew0, ew1), (ht0, ht1)
        EW_PART = [(0, DC * H), (DC * H, 2 * DC * H), (2 * DC * H, EW)]

        def arrived(eng, n):
            eng.wait_ge(piece_in[n % 2], 16 * (n // 2 + 1 + (n == len(PIECES) - 1)))

        def tile_rows(ap, t):
            return ap[t * P:(t + 1) * P, :]

        KV_ORDER = [(0, 0), (0, 1), (1, 0), (1, 1), (0, 2), (1, 2), (0, 3), (1, 3)]
        KV_SLOT = [0, 1, 2, 3, 2, 3, 4, 3]

        def split_views(n, part):
            w, h = PIECES[n]
            src = stage[:, n % 2, :]
            if w in ("sgate", "sup"):
                return [(sgu[:, part, w == "sup", h, :], src[:, 0:HS])]
            if w == "sdown":
                return [(sd[0:SM[m], part, m, :], src[0:SM[m], (m % 2) * D:(m % 2 + 1) * D]) for m in (2 * h, 2 * h + 1)]
            ks = slice(2 * h, 2 * h + 2)
            src = src.rearrange("p (k n) -> p k n", k=2)
            if w == "O":
                return [(wo[:, part, ks, :], src)]
            dst = wq[:, part, ks, :] if w == "Q" else wkv[:, part, w == "V", ks, :]
            return [(dst[:, :, 0:ROT].rearrange("p k (two f) -> p k two f", two=2),
                     src[:, :, 0:ROT].rearrange("p k (f two) -> p k two f", two=2)),
                    (dst[:, :, ROT:D], src[:, :, ROT:D])]

        block = ctx.enter_context(nc.Block())

        @block.sync
        def _(sp):
            def load_piece(n):
                if n >= 2:
                    w, h = PIECES[n - 2]
                    if w in MOD:
                        sp.wait_ge(mod_mm, 2 * MODS.index(w) + h + 1)
                    else:
                        sp.wait_ge(lo_done, SPLITS.index(PIECES[n - 2]) + 1)
                w, h = PIECES[n]
                dst = stage[:, n % 2, :]
                half = slice(2 * h * P, 2 * (h + 1) * P)
                if w in ("sgate", "sup"):
                    src = (sw_gate if w == "sgate" else sw_up)[h * P:(h + 1) * P, :]
                    sp.dma_start(dst[:, 0:HS], src).then_inc(piece_in[n % 2], 16)
                    return
                if w == "sdown":
                    at = 2 * h * P
                    dst = dst.rearrange("p (k n) -> p k n", k=2)
                    if n < len(PIECES) - 1:
                        sp.dma_start(dst, sw_down[at:at + 2 * P, :].rearrange("(k p) n -> p k n", k=2))\
                            .then_inc(piece_in[n % 2], 16)
                    else:
                        sp.dma_start(dst[:, 0, :], sw_down[at:at + P, :]).then_inc(piece_in[n % 2], 16)
                        sp.dma_start(dst[0:SM[-1], 1, :], sw_down[at + P:HS, :]).then_inc(piece_in[n % 2], 16)
                    return
                dst = dst.rearrange("p (k n) -> p k n", k=2)
                if w == "O" and h == 0:
                    src = W_out[0:ROT, :].rearrange("(p k) n -> p k n", k=2)
                elif w == "O":
                    src = W_out[half, :].rearrange("(k p) n -> p k n", k=2)
                else:
                    col = D * ("Q", "K", "V").index(w) if w in "QKV" else D * MOD.index(w)
                    src = (W_in if w in "QKV" else wmod)[half, col:col + D].rearrange("(k p) n -> p k n", k=2)
                sp.dma_start(dst, src).then_inc(piece_in[n % 2], 16)

            def load_x(t):
                if t >= GT:
                    sp.wait_ge(base_out[t % GT], 16 * (t // GT))
                sp.dma_start(rows[:, t % GT, :], tile_rows(X, t)).then_inc(x_in[t % GT], 16)

            def store_base(t):
                sp.wait_ge(base_ready, t + 1)
                sp.dma_start(tile_rows(base_d, t), rows[:, t % GT, :]).then_inc(base_out[t % GT], 16)

            def store_mod(i):
                col = D * MOD.index(MODS[i])
                sp.wait_ge(mod_row, i + 1)
                sp.dma_start(mod_d[:, col:col + D], modrow[i]).then_inc(mod_out, 16)

            def spread_mod(i):
                w = MODS[i]
                col = D * MOD.index(w)
                sp.wait_ge(mod_out, 16 * (i + 1))
                dst = {"sa": bc_s, "ca": bc_c, "ga": bc_ga, "sb": bc_s, "cb": bc_c, "gb": bc_gb}[w]
                if w in ("sb", "cb", "gb"):
                    sp.wait_ge(h_ready, NT)
                    sp.wait_ge(h_read, NT)
                sp.dma_start(dst[:, :, :], mod_d[:, col:col + D].partition_broadcast(P)).then_inc(bc_in, 16)

            for b in range(B):
                sp.dma_start(cT[:, :, b], c[b, :].rearrange("(k p) -> p k", p=P)).then_inc(c_in, 16)
            for n in range(2):
                load_piece(n)
            for t in range(GT):
                load_x(t)
            for n in range(2, 4):
                load_piece(n)
            sp.dma_start(gb_col[:, 0, :], gamma.rearrange("(k p) -> p k", p=P)).then_inc(small_in, 16)
            sp.dma_start(gb_col[:, 1, :], beta.rearrange("(k p) -> p k", p=P)).then_inc(small_in, 16)
            for i, part in enumerate((1, 2, 0)):
                seg = b_in[part * D:(part + 1) * D]
                sp.dma_start(b_col[:, i, 0:2], seg[0:ROT].rearrange("(p k) -> p k", k=2)).then_inc(small_in, 16)
                sp.dma_start(b_col[:, i, 2:4], seg[ROT:D].rearrange("(k p) -> p k", p=P)).then_inc(small_in, 16)
            sp.dma_start(gw[:, :, :], gate_w.rearrange("(k p) e -> p k e", p=P)).then_inc(small_in, 16)
            sp.dma_start(cos[:, :], cos_t).then_inc(small_in, 16)
            sp.dma_start(sin[:, :], sin_t).then_inc(small_in, 16)
            sp.dma_start(bout, b_out.partition_broadcast(P)).then_inc(bout_in, 16)
            for i in range(2):
                store_mod(i)
                spread_mod(i)
            for n in range(4, 10):
                load_piece(n)
            store_mod(2)
            spread_mod(2)
            load_piece(10)
            load_piece(11)
            for t in range(2 * GT):
                store_base(t)
                load_x(GT + t)
            store_mod(3)
            load_piece(12)
            load_piece(13)
            for t in range(2 * GT, 3 * GT):
                store_base(t)
                load_x(GT + t)
            store_mod(4)
            for n in range(14, 18):
                load_piece(n)
            for t in range(3 * GT, NT):
                store_base(t)
            spread_mod(3)
            spread_mod(4)
            load_piece(18)
            load_piece(19)
            store_mod(5)
            spread_mod(5)

            def load_base(t):
                j = t % GT
                sp.wait_ge(base_out[j], 16 * NG)
                if t >= GT:
                    sp.wait_ge(x2_out[j], 16 * (t // GT))
                    sp.wait_ge(h2_half, t - GT + 1)
                sp.dma_start(rows[:, j, :], tile_rows(base_d, t)).then_inc(base_in[j], 16)

            for t in range(GT):
                load_base(t)
            load_piece(20)
            load_piece(21)
            for g in range(NG):
                for j in range(GT):
                    t = g * GT + j
                    sp.wait_ge(x2_ready, t + 1)
                    sp.dma_start(tile_rows(x2_d, t), rows[:, j, :]).then_inc(x2_out[j], 16)
                load_piece(22 + 2 * g)
                load_piece(23 + 2 * g)
                for j in range(GT):
                    t = g * GT + j
                    if g + 1 < NG:
                        load_base(t + GT)
                    sp.wait_ge(h2_ready, t + 1)
                    sp.dma_start(tile_rows(h2_d, t), hx[:, j, :]).then_inc(h2_out[j], 16)
                if g == 0:
                    sp.dma_start(out[T:T + CAP, :], X[0:CAP, :]).then_inc(pad_in, 16)
            load_piece(30)
            sp.wait_ge(tab_ready, 1)
            sp.dma_start(slot_d.rearrange("(p c) two -> p c two", p=P), tab[:, 0:COLS, :]).then_inc(slot0_out, 16)

            def load_x2(t):
                if t >= 2:
                    sp.wait_ge(s_out[t % 2], 16 * (t // 2))
                sp.wait_ge(x2_out[t % GT], 16 * (t // GT + 1))
                sp.dma_start(xrow[:, t % 2, :], tile_rows(x2_d, t)).then_inc(x2_in[t % 2], 16)

            def store_s(t):
                sp.wait_ge(s_row, t + 1)
                sp.dma_start(tile_rows(out, t), xrow[:, t % 2, :]).then_inc(s_out[t % 2], 16)
                if t + 2 < NT:
                    load_x2(t + 2)

            def load_expert(w, par, pieces=range(3)):
                e = w % E if isinstance(w, int) else sp.snap(w % E)
                before = None if isinstance(w, int) else [sp.snap(3 * w + q - 1) for q in range(3)]
                for q in pieces:
                    slot = (par + q) % 2
                    if before:
                        sp.wait_ge(ew_lo, before[q])
                    elif q == 2:
                        sp.wait_ge(ew_lo, 1)
                    if q < 2:
                        src = (w_gate, w_up)[q][bass.ds(e, 1), :, :].rearrange("e (k p) n -> p (e k) n", p=P)
                        dst = ewst[:, slot, 0:DC * H].rearrange("p (k n) -> p k n", k=DC)
                        sp.dma_start(dst, src).then_inc(ew_in[q], 16)
                    else:
                        full = H // P
                        dst = ewst[:, slot, 0:full * D].rearrange("p (k n) -> p k n", k=full)
                        src = w_down[bass.ds(e, 1), 0:full * P, :].rearrange("e (k p) n -> p (e k) n", p=P)
                        sp.dma_start(dst, src).then_inc(ew_in[q], 16)
                        sp.dma_start(ewst[0:RM[-1], slot, full * D:NR * D],
                                     w_down[bass.ds(e, 1), full * P:H, :].rearrange("e p n -> p (e n)"))\
                            .then_inc(ew_in[q], 16)

            sp.wait_ge(t2_lo, NT)
            sp.wait_ge(lg_mm, NG)
            load_x2(0)
            load_x2(1)
            for t in range(NT):
                if t == 2 * GT:
                    sp.wait_ge(slot_out, 16 * 2 * NT)
                    sp.dma_start(tab[:, 0:COLS, :], slot_d.rearrange("(p c) two -> p c two", p=P)).then_inc(tab_in, 16)
                    sp.wait_ge(lo_done, len(SPLITS))
                    load_expert(0, 0, (0, 1))
                if t == 3 * GT:
                    load_expert(0, 0, (2,))
                store_s(t)
            sp.wait_ge(loops_ready, 1)
            n = nc.sync.value_load(loops[0:1, 0:1], min_val=E // 2, max_val=ROUNDS * E // 2)
            with sp.Fori(0, n) as i:
                for par in range(2):
                    load_expert(2 * i + par + 1, 1 - par)

        @block.gpsimd
        def _(pool):
            steps = [0]

            def link(ins):
                steps[0] += 1
                ins.then_inc(pool_step, 1)
                pool.wait_ge(pool_step, steps[0])

            for i, begun in enumerate((added, y_ready, down_mm, r_lo, r_mul)):
                pool.memset(begin[:, i:i + 1], 0.0).then_inc(begun, 1)
            pool.memset(ones[:, :], 1.0).then_inc(consts, 1)
            pool.memset(nhalf[:, :], -0.5).then_inc(consts, 1)
            link(pool.memset(ident[:, :], 0.0))
            pool.affine_select(out=ident[:, :], in_=ident[:, :], compare_op=ALU.not_equal, fill=1.0,
                               base=0, pattern=[[-1, P]], channel_multiplier=1).then_inc(consts, 1)
            pool.wait_ge(consts, 3)
            pool.affine_select(out=upper[:, :], in_=ones[:, :], compare_op=ALU.is_gt, fill=0.0,
                               base=0, pattern=[[1, P]], channel_multiplier=-1).then_inc(consts, 1)

            def norm_power(n):
                pool.wait_ge(ve_ready, n + 1)
                pool.tensor_tensor(rs[:, :], ve[:, :], nhalf[:, 0:GT], ALU.pow).then_inc(rs_ready, 1)

            def base_rows(g):
                b = g // (NG // B)

                def add_bias(j):
                    pool.wait_ge(h_ready, GT * g + j + 1)
                    pool.tensor_tensor(rv[:, j % 2, :], hx[:, j, :], bout, ALU.add).then_inc(h_read, 1)

                def finish(j):
                    pool.wait_ge(h_read, GT * g + j + 1)
                    link(pool.tensor_tensor(rv[:, j % 2, :], rv[:, j % 2, :], bc_ga[:, b, :], ALU.mult))
                    pool.tensor_tensor(rows[:, j, :], rows[:, j, :], rv[:, j % 2, :], ALU.add)\
                        .then_inc(base_ready, 1)

                add_bias(0)
                add_bias(1)
                norm_power(2 * g + 1)
                finish(0)
                pool.wait_ge(base_ready, GT * g + 1)
                add_bias(2)
                finish(1)
                pool.wait_ge(base_ready, GT * g + 2)
                add_bias(3)
                finish(2)
                finish(3)

            def turn_v(g):
                at = slice((g * GN) % S, (g * GN) % S + GN)
                pool.wait_ge(kv_copied, 8 * g + 4)
                pool.wait_ge(base_ready, min(GT * (g + 2), NT))
                pool.tensor_tensor(rv[:, 0, :], kv[:, 2, :], cos[:, at], ALU.mult)
                link(pool.tensor_tensor(rv[:, 1, :], kv[:, 3, :], sin[:, at], ALU.mult))
                pool.tensor_tensor(kv[:, 2, :], kv[:, 2, :], sin[:, at], ALU.mult)
                link(pool.tensor_tensor(kv[:, 3, :], kv[:, 3, :], cos[:, at], ALU.mult))
                link(pool.tensor_tensor(kv[:, 3, :], kv[:, 2, :], kv[:, 3, :], ALU.add))
                pool.tensor_tensor(kv[:, 2, :], rv[:, 0, :], rv[:, 1, :], ALU.subtract).then_inc(v_turned, 1)

            def token_weights(g):
                pool.wait_ge(nrm_ready, g + 1)
                if g:
                    pool.wait_ge(w_mm, g)
                link(pool.tensor_tensor(rnm[:, :, :], nrm[:, :, :], nhalf[:, :].rearrange("p (t k) -> p t k", k=2), ALU.pow))
                pool.tensor_tensor(wtok[:, :], rnm[:, :, 0], rnm[:, :, 1], ALU.mult).then_inc(w_ready, 1)

            pool.wait_ge(bout_in, 16)
            pool.wait_ge(small_in, 16 * 11)
            norm_power(0)
            pool.wait_ge(bc_in, 16 * 3)
            base_rows(0)
            for g in range(NG):
                if g + 1 < NG:
                    norm_power(2 * g + 2)
                    base_rows(g + 1)
                turn_v(g)
                token_weights(g)

            pool.wait_ge(bc_in, 16 * 5)
            for g in range(NG):
                norm_power(2 * NG + g)
                for j in range(GT):
                    pool.wait_ge(h2_half, GT * g + j + 1)
                    pool.tensor_tensor(hx[:, j, :], hx[:, j, :], bc_s[:, g // 2, :], ALU.add).then_inc(h2_ready, 1)

            for j in range(GT):
                pool.wait_ge(x2_out[j], 16 * NG)
            pool.wait_ge(lo_done, len(SPLITS))
            pool.iota(tab[:, :, 0], pattern=[[0, TCOLS // CT], [P, CT]], base=T, channel_multiplier=1)
            pool.memset(tab[:, :, 1], 0)
            pool.iota(rec[:, :, :, 0], pattern=[[0, 2], [P, NT]], base=0, channel_multiplier=1)
            pool.iota(iota8[:, :, :], pattern=[[0, NT], [1, E]], base=-E, channel_multiplier=0,
                      allow_small_or_imprecise_dtypes=True)
            pool.drain().then_inc(tab_ready, 1)

            pool.wait_ge(slots_ready, 1)
            pool.wait_ge(slot0_out, 16)
            for n in range(2 * NT):
                pool.indirect_dma_start(out=slot_d, out_offset=bass.IndirectOffsetOnAxis(ap=sidx[:, n:n + 1], axis=0),
                                        in_=rec[:, n // NT, n % NT, :], in_offset=None).then_inc(slot_out, 16)

            def gather(w, par):
                if not isinstance(w, int):
                    pool.wait_ge(rt_mm, CT * w)
                pool.tensor_copy(gi[:, par, :], gidx[:, bass.ds(w * CT, CT)]).then_inc(idx_ready, 1)
                pool.tensor_copy(si[:, par, :], tab[:, bass.ds(w * CT, CT), 0]).then_inc(idx_ready, 1)
                pool.wait_ge(idx_ready, 2 * w + 2)
                pool.nop(nofuse=True)
                for j in range(CT):
                    pool.indirect_dma_start(out=picked[:, j, :], out_offset=None, in_=h2_d,
                                            in_offset=bass.IndirectOffsetOnAxis(ap=gi[:, par, j:j + 1], axis=0))\
                        .then_inc(picked_in, 16)

            def scatter(u, par):
                for j in range(CT):
                    pool.wait_ge(y_ready, CT * u + j + 1 + 1)
                    pool.nop(nofuse=True)
                    pool.indirect_dma_start(out=out, out_offset=bass.IndirectOffsetOnAxis(ap=si[:, par, j:j + 1], axis=0),
                                            in_=y[:, j, :], in_offset=None, compute_op=ALU.add).then_inc(y_out, 16)
                pool.wait_ge(y_out, 16 * CT * (u + 1))
                pool.nop(nofuse=True).then_inc(added, 1)

            pool.wait_ge(cols_ready, 1)
            pool.wait_ge(s_gu_mm, NS * NG)
            for j in range(GT):
                pool.wait_ge(h2_out[j], 16 * NG)
            gather(0, 0)
            pool.wait_ge(pad_in, 16)
            for i in range(2):
                pool.wait_ge(s_out[i], 16 * NT // 2)
            pool.wait_ge(loops_ready, 1)
            n = nc.gpsimd.value_load(loops[0:1, 0:1], min_val=E // 2, max_val=ROUNDS * E // 2)
            with pool.Fori(0, n) as i:
                for par in range(2):
                    gather(2 * i + par + 1, 1 - par)
                    scatter(2 * i + par, par)

        @block.scalar
        def _(act):
            def split_hi(n):
                w, h = PIECES[n]
                arrived(act, n)
                for dst, src in split_views(n, 0):
                    last = nc.scalar.activation(dst, src, ACT.Copy)
                last.then_inc(hi_done, 1)

            def transposed(g):
                for k in range(DC):
                    n = DC * g + k
                    act.wait_ge(t_mm, n + 1)
                    if n >= 2:
                        act.wait_ge(t_lo, n - 1)
                    src = bank[T_BANKS[k % 2]][:, :]
                    nc.scalar.activation(atmp[:, k % 2, :], src, ACT.Identity,
                                         bias=gb_col[:, 1, k:k + 1], scale=gb_col[:, 0, k:k + 1])
                    nc.scalar.activation(xt[:, g, 0, k, :], src, ACT.Identity, bias=gb_col[:, 1, k:k + 1],
                                         scale=gb_col[:, 0, k:k + 1]).then_inc(t_hi, 1)

            def copy_kv(g, n):
                i, m = KV_ORDER[n]
                N = 8 * g + n
                act.wait_ge(kv_mm, N + 1)
                if n < 4 and g:
                    act.wait_ge(a_done, DC * g)
                if n >= 4:
                    act.wait_ge(prod, DC * g + (1, 2, 2, 3)[n - 4])
                bias = b_col[:, i, m:m + 1]
                src = bank[KV_BANKS[n % 4]][:, :]
                nc.scalar.activation(kv[:, KV_SLOT[n], :], src, ACT.Identity, bias=bias).then_inc(kv_copied, 1)
                if N >= 2:
                    act.wait_ge(sq_mm, N - 1)
                nc.scalar.activation(sq[:, n % 2, :], src, ACT.Square, bias=bias).then_inc(sq_ready, 1)

            act.wait_ge(c_in, 16 * B)
            nc.scalar.activation(scT[:, :, :], cT[:, :, :], ACT.Silu).then_inc(sc_ready, 1)
            for n in range(4, 8):
                split_hi(n)
            act.wait_ge(small_in, 16 * 11)
            transposed(0)
            for g in range(NG):
                for n in range(6):
                    copy_kv(g, n)
                if g + 1 < NG:
                    transposed(g + 1)
                copy_kv(g, 6)
                copy_kv(g, 7)
                if g == 1:
                    for n in range(14, 18):
                        split_hi(n)

            def scaled_q(g):
                b = g // 2
                act.wait_ge(a_ready, b + 1)
                for m in range(DC):
                    act.wait_ge(q_mm, DC * g + m + 1)
                    if g == 0:
                        act.wait_ge(t_lo, NT)
                        act.wait_ge(a_done, NT)
                    else:
                        act.wait_ge(y_mm, GT * g)
                        act.wait_ge(lg_mm, g)
                        act.wait_ge(t2_lo, DC * g)
                    src = bank[Q_BANKS[(DC * g + m) % 3]][:, :]
                    col = dict(bias=a_col[:, b, 1, m:m + 1], scale=a_col[:, b, 0, m:m + 1])
                    nc.scalar.activation(tmp[:, m, :], src, ACT.Identity, **col)
                    nc.scalar.activation(qa[:, 0, m, :], src, ACT.Identity, **col).then_inc(qa_hi, 1)

            def transposed2(g):
                for k in range(DC):
                    n = DC * g + k
                    act.wait_ge(t2_mm, n + 1)
                    src = bank[T2_BANKS[k % 2]][:, :]
                    if k == 0:
                        act.wait_ge(qa_lo, DC * (g + 1))
                    nc.scalar.activation(tmp[:, k, :], src, ACT.Copy)
                    nc.scalar.activation(xt[:, g, 0, k, :], src, ACT.Copy).then_inc(t2_hi, 1)

            def s_silu_of(g, m):
                n = NS * g + m
                r = SM[m]
                act.wait_ge(s_gu_mm, n + 1)
                if n >= 3:
                    act.wait_ge(s_lo, n - 2)
                nc.scalar.activation(gbuf[n % 3][0:r, :], bank[GATE_BANKS[m % 2]][0:r, :], ACT.Silu).then_inc(s_silu, 1)

            def s_hi_of(g, m):
                n = NS * g + m
                r = SM[m]
                act.wait_ge(s_mul, n + 1)
                if g:
                    act.wait_ge(s_down_mm, GT * g)
                nc.scalar.activation(gtS[0:r, 0, m, :], gbuf[n % 3][0:r, :], ACT.Copy).then_inc(s_hi, 1)

            def shared(g):
                for m in range(NS):
                    s_silu_of(g, m)
                    if m:
                        s_hi_of(g, m - 1)
                    if g == 0 and m >= 3:
                        split_hi(25 + m)
                s_hi_of(g, NS - 1)

            def expert_hi(w, par, q):
                lo, hi = EW_PART[q]
                slot = (par + q) % 2
                act.wait_ge(ew_in[q], (16 if q < 2 else 32) * (w + 1))
                if not isinstance(w, int):
                    act.wait_ge(down_mm, CT * (w - 1) + 1)
                if q < 2:
                    nc.scalar.activation(ew[par][:, 0, lo:hi], ewst[:, slot, 0:hi - lo], ACT.Copy).then_inc(ew_hi, 1)
                    return
                full = H // P * D
                nc.scalar.activation(ew[par][:, 0, lo:lo + full], ewst[:, slot, 0:full], ACT.Copy)
                nc.scalar.activation(ew[par][0:RM[-1], 0, lo + full:hi], ewst[0:RM[-1], slot, full:NR * D], ACT.Copy)\
                    .then_inc(ew_hi, 1)

            def picked_hi(w, par):
                for s in range(CT):
                    act.wait_ge(rt_mm, CT * w + s + 1)
                    src = bank[RT_BANKS[(par + s) % 2]]
                    if s < DC:
                        nc.scalar.activation(ht[par][:, 0, s, 0:GN], src[:, :], ACT.Copy).then_inc(rt_hi, 1)
                    else:
                        nc.scalar.activation(ht[par][:, 0, :, GN:CAP], src[:, :].rearrange("p (k t) -> p k t", k=DC),
                                             ACT.Copy).then_inc(rt_hi, 1)

            def select_gb(u, par, j):
                if j == 0:
                    act.wait_ge(wc_ready, u + 1)
                    act.wait_ge(y_ready, CT * u + 1)
                nc.scalar.activation(gsel[:, j, :], bc_gb[:, 1, :], ACT.Copy, scale=wc[:, par, 1, j:j + 1])\
                    .then_inc(gs_ready, 1)

            def r_silu_of(u, par, c):
                half, m = divmod(c, NR)
                r = RM[m]
                act.wait_ge(gu_mm, 2 * NR * u + c + 1)
                act.wait_ge(r_lo, 2 * NR * u + max(c - 2, 0) + 1)
                nc.scalar.activation(gbuf[c % 3][0:r, 0:HALF], bank[GATE_BANKS[c % 2]][0:r, 0:HALF], ACT.Silu)\
                    .then_inc(r_silu, 1)

            def r_hi_of(u, par, c):
                half, m = divmod(c, NR)
                r = RM[m]
                act.wait_ge(r_mul, 2 * NR * u + c + 1 + 1)
                if c == 0:
                    act.wait_ge(down_mm, CT * u + 1)
                nc.scalar.activation(gtR[0:r, 0, m, half * HALF:(half + 1) * HALF], gbuf[c % 3][0:r, 0:HALF],
                                     ACT.Copy)\
                    .then_inc(r_hi, 1)

            act.wait_ge(a_done, NT)
            act.wait_ge(sq_mm, 8 * NG)
            scaled_q(0)
            for g in range(NG):
                for n in range(20 + 2 * g, 22 + 2 * g):
                    split_hi(n)
                if g == NG - 1:
                    shared(0)
                transposed2(g)
                if g + 1 < NG:
                    scaled_q(g + 1)

            act.wait_ge(lg_ready, 1)
            nc.scalar.activation(sc[:, :, :], sc[:, :, :], ACT.Exp).then_inc(exp_ready, 1)
            shared(1)
            shared(2)
            expert_hi(0, 0, 0)
            expert_hi(0, 0, 1)
            shared(3)
            expert_hi(0, 0, 2)
            for i in range(2):
                act.wait_ge(s_out[i], 16 * NT // 2)
            picked_hi(0, 0)
            act.wait_ge(loops_ready, 1)
            n = nc.scalar.value_load(loops[0:1, 0:1], min_val=E // 2, max_val=ROUNDS * E // 2)
            nc.scalar.preload_act_table(ACT.Silu)
            with act.Fori(0, n) as i:
                for par in range(2):
                    u = 2 * i + par
                    for c in range(2 * NR):
                        r_silu_of(u, par, c)
                        if c:
                            r_hi_of(u, par, c - 1)
                        if c % 2 == 1:
                            expert_hi(u + 1, 1 - par, c // 2)
                        if c < CT:
                            select_gb(u, par, c)
                    r_hi_of(u, par, 2 * NR - 1)
                    picked_hi(u + 1, 1 - par)

        @block.vector
        def _(dve):
            steps = [0]

            def link(ins):
                steps[0] += 1
                ins.then_inc(dve_step, 1)
                dve.wait_ge(dve_step, steps[0])

            def split_lo(n):
                i = SPLITS.index(PIECES[n])
                arrived(dve, n)
                dve.wait_ge(hi_done, i + 1)
                his = split_views(n, 0)
                for (dst, src), (hi, _) in zip(split_views(n, 1), his):
                    last = dve.tensor_tensor(dst, src, hi.bitcast(F32), ALU.subtract)
                last.then_inc(lo_done, 1)

            def mod_vector(i):
                w = MODS[i]
                row = modrow[i]
                src = bank[W_BANK][0:B, :]
                dve.wait_ge(mod_mm, 2 * i + 2)
                if i:
                    dve.wait_ge(mod_out, 16 * i)
                if w in ("sa", "sb"):
                    dve.tensor_copy(row, src).then_inc(mod_row, 1)
                elif w in ("ca", "cb"):
                    dve.tensor_scalar_add(row, src, 1.0).then_inc(mod_row, 1)
                else:
                    link(dve.tensor_copy(row, src))
                    link(dve.scalar_tensor_tensor(mabs, row, -1.0, row, ALU.mult, ALU.max))
                    dve.tensor_scalar(row, row, 0.0, 2.0, ALU.is_ge, ALU.mult)
                    link(dve.tensor_scalar_max(mabs, mabs, 0.25))
                    dve.scalar_tensor_tensor(row, row, -1.0, mabs, ALU.add, ALU.mult)\
                        .then_inc(mod_row, 1)

            def variance(n, src):
                for j in range(GT):
                    last = dve.bn_stats(st6[:, j, :], src[:, j, :])
                link(last)
                for j in range(GT):
                    last = dve.bn_aggr(mv[:, j, :], st6[:, j, :])
                link(last)
                dve.tensor_scalar_add(ve[:, :], mv[:, :, 1], EPS).then_inc(ve_ready, 1)
                dve.wait_ge(rs_ready, n + 1)

            def norm_rows(j, src):
                return dve.tensor_scalar(hx[:, j, :], src[:, j, :], mv[:, j, 0:1], rs[:, j:j + 1],
                                         ALU.subtract, ALU.mult)

            def first_norm(g):
                b = g // (NG // B)
                for j in range(GT):
                    dve.wait_ge(x_in[j], 16 * (g + 1))
                variance(2 * g, rows)
                if g:
                    dve.wait_ge(t_mm, DC * g)
                for j in range(GT):
                    last = norm_rows(j, rows)
                link(last)
                if g == 0:
                    dve.wait_ge(bc_in, 16 * 2)
                for j in range(GT):
                    last = dve.tensor_tensor(hx[:, j, :], hx[:, j, :], bc_c[:, b, :], ALU.mult)
                link(last)
                for j in range(GT):
                    dve.tensor_tensor(hx[:, j, :], hx[:, j, :], bc_s[:, b, :], ALU.add).then_inc(h_ready, 1)
                dve.wait_ge(h_ready, GT * (g + 1))
                variance(2 * g + 1, hx)

            def second_norm(g):
                for j in range(GT):
                    dve.wait_ge(h_read, GT * g + j + 1)
                    norm_rows(j, hx).then_inc(xn_ready, 1)

            def transposed_lo(g):
                for k in range(DC):
                    dve.wait_ge(t_hi, DC * g + k + 1)
                    dve.tensor_tensor(xt[:, g, 1, k, :], atmp[:, k % 2, :], xt[:, g, 0, k, :].bitcast(F32),
                                      ALU.subtract).then_inc(t_lo, 1)

            def turn_k(g):
                at = slice((g * GN) % S, (g * GN) % S + GN)
                dve.wait_ge(kv_copied, 8 * g + 2)
                dve.tensor_tensor(rk[:, 0, :], kv[:, 0, :], cos[:, at], ALU.mult)
                link(dve.tensor_tensor(rk[:, 1, :], kv[:, 1, :], sin[:, at], ALU.mult))
                dve.tensor_tensor(kv[:, 0, :], kv[:, 0, :], sin[:, at], ALU.mult)
                link(dve.tensor_tensor(kv[:, 1, :], kv[:, 1, :], cos[:, at], ALU.mult))
                link(dve.tensor_tensor(kv[:, 1, :], kv[:, 0, :], kv[:, 1, :], ALU.add))
                link(dve.tensor_tensor(kv[:, 0, :], rk[:, 0, :], rk[:, 1, :], ALU.subtract))
                dve.wait_ge(v_turned, g + 1)
                dve.tensor_tensor(kv[:, 0, :], kv[:, 0, :], kv[:, 2, :], ALU.mult).then_inc(prod, 1)
                dve.tensor_tensor(kv[:, 1, :], kv[:, 1, :], kv[:, 3, :], ALU.mult).then_inc(prod, 1)

            def product(g, m):
                dve.wait_ge(kv_copied, 8 * g + 2 * m + 2)
                s = (0, 0, 2, 4)[m]
                dve.tensor_tensor(kv[:, s, :], kv[:, s, :], kv[:, 3, :], ALU.mult).then_inc(prod, 1)

            def sum_products(g):
                dve.wait_ge(w_mm, g + 1)
                dve.wait_ge(prod, DC * (g + 1))
                for m in range(DC):
                    weighted = kv[:, (0, 1, 2, 4)[m], :]
                    dve.tensor_tensor_reduce(out=weighted, in0=weighted,
                                             in1=bank[W_BANK][:, :], scale=1.0, scalar=0.0, op0=ALU.mult,
                                             op1=ALU.add, accum_out=a_part[:, g, m:m + 1]).then_inc(a_done, 1)

            def finish_a(b):
                n = NG // B
                dve.wait_ge(a_done, DC * n * (b + 1))
                link(dve.tensor_tensor(a_col[:, b, 0, :], a_part[:, n * b, :], a_part[:, n * b + 1, :], ALU.add))
                link(dve.tensor_scalar(a_col[:, b, 0, :], a_col[:, b, 0, :], 0.5, 0.5, ALU.mult, ALU.add))
                dve.tensor_tensor(a_col[:, b, 1, :], a_col[:, b, 0, :], b_col[:, 2, :], ALU.mult).then_inc(a_ready, 1)

            mod_vector(0)
            mod_vector(1)
            for n in range(4, 8):
                split_lo(n)
            mod_vector(2)
            dve.wait_ge(small_in, 16 * 11)
            first_norm(0)
            second_norm(0)
            transposed_lo(0)
            for g in range(NG):
                if g:
                    sum_products(g - 1)
                if g == 2:
                    finish_a(0)
                if g + 1 < NG:
                    first_norm(g + 1)
                turn_k(g)
                if g + 1 < NG:
                    second_norm(g + 1)
                product(g, 2)
                if g + 1 < NG:
                    transposed_lo(g + 1)
                product(g, 3)
                dve.wait_ge(sq_mm, 8 * (g + 1))
                if g:
                    dve.wait_ge(w_ready, g)
                dve.tensor_copy(nrm[:, :, :], bank[NORM_BANK][:, 0:2 * GT].rearrange("p (t k) -> p t k", k=2))\
                    .then_inc(nrm_ready, 1)
                if g < 2:
                    mod_vector(3 + g)
                if g == 1:
                    for n in range(14, 18):
                        split_lo(n)
            sum_products(NG - 1)
            finish_a(1)
            mod_vector(5)

            def qa_lo_parts(g):
                for m in range(DC):
                    dve.wait_ge(qa_hi, DC * g + m + 1)
                    dve.tensor_tensor(qa[:, 1, m, :], tmp[:, m, :], qa[:, 0, m, :].bitcast(F32), ALU.subtract)\
                        .then_inc(qa_lo, 1)

            def residual_norm(g):
                b = g // (NG // B)
                for j in range(GT):
                    t = GT * g + j
                    dve.wait_ge(y_mm, t + 1)
                    if g:
                        dve.wait_ge(t2_mm, DC * g)
                        dve.wait_ge(h2_out[j], 16 * g)
                    link(dve.tensor_tensor(hx[:, j, :], bank[Y_BANKS[t % 2]][:, :], bc_ga[:, b, :], ALU.mult))
                    dve.wait_ge(base_in[j], 16 * (g + 1))
                    dve.tensor_tensor(rows[:, j, :], rows[:, j, :], hx[:, j, :], ALU.add).then_inc(x2_ready, 1)
                dve.wait_ge(x2_ready, GT * (g + 1))
                variance(2 * NG + g, rows)
                for j in range(GT):
                    last = norm_rows(j, rows)
                link(last)
                for j in range(GT):
                    dve.tensor_tensor(hx[:, j, :], hx[:, j, :], bc_c[:, b, :], ALU.mult).then_inc(h2_half, 1)

            def s_mul_of(g, m):
                n = NS * g + m
                r = SM[m]
                dve.wait_ge(s_silu, n + 1)
                dve.tensor_tensor(gbuf[n % 3][0:r, :], gbuf[n % 3][0:r, :], bank[UP_BANKS[m % 2]][0:r, :], ALU.mult)\
                    .then_inc(s_mul, 1)

            def s_lo_of(g, m):
                n = NS * g + m
                r = SM[m]
                dve.wait_ge(s_hi, n + 1)
                dve.tensor_tensor(gtS[0:r, 1, m, :], gbuf[n % 3][0:r, :], gtS[0:r, 0, m, :].bitcast(F32), ALU.subtract)\
                    .then_inc(s_lo, 1)

            def shared(g):
                for m in range(NS):
                    s_mul_of(g, m)
                    if m:
                        s_lo_of(g, m - 1)
                    if g == 0 and m >= 3:
                        split_lo(25 + m)
                s_lo_of(g, NS - 1)

            def shared_rows(g):
                b = g // (NG // B)
                for j in range(GT):
                    t = GT * g + j
                    dve.wait_ge(s_down_mm, t + 1)
                    link(dve.tensor_tensor(srow[:, t % 2, :], bank[DOWN_BANKS[t % 2]][:, :], bc_gb[:, b, :], ALU.mult))
                    dve.wait_ge(x2_in[t % 2], 16 * (t // 2 + 1))
                    dve.tensor_tensor(xrow[:, t % 2, :], xrow[:, t % 2, :], srow[:, t % 2, :], ALU.add).then_inc(s_row, 1)

            full_e = [P, NT, E]

            def gate_scores():
                dve.wait_ge(lg_mm, NG)
                link(dve.tensor_copy(lg[:, :, :], bank[LG_BANK][:, 0:NT * E].rearrange("p (t e) -> p t e", e=E)))
                link(dve.tensor_reduce(mx[:, 0, :, 0], lg[:, :, :], AX.X, ALU.max))
                dve.tensor_tensor(sc[:, :, :], lg[:, :, :], mx[:, 0, :, :].to_broadcast(full_e), ALU.subtract)\
                    .then_inc(lg_ready, 1)

            def top_two():
                dve.wait_ge(exp_ready, 1)
                dve.wait_ge(tab_ready, 1)
                link(dve.tensor_reduce(mx[:, 0, :, 0], sc[:, :, :], AX.X, ALU.add))
                link(dve.reciprocal(mx[:, 1, :, 0], mx[:, 0, :, 0]))
                link(dve.tensor_tensor(sc[:, :, :], sc[:, :, :], mx[:, 1, :, :].to_broadcast(full_e), ALU.mult))
                for k in range(2):
                    link(dve.tensor_reduce(wt[:, k, :, 0], sc[:, :, :], AX.X, ALU.max))
                    link(dve.tensor_tensor(eq[:, :, :], sc[:, :, :], wt[:, k, :, :].to_broadcast(full_e), ALU.is_equal))
                    link(dve.tensor_tensor(eq[:, :, :], eq[:, :, :], iota8[:, :, :], ALU.mult))
                    link(dve.tensor_reduce(ix[:, k, :, 0], eq[:, :, :], AX.X, ALU.min))
                    link(dve.tensor_tensor(oh[:, k, :, :], iota8[:, :, :], ix[:, k, :, :].to_broadcast(full_e), ALU.is_equal))
                    if k == 0:
                        link(dve.scalar_tensor_tensor(sc[:, :, :], oh[:, 0, :, :], -2.0, sc[:, :, :], ALU.mult, ALU.add))
                dve.tensor_tensor(both[:, :, :], oh[:, 0, :, :], oh[:, 1, :, :], ALU.add).then_inc(both_ready, 1)

            def slots():
                dve.wait_ge(rank_mm, 1)
                src = bank[LG_BANK][:, NT * E:3 * NT * E].rearrange("p (i t e) -> p i t e", i=2, e=E)
                dve.tensor_copy(within[:, :, :], src[:, 0, :, :])
                link(dve.tensor_copy(upto[:, 0, :, :], src[:, 1, :, :]))
                dve.tensor_copy(upto[:, 1, :, :], upto[:, 0, :, :]).then_inc(rank_read, 1)
                dve.wait_ge(rank_read, 1)
                at, step = 1, 1
                while step < NT:
                    dve.tensor_copy(upto[:, 3 - at, 0:step, :], upto[:, at, 0:step, :])
                    link(dve.tensor_tensor(upto[:, 3 - at, step:NT, :], upto[:, at, step:NT, :],
                                           upto[:, at, 0:NT - step, :], ALU.add))
                    at, step = 3 - at, 2 * step
                link(dve.tensor_reduce(cntf[:, 0:1], upto[:, at, NT - 1, :], AX.X, ALU.max))
                link(dve.tensor_single_scalar(cntf[:, 1:2], cntf[:, 0:1], float(CAP), ALU.is_gt))
                for r in range(2, ROUNDS):
                    link(dve.scalar_tensor_tensor(cntf[:, 1:2], cntf[:, 0:1], float(CAP * r), cntf[:, 1:2], ALU.is_gt, ALU.add))
                link(dve.tensor_scalar(cntf[:, 1:2], cntf[:, 1:2], E / 2, E / 2, ALU.mult, ALU.add))
                dve.tensor_copy(loops[:, :], cntf[:, 1:2]).then_inc(loops_ready, 1)
                link(dve.tensor_tensor(upto[:, 0, :, :], upto[:, at, :, :], upto[:, 0, :, :], ALU.subtract))
                link(dve.tensor_tensor(within[:, :, :], within[:, :, :], upto[:, 0, :, :], ALU.add))
                for k in range(2):
                    link(dve.tensor_tensor(upto[:, 1 + k, :, :], oh[:, k, :, :], within[:, :, :], ALU.mult))
                    link(dve.tensor_reduce(rr[:, k, :, 0], upto[:, 1 + k, :, :], AX.X, ALU.add))

                def flat(a):
                    return a[:, :, :, :].rearrange("p k t o -> p (k t o)")

                link(dve.tensor_single_scalar(flat(rd), flat(rr), float(CAP), ALU.is_ge))
                for r in range(2, ROUNDS):
                    link(dve.scalar_tensor_tensor(flat(rd), flat(rr), float(CAP * r), flat(rd), ALU.is_ge, ALU.add))
                link(dve.scalar_tensor_tensor(flat(rr), flat(rd), -float(CAP), flat(rr), ALU.mult, ALU.add))
                link(dve.tensor_single_scalar(flat(qq), flat(rr), float(P), ALU.is_ge))
                for r in range(2, CT):
                    link(dve.scalar_tensor_tensor(flat(qq), flat(rr), float(P * r), flat(qq), ALU.is_ge, ALU.add))
                link(dve.scalar_tensor_tensor(flat(rr), flat(qq), -float(P), flat(rr), ALU.mult, ALU.add))
                link(dve.tensor_scalar(flat(sl), flat(ix), float(CT), float(E * CT), ALU.mult, ALU.add))
                link(dve.scalar_tensor_tensor(flat(sl), flat(rd), float(E * CT), flat(sl), ALU.mult, ALU.add))
                link(dve.tensor_tensor(flat(sl), flat(sl), flat(qq), ALU.add))
                link(dve.scalar_tensor_tensor(flat(sl), flat(rr), float(COLS), flat(sl), ALU.mult, ALU.add))
                link(dve.tensor_copy(sidx[:, :], flat(sl)))
                dve.tensor_copy(rec[:, :, :, :].bitcast(F32)[:, :, :, 1], wt[:, :, :, 0]).then_inc(slots_ready, 1)

            def columns():
                dve.wait_ge(tab_in, 16)
                bits = tab[:, :, :].bitcast(F32)[:, :, 1]
                dve.tensor_scalar_min(gidx[:, :], tab[:, :, 0], T - 1)
                dve.scalar_tensor_tensor(w01[:, 0, :], tab[:, :, 0], float(S), bits, ALU.is_lt, ALU.mult)
                link(dve.scalar_tensor_tensor(w01[:, 1, :], tab[:, :, 0], float(S), bits, ALU.is_ge, ALU.mult))
                dve.drain().then_inc(cols_ready, 1)

            def expert_lo(w, par, q):
                lo, hi = EW_PART[q]
                slot = (par + q) % 2
                dve.wait_ge(ew_hi, 3 * w + q + 1)
                parts = [(P, lo, hi, 0)]
                if q == 2:
                    full = H // P * D
                    parts = [(P, lo, lo + full, 0), (RM[-1], lo + full, hi, full)]
                for r, a, z, at in parts:
                    last = dve.tensor_tensor(ew[par][0:r, 1, a:z], ewst[0:r, slot, at:at + z - a],
                                             ew[par][0:r, 0, a:z].bitcast(F32), ALU.subtract)
                last.then_inc(ew_lo, 1)

            def picked_lo(w, par):
                for s in range(CT):
                    dve.wait_ge(rt_hi, CT * w + s + 1)
                    src = bank[RT_BANKS[(par + s) % 2]][:, :]
                    at = (slice(s, s + 1), slice(0, GN)) if s < DC else (slice(0, DC), slice(GN, CAP))
                    src = src.rearrange("p (k t) -> p k t", k=1 if s < DC else DC)
                    dve.tensor_tensor(ht[par][:, 1, at[0], at[1]], src, ht[par][:, 0, at[0], at[1]].bitcast(F32),
                                      ALU.subtract).then_inc(rt_lo, 1)

            def turn_columns(w, par):
                dve.tensor_copy(wc[:, par, :, :], w01[:, :, bass.ds(w * CT, CT)]).then_inc(wc_ready, 1)

            def select_gb(u, par, j):
                dve.wait_ge(gs_ready, CT * u + j + 1)
                dve.scalar_tensor_tensor(gsel[:, j, :], bc_gb[:, 0, :], wc[:, par, 0, j:j + 1], gsel[:, j, :],
                                         ALU.mult, ALU.add).then_inc(gsel_ready, 1)

            def r_mul_of(u, c):
                half, m = divmod(c, NR)
                r = RM[m]
                dve.wait_ge(r_silu, 2 * NR * u + c + 1)
                dve.tensor_tensor(gbuf[c % 3][0:r, 0:HALF], gbuf[c % 3][0:r, 0:HALF], bank[UP_BANKS[c % 2]][0:r, 0:HALF], ALU.mult)\
                    .then_inc(r_mul, 1)

            def r_lo_of(u, c):
                half, m = divmod(c, NR)
                r, at = RM[m], slice(half * HALF, (half + 1) * HALF)
                dve.wait_ge(r_hi, 2 * NR * u + c + 1)
                dve.tensor_tensor(gtR[0:r, 1, m, at], gbuf[c % 3][0:r, 0:HALF], gtR[0:r, 0, m, at].bitcast(F32), ALU.subtract)\
                    .then_inc(r_lo, 1)

            def expert_rows(u, j, par):
                dve.wait_ge(down_mm, CT * u + j + 1 + 1)
                if j == 0:
                    dve.wait_ge(gsel_ready, CT * u + CT)
                    dve.wait_ge(added, u + 1)
                dve.tensor_tensor(y[:, j, :], bank[DOWN_BANKS[(par + j) % 2]][:, :], gsel[:, j, :], ALU.mult)\
                    .then_inc(y_ready, 1)

            qa_lo_parts(0)
            dve.wait_ge(bc_in, 16 * 5)
            for g in range(NG):
                for n in range(20 + 2 * g, 22 + 2 * g):
                    split_lo(n)
                residual_norm(g)
                if g == NG - 1:
                    shared(0)
                for k in range(DC):
                    dve.wait_ge(t2_hi, DC * g + k + 1)
                    dve.tensor_tensor(xt[:, g, 1, k, :], tmp[:, k, :], xt[:, g, 0, k, :].bitcast(F32),
                                      ALU.subtract).then_inc(t2_lo, 1)
                if g + 1 < NG:
                    qa_lo_parts(g + 1)

            gate_scores()
            dve.wait_ge(bc_in, 16 * 6)
            shared_rows(0)
            top_two()
            shared(1)
            slots()
            shared_rows(1)
            shared(2)
            shared_rows(2)
            columns()
            expert_lo(0, 0, 0)
            expert_lo(0, 0, 1)
            shared(3)
            expert_lo(0, 0, 2)
            shared_rows(3)
            picked_lo(0, 0)
            turn_columns(0, 0)
            for i in range(2):
                dve.wait_ge(s_out[i], 16 * NT // 2)
            dve.wait_ge(loops_ready, 1)
            n = nc.vector.value_load(loops[0:1, 0:1], min_val=E // 2, max_val=ROUNDS * E // 2)
            with dve.Fori(0, n) as i:
                for par in range(2):
                    u = 2 * i + par
                    for c in range(2 * NR):
                        r_mul_of(u, c)
                        if c:
                            r_lo_of(u, c - 1)
                        if c % 2 == 1:
                            expert_lo(u + 1, 1 - par, c // 2)
                        if c < CT:
                            select_gb(u, par, c)
                    r_lo_of(u, 2 * NR - 1)
                    picked_lo(u + 1, 1 - par)
                    turn_columns(u + 1, 1 - par)
                    for j in range(CT):
                        expert_rows(u, j, par)

        @block.tensor
        def _(pe):
            def product3(dst, a, b, first, last):
                nc.tensor.matmul(dst, a[0], b[0], start=first, stop=False)
                nc.tensor.matmul(dst, a[0], b[1], start=False, stop=False)
                return nc.tensor.matmul(dst, a[1], b[0], start=False, stop=last)

            def mod_matmul(i):
                w = MODS[i]
                if i:
                    pe.wait_ge(mod_row, i)
                if i > 3:
                    pe.wait_ge(a_done, DC if i == 4 else NT)
                for h in range(2):
                    n = PIECES.index((w, h))
                    arrived(pe, n)
                    for k in range(2):
                        last = nc.tensor.matmul(bank[W_BANK][0:B, :], scT[:, 2 * h + k, :], stage[:, n % 2, k * D:(k + 1) * D],
                                                start=h + k == 0, stop=h + k == 2)
                    last.then_inc(mod_mm, 1)

            def transposes(g):
                pe.wait_ge(xn_ready, GT * (g + 1))
                for k in range(DC):
                    n = DC * g + k
                    if n >= 2:
                        pe.wait_ge(t_hi, n - 1)
                    for j in range(GT):
                        last = nc.tensor.transpose(bank[T_BANKS[k % 2]][:, j * P:(j + 1) * P],
                                                   hx[:, j, k * P:(k + 1) * P], ident[:, :])
                    last.then_inc(t_mm, 1)

            def kv_matmul(g, n):
                i, m = KV_ORDER[n]
                N = 8 * g + n
                if n == 0:
                    pe.wait_ge(t_lo, DC * (g + 1))
                if N >= 4:
                    pe.wait_ge(sq_ready, N - 3)
                for k in range(DC):
                    last = product3(bank[KV_BANKS[n % 4]][:, :],
                                    [wkv[:, s, i, k, m * P:(m + 1) * P] for s in range(2)],
                                    [xt[:, g, s, k, :] for s in range(2)], k == 0, k == DC - 1)
                last.then_inc(kv_mm, 1)

            def square_sums(g, n):
                i, m = KV_ORDER[n]
                pe.wait_ge(sq_ready, 8 * g + n + 1)
                if n == 0 and g:
                    pe.wait_ge(nrm_ready, g)
                for j in range(GT):
                    last = nc.tensor.matmul(bank[NORM_BANK][:, 2 * j + i:2 * j + i + 1], sq[:, n % 2, j * P:(j + 1) * P],
                                            ones[:, 0:1], start=n == 0 and j == 0, stop=n == 7 and j == GT - 1,
                                            skip_group_check=True)
                last.then_inc(sq_mm, 1)

            def spread_weights(g):
                pe.wait_ge(w_ready, g + 1)
                pe.wait_ge(mod_row, min(4 + g, 5))
                if g:
                    pe.wait_ge(a_done, DC * g)
                for j in range(GT):
                    last = nc.tensor.matmul(bank[W_BANK][:, j * P:(j + 1) * P], wtok[:, j:j + 1].to_broadcast([P, P]),
                                            ident[:, :], start=True, stop=True)
                last.then_inc(w_mm, 1)

            def q_matmul(g, chunks=range(DC)):
                for m in chunks:
                    n = DC * g + m
                    if n >= 3:
                        pe.wait_ge(qa_hi, n - 2)
                    for k in range(DC):
                        last = product3(bank[Q_BANKS[n % 3]][:, :], [wq[:, s, k, m * P:(m + 1) * P] for s in range(2)],
                                        [xt[:, g, s, k, :] for s in range(2)], k == 0, k == DC - 1)
                    last.then_inc(q_mm, 1)

            pe.wait_ge(consts, 4)
            pe.wait_ge(sc_ready, 1)
            for i in range(3):
                mod_matmul(i)
            transposes(0)
            pe.wait_ge(lo_done, 4)
            for g in range(NG):
                for n in range(8):
                    kv_matmul(g, n)
                    if n == 0 and g:
                        spread_weights(g - 1)
                    if n:
                        square_sums(g, n - 1)
                    if n == 5 and g + 1 < NG:
                        transposes(g + 1)
                if g == 0:
                    mod_matmul(3)
                if g == 1:
                    mod_matmul(4)
                if g == NG - 1:
                    pe.wait_ge(lo_done, 8)
                    pe.wait_ge(sq_ready, 8 * NG)
                    q_matmul(0, range(3))
                square_sums(g, 7)
            spread_weights(NG - 1)
            q_matmul(0, range(3, DC))
            mod_matmul(5)

            def shared_gate_up(g):
                for m in range(NS):
                    n, r = NS * g + m, SM[m]
                    if n >= 2:
                        pe.wait_ge(s_mul, n - 1)
                    for i, to in enumerate((GATE_BANKS, UP_BANKS)):
                        for k in range(DC):
                            last = product3(bank[to[m % 2]][0:r, :], [sgu[:, s, i, k, m * P:m * P + r] for s in range(2)],
                                            [xt[:, g, s, k, :] for s in range(2)], k == 0, k == DC - 1)
                    last.then_inc(s_gu_mm, 1)

            def shared_down(g):
                for pair in range(GT // 2):
                    for chunks in (range(NS - 1), range(NS - 1, NS)):
                        for j in (2 * pair, 2 * pair + 1):
                            t = GT * g + j
                            if chunks[0] == 0 and t >= 2:
                                pe.wait_ge(s_row, t - 1)
                            for m in chunks:
                                if j == 0 or m == NS - 1:
                                    pe.wait_ge(s_lo, NS * g + m + 1)
                                r = SM[m]
                                last = product3(bank[DOWN_BANKS[t % 2]][:, :],
                                                [gtS[0:r, s, m, j * P:(j + 1) * P] for s in range(2)],
                                                [sd[0:r, s, m, :] for s in range(2)], m == 0, m == NS - 1)
                            if chunks[0]:
                                last.then_inc(s_down_mm, 1)

            def turn_rows(w, par):
                pe.wait_ge(picked_in, 16 * CT * (w + 1))
                for s in range(CT):
                    if not isinstance(w, int) or s >= 2:
                        pe.wait_ge(rt_lo, CT * w + s - 1)
                    for i in range(DC):
                        j, k = (i, s) if s < DC else (DC, i)
                        last = nc.tensor.transpose(bank[RT_BANKS[(par + s) % 2]][:, i * P:(i + 1) * P],
                                                   picked[:, j, k * P:(k + 1) * P], ident[:, :])
                    last.then_inc(rt_mm, 1)

            def expert_gate_up(u, par):
                for c in range(2 * NR):
                    half, m = divmod(c, NR)
                    r, at = RM[m], slice(half * HALF, (half + 1) * HALF)
                    if c == 0:
                        pe.wait_ge(rt_lo, CT * u + CT)
                        pe.wait_ge(ew_lo, 3 * u + 2)
                    pe.wait_ge(r_mul, 2 * NR * u + max(c - 1, 0) + 1)
                    for i, to in enumerate((GATE_BANKS, UP_BANKS)):
                        for k in range(DC):
                            col = (i * DC + k) * H + m * P
                            last = product3(bank[to[c % 2]][0:r, 0:HALF], [ew[par][:, s, col:col + r] for s in range(2)],
                                            [ht[par][:, s, k, at] for s in range(2)], k == 0, k == DC - 1)
                    last.then_inc(gu_mm, 1)

            def expert_down(u, par):
                pe.wait_ge(ew_lo, 3 * u + 3)
                for j in range(CT):
                    if j == 0:
                        pe.wait_ge(r_lo, 2 * NR * u + NR + 1)
                    if j == 2:
                        pe.wait_ge(r_lo, 2 * NR * (u + 1) + 1)
                    pe.wait_ge(y_ready, CT * u + max(j - 1, 0) + 1)
                    for m in range(NR):
                        r, col = RM[m], 2 * DC * H + m * D
                        last = product3(bank[DOWN_BANKS[(par + j) % 2]][:, :],
                                        [gtR[0:r, s, m, j * P:(j + 1) * P] for s in range(2)],
                                        [ew[par][0:r, s, col:col + D] for s in range(2)], m == 0, m == NR - 1)
                    last.then_inc(down_mm, 1)

            for g in range(NG):
                pe.wait_ge(qa_lo, DC * (g + 1))
                for j in range(GT):
                    t = GT * g + j
                    if t >= 2:
                        pe.wait_ge(x2_ready, t - 1)
                    for m in range(DC):
                        last = product3(bank[Y_BANKS[t % 2]][:, :], [qa[:, s, m, j * P:(j + 1) * P] for s in range(2)],
                                        [wo[:, s, m, :] for s in range(2)], m == 0, m == DC - 1)
                    last.then_inc(y_mm, 1)
                if g + 1 < NG:
                    q_matmul(g + 1, range(3))
                else:
                    pe.wait_ge(lo_done, SPLITS.index(("sup", DC - 1)) + 1)
                    shared_gate_up(0)
                    pe.wait_ge(s_mul, NS)
                pe.wait_ge(h2_ready, GT * (g + 1))
                for k in range(DC):
                    n = DC * g + k
                    if n >= 2:
                        pe.wait_ge(t2_hi, n - 1)
                    for j in range(GT):
                        last = nc.tensor.transpose(bank[T2_BANKS[k % 2]][:, j * P:(j + 1) * P],
                                                   hx[:, j, k * P:(k + 1) * P], ident[:, :])
                    last.then_inc(t2_mm, 1)
                pe.wait_ge(t2_hi, DC * (g + 1))
                for j in range(GT):
                    t = GT * g + j
                    for k in range(DC):
                        last = nc.tensor.matmul(bank[LG_BANK][:, t * E:(t + 1) * E], tmp[:, k, j * P:(j + 1) * P],
                                                gw[:, k, :], start=k == 0, stop=k == DC - 1)
                last.then_inc(lg_mm, 1)
                if g + 1 < NG:
                    q_matmul(g + 1, range(3, DC))

            pe.wait_ge(lo_done, len(SPLITS))
            for g in range(NG):
                if g:
                    if g == NG - 1:
                        pe.wait_ge(t2_lo, NT)
                    shared_gate_up(g)
                if g == 1:
                    pe.wait_ge(both_ready, 1)
                    for i, lhs in enumerate((upper, ones)):
                        last = nc.tensor.matmul(bank[LG_BANK][:, (1 + i) * NT * E:(2 + i) * NT * E], lhs[:, :],
                                                both[:, :, :].rearrange("p t e -> p (t e)"), start=True, stop=True)
                    last.then_inc(rank_mm, 1)
                shared_down(g)
            pe.wait_ge(rank_read, 1)
            turn_rows(0, 0)
            pe.wait_ge(loops_ready, 1)
            n = nc.tensor.value_load(loops[0:1, 0:1], min_val=E // 2, max_val=ROUNDS * E // 2)
            with pe.Fori(0, n) as i:
                for par in range(2):
                    u = 2 * i + par
                    expert_gate_up(u, par)
                    turn_rows(u + 1, 1 - par)
                    expert_down(u, par)


_INS = ['L0_attn_X', 'L0_attn_W_in', 'L0_attn_b_in', 'L0_attn_W_out', 'L0_attn_b_out', 'L0_attn_gamma',
        'L0_attn_beta', 'L0_ffn_gate_w', 'L0_ffn_w_gate', 'L0_ffn_w_up', 'L0_ffn_w_down', 'L0_ffn_sw_gate',
        'L0_ffn_sw_up', 'L0_ffn_sw_down', 'L0_c', 'L0_wmod']


def rotary_tables():
    inv = np.float32(1.0) / np.float32(10000.0) ** (np.arange(0, ROT, 2, dtype=np.float32) / np.float32(ROT))
    angle = (np.arange(S, dtype=np.float32)[:, None] * inv[None, :].astype(np.float32)).T
    return np.ascontiguousarray(np.cos(angle)), np.ascontiguousarray(np.sin(angle))


def kernel(**inputs):
    import concourse.bacc as bacc
    from concourse.bass_utils import run_bass_kernel_spmd as run

    nc = bacc.Bacc("TRN2", target_bir_lowering=False, num_devices=1)
    arrays, args = {}, []

    def give(name, a):
        a = np.ascontiguousarray(a)
        arrays[name] = a
        args.append(nc.dram_tensor(name, a.shape, mybir.dt.from_np(a.dtype), kind="ExternalInput").ap())

    for name in _INS:
        a = np.asarray(inputs[name])
        give("in_" + name, a.reshape(T, D) if name == 'L0_attn_X' else a)
    for name, a in zip(("cos_table", "sin_table"), rotary_tables()):
        give(name, a)
    args.append(nc.dram_tensor("out_rows", (T + CAP, D), F32, kind="ExternalOutput").ap())
    build(nc, *args)
    r = run(nc, [arrays], core_ids=[0])
    return r.results[0]["out_rows"][:T].reshape(B, S, D)
```

```python
import numpy as np
import concourse.bass as bass
from concourse import mybir
from contextlib import ExitStack

F32, F32R, I32 = mybir.dt.float32, mybir.dt.float32r, mybir.dt.int32
ALU, ACT, AX = mybir.AluOpType, mybir.ActivationFunctionType, mybir.AxisListType

P = 128
B, S, D = 2, 1024, 512
T = B * S
NT = T // P
GT = 4
GN = GT * P
NG = T // GN
DC = D // P
ROT = D // 2
EPS = 1e-5
E, H, HS = 8, 352, 704
SM = [min(P, HS - P * m) for m in range(-(-HS // P))]
RM = [min(P, H - P * m) for m in range(-(-H // P))]
NS, NR = len(SM), len(RM)
CT = 5
CAP = CT * P
ROUNDS = -(-T // CAP)
COLS = ROUNDS * E * CT
TCOLS = COLS + 2 * CT
HALF = CAP // 2
EW = 2 * DC * H + NR * D

MOD = ["sa", "ca", "ga", "sb", "cb", "gb"]
WEIGHTS = ["sa", "ca", "K", "V", "ga", "sb", "cb", "gb", "Q", "O"]
PIECES = [(w, h) for w in WEIGHTS for h in range(2)]
PIECES += [(w, k) for k in range(DC) for w in ("sgate", "sup")]
PIECES += [("sdown", k) for k in range(NS // 2)]
MODS = [w for w in WEIGHTS if w in MOD]
EARLY = 8
SPLITS = [p for p in PIECES if p[0] not in MOD]


def build(nc, X, W_in, b_in, W_out, b_out, gamma, beta, gate_w, w_gate, w_up, w_down,
          sw_gate, sw_up, sw_down, c, wmod, cos_t, sin_t, out):
    def dram(name, shape, dt=F32):
        return nc.dram_tensor(name, shape, dt, kind="Internal").ap()

    mod_d = dram("mod_d", [B, 6 * D])
    base_d = dram("base_d", [T, D])
    x2_d = dram("x2_d", [T, D])
    h2_d = dram("h2_d", [T, D])
    slot_d = dram("slot_d", [P * COLS, 2], I32)

    ctx = ExitStack()
    with ctx:
        ctx.enter_context(nc.allow_non_contiguous_dma(reason="vectors of a few hundred values"))

        def sem(name):
            return ctx.enter_context(nc.semaphore(name))

        def region(stack):
            return lambda name, shape, dt=F32: stack.enter_context(nc.sbuf_tensor(name, shape, dt))

        sb = region(ctx)

        with ExitStack() as r_phase:
            al = region(r_phase)
            ew0 = al("ew0", [P, 2, EW], F32R)
            ht0 = al("ht0", [P, 2, DC, CAP], F32R)
            picked = al("picked", [P, CT, D])
        with ExitStack() as start:
            al = region(start)
            al("xt_head", [P, NG // 2, 2 * DC * GN])
            early = al("early", [P, EARLY, 2 * D])
        xt = sb("xt", [P, NG, 2, DC, GN], F32R)
        with ExitStack() as a1_phase:
            al = region(a1_phase)
            wkv = al("wkv", [P, 2, 2, DC, D], F32R)
            cos = al("cos", [P, S])
            sin = al("sin", [P, S])
            sq = al("sq", [P, 2, GN])
        with ExitStack() as r_phase:
            ew1 = region(r_phase)("ew1", [P, 2, EW], F32R)
        sgu = sb("sgu", [P, 2, 2, DC, HS], F32R)
        bc_s = sb("bc_s", [P, B, D])
        bc_c = sb("bc_c", [P, B, D])
        bc_ga = sb("bc_ga", [P, B, D])
        bc_gb = sb("bc_gb", [P, B, D])
        bout, mabs = bc_gb[:, 0, :], bc_gb[0:B, 1, :]
        ident = sb("ident", [P, P])
        ones = sb("ones", [P, P])
        upper = sb("upper", [P, P])
        nhalf = sb("nhalf", [P, 2 * GT])
        cT = sb("cT", [P, DC, B])
        scT = sb("scT", [P, DC, B])
        gb_col = sb("gb_col", [P, 2, DC])
        b_col = sb("b_col", [P, 3, DC])
        a_part = sb("a_part", [P, NG, DC])
        a_col = sb("a_col", [P, B, 2, DC])
        st6 = sb("st6", [P, GT, 6])
        mv = sb("mv", [P, GT, 2])
        ve = sb("ve", [P, GT])
        rs = sb("rs", [P, GT])
        nrm = sb("nrm", [P, GT, 2])
        rnm = sb("rnm", [P, GT, 2])
        wtok = sb("wtok", [P, GT])
        gw = sb("gw", [P, DC, E])
        lg = sb("lg", [P, NT, E])
        cntf = sb("cntf", [P, 2])
        loops = sb("loops", [P, 1], I32)
        gi = sb("gi", [P, 2, CT], I32)
        si = sb("si", [P, 2, CT], I32)
        wc = sb("wc", [P, 2, 2, CT])
        begin = sb("begin", [P, 5])
        with ExitStack() as a_phase:
            al = region(a_phase)
            with ExitStack() as a1_phase:
                rows1 = region(a1_phase)("rows1", [P, GT, D])
            wq = al("wq", [P, 2, DC, D], F32R)
            with ExitStack() as a1_phase:
                al1 = region(a1_phase)
                xn = al1("xn", [P, GT, D])
                hb = al1("hb", [P, 2, D])
            wo = al("wo", [P, 2, DC, D], F32R)
            with ExitStack() as a1_phase:
                al1 = region(a1_phase)
                atmp = al1("atmp", [P, 2, GN])
                kv = al1("kv", [P, 5, GN])
                rk = al1("rk", [P, 2, GN])
                rv = al1("rv", [P, 2, GN])
                mrow = al1("mrow", [B, D])
            qa = al("qa", [P, 2, DC, GN], F32R)
            tmp = al("tmp", [P, DC, GN])
            stage = al("stage", [P, 2, 2 * D])
            rows = al("rows", [P, GT, D])
            hx = al("hx", [P, GT, D])
        with ExitStack() as s_phase:
            al = region(s_phase)
            with ExitStack() as r_phase:
                al2 = region(r_phase)
                gtR = al2("gtR", [P, 2, NR, CAP], F32R)
                y = al2("y", [P, CT, D])
                gsel = al2("gsel", [P, CT, D])
                ht1 = al2("ht1", [P, 2, DC, CAP], F32R)
            sd = al("sd", [P, 2, NS, D], F32R)
            gtS = al("gtS", [P, 2, NS, GN], F32R)
            xrow = al("xrow", [P, 2, D])
            srow = al("srow", [P, 2, D])
            with ExitStack() as routing:
                al2 = region(routing)
                iota8 = al2("iota8", [P, NT, E])
                sc = al2("sc", [P, NT, E])
                eq = al2("eq", [P, NT, E])
                oh = al2("oh", [P, 2, NT, E])
                both = al2("both", [P, NT, E])
                within = al2("within", [P, NT, E])
                upto = al2("upto", [P, 3, NT, E])
                mx = al2("mx", [P, 2, NT, 1])
                wt = al2("wt", [P, 2, NT, 1])
                ix = al2("ix", [P, 2, NT, 1])
                rr = al2("rr", [P, 2, NT, 1])
                rd = al2("rd", [P, 2, NT, 1])
                qq = al2("qq", [P, 2, NT, 1])
                sl = al2("sl", [P, 2, NT, 1])
                sidx = al2("sidx", [P, 2 * NT], I32)
                rec = al2("rec", [P, 2, NT, 2], I32)
            ewst = al("ewst", [P, 2, NR * D])
            tab = al("tab", [P, TCOLS, 2], I32)
            w01 = al("w01", [P, 2, TCOLS])
            gidx = al("gidx", [P, TCOLS], I32)
        gbuf = [a[:, 0, :] for a in (bc_s, bc_c, bc_ga)]

        a1_rows = (rows, rows1)
        ygate = bc_gb

        bank = [ctx.enter_context(nc.psum_tensor(f"bank{i}", [P, GN], F32)) for i in range(8)]
        T_BANKS, KV_BANKS, NORM_BANK, W_BANK = (0, 1), (2, 3, 4, 5), 6, 7
        GATE_BANKS, UP_BANKS, DOWN_BANKS, RT_BANKS = (2, 4), (3, 5), (6, 7), (0, 1)
        Q_BANKS, Y_BANKS, T2_BANKS, LG_BANK = (2, 3, 4), (6, 7), (0, 5), 1

        consts = sem("consts")
        small_in, bias_in, table_in = sem("small_in"), sem("bias_in"), sem("table_in")
        c_in = sem("c_in")
        sc_ready = sem("sc_ready")
        early_in = [sem(f"early_in{i}") for i in range(EARLY)]
        piece_in = [sem(f"piece_in{i}") for i in range(2)]
        mod_mm, mod_row, mod_out, bc_in = sem("mod_mm"), sem("mod_row"), sem("mod_out"), sem("bc_in")
        bout_in = sem("bout_in")
        hi_done, lo_done = sem("hi_done"), sem("lo_done")
        x_in = [sem(f"x_in{j}") for j in range(2 * GT)]
        dve_step, pool_step, act_step = sem("dve_step"), sem("pool_step"), sem("act_step")
        ve_ready, rs_ready = sem("ve_ready"), sem("rs_ready")
        h_ready, h_read, base_ready = sem("h_ready"), sem("h_read"), sem("base_ready")
        base_out = [sem(f"base_out{j}") for j in range(2 * GT)]
        xn_ready, t_mm, t_hi, t_lo = sem("xn_ready"), sem("t_mm"), sem("t_hi"), sem("t_lo")
        kv_mm, kv_copied, sq_ready, sq_mm = sem("kv_mm"), sem("kv_copied"), sem("sq_ready"), sem("sq_mm")
        v_turned, prod, nrm_ready, w_ready = sem("v_turned"), sem("prod"), sem("nrm_ready"), sem("w_ready")
        w_mm, a_done, a_ready = sem("w_mm"), sem("a_done"), sem("a_ready")
        q_mm, qa_hi, qa_lo, y_mm = sem("q_mm"), sem("qa_hi"), sem("qa_lo"), sem("y_mm")
        base_in = [sem(f"base_in{j}") for j in range(GT)]
        x2_ready, h2_half, h2_ready = sem("x2_ready"), sem("h2_half"), sem("h2_ready")
        x2_out = [sem(f"x2_out{j}") for j in range(GT)]
        h2_out = [sem(f"h2_out{j}") for j in range(GT)]
        t2_mm, t2_hi, t2_lo, lg_mm = sem("t2_mm"), sem("t2_hi"), sem("t2_lo"), sem("lg_mm")

        slot0_out, slot_out, tab_in = sem("slot0_out"), sem("slot_out"), sem("tab_in")
        pad_in, tab_ready = sem("pad_in"), sem("tab_ready")
        lg_ready, exp_ready = sem("lg_ready"), sem("exp_ready")
        both_ready, rank_mm, rank_read = sem("both_ready"), sem("rank_mm"), sem("rank_read")
        slots_ready, loops_ready, cols_ready = sem("slots_ready"), sem("loops_ready"), sem("cols_ready")
        s_gu_mm, s_silu, s_mul, s_hi, s_lo = sem("s_gu_mm"), sem("s_silu"), sem("s_mul"), sem("s_hi"), sem("s_lo")
        s_down_mm, s_row = sem("s_down_mm"), sem("s_row")
        x2_in = [sem(f"x2_in{i}") for i in range(2)]
        s_out = [sem(f"s_out{i}") for i in range(2)]
        ew_in = [sem(f"ew_in{q}") for q in range(3)]
        ew_hi, ew_lo = sem("ew_hi"), sem("ew_lo")
        gi_ready, si_ready, picked_in = sem("gi_ready"), sem("si_ready"), sem("picked_in")
        wc_ready, gs_ready, gsel_ready = sem("wc_ready"), sem("gs_ready"), sem("gsel_ready")
        rt_mm, rt_hi, rt_lo = sem("rt_mm"), sem("rt_hi"), sem("rt_lo")
        gu_mm, r_silu, r_mul, r_hi, r_lo = sem("gu_mm"), sem("r_silu"), sem("r_mul"), sem("r_hi"), sem("r_lo")
        down_mm, y_ready, y_out, added = sem("down_mm"), sem("y_ready"), sem("y_out"), sem("added")

        ew, ht = (ew0, ew1), (ht0, ht1)
        EW_AT = {0: 0, 2: 1, 4: 2}
        ROWS_AT = [(), (), (0, 1), (), (2, 3), (4,)]
        GB_AT = [(), (0, 1), (), (2,), (), (), (3, 4)]
        EW_PART = [(0, DC * H), (DC * H, 2 * DC * H), (2 * DC * H, EW)]

        def arrived(eng, n):
            if n < EARLY:
                return eng.wait_ge(early_in[n], 16)
            n -= EARLY
            eng.wait_ge(piece_in[n % 2], 16 * (n // 2 + 1 + (n == len(PIECES) - EARLY - 1)))

        def piece_slot(n):
            return early[:, n, :] if n < EARLY else stage[:, n % 2, :]

        def tile_rows(ap, t):
            return ap[t * P:(t + 1) * P, :]

        KV_ORDER = [(0, 0), (0, 1), (1, 0), (1, 1), (0, 2), (1, 2), (0, 3), (1, 3)]
        KV_SLOT = [0, 1, 2, 3, 2, 3, 4, 3]

        def split_views(n, part):
            w, h = PIECES[n]
            src = piece_slot(n)
            if w in ("sgate", "sup"):
                return [(sgu[:, part, w == "sup", h, :], src[:, 0:HS])]
            if w == "sdown":
                return [(sd[0:SM[m], part, m, :], src[0:SM[m], (m % 2) * D:(m % 2 + 1) * D]) for m in (2 * h, 2 * h + 1)]
            ks = slice(2 * h, 2 * h + 2)
            src = src.rearrange("p (k n) -> p k n", k=2)
            if w == "O":
                return [(wo[:, part, ks, :], src)]
            dst = wq[:, part, ks, :] if w == "Q" else wkv[:, part, w == "V", ks, :]
            return [(dst[:, :, 0:ROT].rearrange("p k (two f) -> p k two f", two=2),
                     src[:, :, 0:ROT].rearrange("p k (f two) -> p k two f", two=2)),
                    (dst[:, :, ROT:D], src[:, :, ROT:D])]

        block = ctx.enter_context(nc.Block())

        @block.sync
        def _(sp):
            def load_piece(n):
                if n >= EARLY + 2:
                    w, h = PIECES[n - 2]
                    if w in MOD:
                        sp.wait_ge(mod_mm, 2 * MODS.index(w) + h + 1)
                    else:
                        sp.wait_ge(lo_done, SPLITS.index(PIECES[n - 2]) + 1)
                w, h = PIECES[n]
                dst = piece_slot(n)
                arrives = early_in[n] if n < EARLY else piece_in[n % 2]
                half = slice(2 * h * P, 2 * (h + 1) * P)
                if w in ("sgate", "sup"):
                    src = (sw_gate if w == "sgate" else sw_up)[h * P:(h + 1) * P, :]
                    sp.dma_start(dst[:, 0:HS], src).then_inc(piece_in[n % 2], 16)
                    return
                if w == "sdown":
                    at = 2 * h * P
                    dst = dst.rearrange("p (k n) -> p k n", k=2)
                    if n < len(PIECES) - 1:
                        sp.dma_start(dst, sw_down[at:at + 2 * P, :].rearrange("(k p) n -> p k n", k=2))\
                            .then_inc(piece_in[n % 2], 16)
                    else:
                        sp.dma_start(dst[:, 0, :], sw_down[at:at + P, :]).then_inc(piece_in[n % 2], 16)
                        sp.dma_start(dst[0:SM[-1], 1, :], sw_down[at + P:HS, :]).then_inc(piece_in[n % 2], 16)
                    return
                dst = dst.rearrange("p (k n) -> p k n", k=2)
                if w == "O" and h == 0:
                    src = W_out[0:ROT, :].rearrange("(p k) n -> p k n", k=2)
                elif w == "O":
                    src = W_out[half, :].rearrange("(k p) n -> p k n", k=2)
                else:
                    col = D * ("Q", "K", "V").index(w) if w in "QKV" else D * MOD.index(w)
                    src = (W_in if w in "QKV" else wmod)[half, col:col + D].rearrange("(k p) n -> p k n", k=2)
                sp.dma_start(dst, src).then_inc(arrives, 16)

            def load_x(t):
                slot, g = t % (2 * GT), t // GT
                if g >= 2:
                    sp.wait_ge(base_out[slot], 16 * (g // 2))
                sp.dma_start(a1_rows[g % 2][:, t % GT, :], tile_rows(X, t)).then_inc(x_in[slot], 16)

            def store_base(t):
                slot, g = t % (2 * GT), t // GT
                sp.wait_ge(base_ready, t + 1)
                sp.dma_start(tile_rows(base_d, t), a1_rows[g % 2][:, t % GT, :]).then_inc(base_out[slot], 16)

            def store_mod(i):
                col = D * MOD.index(MODS[i])
                sp.wait_ge(mod_row, i + 1)
                sp.dma_start(mod_d[:, col:col + D], mrow[:, :]).then_inc(mod_out, 16)

            def spread_mod(i):
                w = MODS[i]
                col = D * MOD.index(w)
                sp.wait_ge(mod_out, 16 * (i + 1))
                dst = {"sa": bc_s, "ca": bc_c, "ga": bc_ga, "sb": bc_s, "cb": bc_c, "gb": bc_gb}[w]
                if w in ("sb", "cb"):
                    sp.wait_ge(h_ready, NT)
                if w == "gb":
                    sp.wait_ge(h_read, NT)
                    sp.wait_ge(x2_ready, NT)
                sp.dma_start(dst[:, :, :], mod_d[:, col:col + D].partition_broadcast(P)).then_inc(bc_in, 16)

            for b in range(B):
                sp.dma_start(cT[:, :, b], c[b, :].rearrange("(k p) -> p k", p=P)).then_inc(c_in, 16)
            for n in range(4):
                load_piece(n)
            for t in range(GT):
                load_x(t)
            for n in range(4, EARLY):
                load_piece(n)
            sp.dma_start(gb_col[:, 0, :], gamma.rearrange("(k p) -> p k", p=P)).then_inc(small_in, 16)
            sp.dma_start(gb_col[:, 1, :], beta.rearrange("(k p) -> p k", p=P)).then_inc(small_in, 16)
            for i in range(2):
                store_mod(i)
                spread_mod(i)
            load_piece(8)
            load_piece(9)
            sp.dma_start(bout, b_out.partition_broadcast(P)).then_inc(bout_in, 16)
            for i, part in enumerate((1, 2, 0)):
                seg = b_in[part * D:(part + 1) * D]
                sp.dma_start(b_col[:, i, 0:2], seg[0:ROT].rearrange("(p k) -> p k", k=2)).then_inc(bias_in, 16)
                sp.dma_start(b_col[:, i, 2:4], seg[ROT:D].rearrange("(k p) -> p k", p=P)).then_inc(bias_in, 16)
            for t in range(GT, 2 * GT):
                load_x(t)
            sp.dma_start(cos[:, :], cos_t).then_inc(table_in, 16)
            sp.dma_start(sin[:, :], sin_t).then_inc(table_in, 16)
            sp.dma_start(gw[:, :, :], gate_w.rearrange("(k p) e -> p k e", p=P)).then_inc(table_in, 16)
            store_mod(2)
            spread_mod(2)
            load_piece(10)
            load_piece(11)
            for t in range(GT):
                store_base(t)
                load_x(2 * GT + t)
            store_mod(3)
            load_piece(12)
            load_piece(13)
            for t in range(GT, 2 * GT):
                store_base(t)
                load_x(2 * GT + t)
            store_mod(4)
            load_piece(14)
            load_piece(15)
            for t in range(2 * GT, NT):
                store_base(t)
            store_mod(5)
            load_piece(16)
            load_piece(17)
            spread_mod(3)
            spread_mod(4)
            load_piece(18)
            load_piece(19)

            def load_base(t):
                j = t % GT
                for slot in (j, GT + j):
                    sp.wait_ge(base_out[slot], 16 * NG // 2)
                if t >= GT:
                    sp.wait_ge(x2_out[j], 16 * (t // GT))
                    sp.wait_ge(h2_half, t - GT + 1)
                sp.dma_start(rows[:, j, :], tile_rows(base_d, t)).then_inc(base_in[j], 16)

            for t in range(GT):
                load_base(t)
            load_piece(20)
            load_piece(21)
            for g in range(NG):
                for j in range(GT):
                    t = g * GT + j
                    sp.wait_ge(x2_ready, t + 1)
                    sp.dma_start(tile_rows(x2_d, t), rows[:, j, :]).then_inc(x2_out[j], 16)
                load_piece(22 + 2 * g)
                load_piece(23 + 2 * g)
                for j in range(GT):
                    t = g * GT + j
                    if g + 1 < NG:
                        load_base(t + GT)
                    sp.wait_ge(h2_ready, t + 1)
                    sp.dma_start(tile_rows(h2_d, t), hx[:, j, :]).then_inc(h2_out[j], 16)
                if g == 0:
                    sp.dma_start(out[T:T + CAP, :], X[0:CAP, :]).then_inc(pad_in, 16)
            load_piece(30)
            spread_mod(5)
            sp.wait_ge(tab_ready, 1)
            sp.dma_start(slot_d.rearrange("(p c) two -> p c two", p=P), tab[:, 0:COLS, :]).then_inc(slot0_out, 16)

            def load_x2(t):
                if t >= 2:
                    sp.wait_ge(s_out[t % 2], 16 * (t // 2))
                sp.wait_ge(x2_out[t % GT], 16 * (t // GT + 1))
                sp.dma_start(xrow[:, t % 2, :], tile_rows(x2_d, t)).then_inc(x2_in[t % 2], 16)

            def store_s(t):
                sp.wait_ge(s_row, t + 1)
                sp.dma_start(tile_rows(out, t), xrow[:, t % 2, :]).then_inc(s_out[t % 2], 16)
                if t + 2 < NT:
                    load_x2(t + 2)

            def load_expert(w, par, pieces=range(3)):
                e = w % E if isinstance(w, int) else sp.snap(w % E)
                before = None if isinstance(w, int) else [sp.snap(3 * w + q - 1) for q in range(3)]
                for q in pieces:
                    slot = (par + q) % 2
                    if before:
                        sp.wait_ge(ew_lo, before[q])
                    elif q == 2:
                        sp.wait_ge(ew_lo, 1)
                    if q < 2:
                        src = (w_gate, w_up)[q][bass.ds(e, 1), :, :].rearrange("e (k p) n -> p (e k) n", p=P)
                        dst = ewst[:, slot, 0:DC * H].rearrange("p (k n) -> p k n", k=DC)
                        sp.dma_start(dst, src).then_inc(ew_in[q], 16)
                    else:
                        full = H // P
                        dst = ewst[:, slot, 0:full * D].rearrange("p (k n) -> p k n", k=full)
                        src = w_down[bass.ds(e, 1), 0:full * P, :].rearrange("e (k p) n -> p (e k) n", p=P)
                        sp.dma_start(dst, src).then_inc(ew_in[q], 16)
                        sp.dma_start(ewst[0:RM[-1], slot, full * D:NR * D],
                                     w_down[bass.ds(e, 1), full * P:H, :].rearrange("e p n -> p (e n)"))\
                            .then_inc(ew_in[q], 16)

            sp.wait_ge(t2_lo, NT)
            sp.wait_ge(lg_mm, NG)
            load_x2(0)
            load_x2(1)
            for t in range(NT):
                if t == 2 * GT:
                    sp.wait_ge(slot_out, 16 * 2 * NT)
                    sp.dma_start(tab[:, 0:COLS, :], slot_d.rearrange("(p c) two -> p c two", p=P)).then_inc(tab_in, 16)
                    sp.wait_ge(lo_done, len(SPLITS))
                    load_expert(0, 0, (0, 1))
                if t == 3 * GT:
                    load_expert(0, 0, (2,))
                store_s(t)
            sp.wait_ge(loops_ready, 1)
            n = nc.sync.value_load(loops[0:1, 0:1], min_val=E // 2, max_val=ROUNDS * E // 2)
            with sp.Fori(0, n) as i:
                for par in range(2):
                    load_expert(2 * i + par + 1, 1 - par)

        @block.gpsimd
        def _(pool):
            steps = [0]

            def link(ins):
                steps[0] += 1
                ins.then_inc(pool_step, 1)
                pool.wait_ge(pool_step, steps[0])

            for i, begun in enumerate((added, y_ready, down_mm, r_lo, r_mul)):
                pool.memset(begin[:, i:i + 1], 0.0).then_inc(begun, 1)
            pool.memset(ones[:, :], 1.0).then_inc(consts, 1)
            pool.memset(nhalf[:, :], -0.5).then_inc(consts, 1)
            link(pool.memset(ident[:, :], 0.0))
            pool.affine_select(out=ident[:, :], in_=ident[:, :], compare_op=ALU.not_equal, fill=1.0,
                               base=0, pattern=[[-1, P]], channel_multiplier=1).then_inc(consts, 1)
            pool.wait_ge(consts, 3)
            pool.affine_select(out=upper[:, :], in_=ones[:, :], compare_op=ALU.is_gt, fill=0.0,
                               base=0, pattern=[[1, P]], channel_multiplier=-1).then_inc(consts, 1)

            def norm_power(n):
                pool.wait_ge(ve_ready, n + 1)
                pool.tensor_tensor(rs[:, :], ve[:, :], nhalf[:, 0:GT], ALU.pow).then_inc(rs_ready, 1)

            def add_bias(g, j):
                pool.wait_ge(h_ready, GT * g + j + 1)
                if GT * g + j >= 2:
                    pool.wait_ge(base_ready, GT * g + j - 1)
                pool.tensor_tensor(hb[:, j % 2, :], hx[:, j, :], bout, ALU.add).then_inc(h_read, 1)

            def finish_base(g, j):
                row = a1_rows[g % 2][:, j, :]
                pool.wait_ge(h_read, GT * g + j + 1)
                link(pool.tensor_tensor(hb[:, j % 2, :], hb[:, j % 2, :], bc_ga[:, g // (NG // B), :], ALU.mult))
                pool.tensor_tensor(row, row, hb[:, j % 2, :], ALU.add).then_inc(base_ready, 1)

            def base_start(g):
                add_bias(g, 0)
                add_bias(g, 1)
                norm_power(2 * g + 1)

            def base_rest(g):
                finish_base(g, 0)
                add_bias(g, 2)
                finish_base(g, 1)
                add_bias(g, 3)
                finish_base(g, 2)
                finish_base(g, 3)

            def turn_v(g):
                at = slice((g * GN) % S, (g * GN) % S + GN)
                pool.wait_ge(kv_copied, 8 * g + 4)
                pool.tensor_tensor(rv[:, 0, :], kv[:, 2, :], cos[:, at], ALU.mult)
                link(pool.tensor_tensor(rv[:, 1, :], kv[:, 3, :], sin[:, at], ALU.mult))
                pool.tensor_tensor(kv[:, 2, :], kv[:, 2, :], sin[:, at], ALU.mult)
                link(pool.tensor_tensor(kv[:, 3, :], kv[:, 3, :], cos[:, at], ALU.mult))
                link(pool.tensor_tensor(kv[:, 3, :], kv[:, 2, :], kv[:, 3, :], ALU.add))
                pool.tensor_tensor(kv[:, 2, :], rv[:, 0, :], rv[:, 1, :], ALU.subtract).then_inc(v_turned, 1)

            def token_weights(g):
                pool.wait_ge(nrm_ready, g + 1)
                if g:
                    pool.wait_ge(w_mm, g)
                link(pool.tensor_tensor(rnm[:, :, :], nrm[:, :, :], nhalf[:, :].rearrange("p (t k) -> p t k", k=2), ALU.pow))
                pool.tensor_tensor(wtok[:, :], rnm[:, :, 0], rnm[:, :, 1], ALU.mult).then_inc(w_ready, 1)

            norm_power(0)
            pool.wait_ge(bout_in, 16)
            base_start(0)
            pool.wait_ge(bc_in, 16 * 3)
            base_rest(0)
            pool.wait_ge(table_in, 16 * 3)
            for g in range(NG):
                if g + 1 < NG:
                    norm_power(2 * g + 2)
                    base_start(g + 1)
                turn_v(g)
                if g + 1 < NG:
                    base_rest(g + 1)
                token_weights(g)

            pool.wait_ge(bc_in, 16 * 5)
            for g in range(NG):
                norm_power(2 * NG + g)
                for j in range(GT):
                    pool.wait_ge(h2_half, GT * g + j + 1)
                    pool.tensor_tensor(hx[:, j, :], hx[:, j, :], bc_s[:, g // 2, :], ALU.add).then_inc(h2_ready, 1)

            for j in range(GT):
                pool.wait_ge(x2_out[j], 16 * NG)
            pool.wait_ge(lo_done, len(SPLITS))
            pool.iota(tab[:, :, 0], pattern=[[0, TCOLS // CT], [P, CT]], base=T, channel_multiplier=1)
            pool.memset(tab[:, :, 1], 0)
            pool.iota(rec[:, :, :, 0], pattern=[[0, 2], [P, NT]], base=0, channel_multiplier=1)
            pool.iota(iota8[:, :, :], pattern=[[0, NT], [1, E]], base=-E, channel_multiplier=0,
                      allow_small_or_imprecise_dtypes=True)
            pool.drain().then_inc(tab_ready, 1)

            pool.wait_ge(slots_ready, 1)
            pool.wait_ge(slot0_out, 16)
            for n in range(2 * NT):
                pool.indirect_dma_start(out=slot_d, out_offset=bass.IndirectOffsetOnAxis(ap=sidx[:, n:n + 1], axis=0),
                                        in_=rec[:, n // NT, n % NT, :], in_offset=None).then_inc(slot_out, 16)

            def gather(w, par):
                pool.tensor_copy(gi[:, par, :], gidx[:, bass.ds(w * CT, CT)]).then_inc(gi_ready, 1)
                pool.wait_ge(gi_ready, w + 1)
                if not isinstance(w, int) or w:
                    pool.wait_ge(rt_mm, CT * w)
                pool.nop(nofuse=True)
                for j in range(CT):
                    pool.indirect_dma_start(out=picked[:, j, :], out_offset=None, in_=h2_d,
                                            in_offset=bass.IndirectOffsetOnAxis(ap=gi[:, par, j:j + 1], axis=0))\
                        .then_inc(picked_in, 16)

            def scatter(u, par):
                pool.tensor_copy(si[:, par, :], tab[:, bass.ds(u * CT, CT), 0]).then_inc(si_ready, 1)
                pool.wait_ge(si_ready, u + 1)
                for j in range(CT):
                    pool.wait_ge(y_ready, CT * u + j + 1 + 1)
                    pool.nop(nofuse=True)
                    pool.indirect_dma_start(out=out, out_offset=bass.IndirectOffsetOnAxis(ap=si[:, par, j:j + 1], axis=0),
                                            in_=y[:, j, :], in_offset=None, compute_op=ALU.add).then_inc(y_out, 16)
                pool.wait_ge(y_out, 16 * CT * (u + 1))
                pool.nop(nofuse=True).then_inc(added, 1)

            pool.wait_ge(cols_ready, 1)
            pool.wait_ge(s_gu_mm, NS * NG)
            for j in range(GT):
                pool.wait_ge(h2_out[j], 16 * NG)
            gather(0, 0)
            gather(1, 1)
            pool.wait_ge(pad_in, 16)
            for i in range(2):
                pool.wait_ge(s_out[i], 16 * NT // 2)
            pool.wait_ge(loops_ready, 1)
            n = nc.gpsimd.value_load(loops[0:1, 0:1], min_val=E // 2, max_val=ROUNDS * E // 2)
            with pool.Fori(0, n) as i:
                for par in range(2):
                    gather(2 * i + par + 2, par)
                    scatter(2 * i + par, par)

        @block.scalar
        def _(act):
            def split_hi(n):
                w, h = PIECES[n]
                arrived(act, n)
                for dst, src in split_views(n, 0):
                    last = nc.scalar.activation(dst, src, ACT.Copy)
                last.then_inc(hi_done, 1)

            def transposed(g):
                for k in range(DC):
                    n = DC * g + k
                    act.wait_ge(t_mm, n + 1)
                    if n >= 2:
                        act.wait_ge(t_lo, n - 1)
                    src = bank[T_BANKS[k % 2]][:, :]
                    nc.scalar.activation(atmp[:, k % 2, :], src, ACT.Identity,
                                         bias=gb_col[:, 1, k:k + 1], scale=gb_col[:, 0, k:k + 1])
                    nc.scalar.activation(xt[:, g, 0, k, :], src, ACT.Identity, bias=gb_col[:, 1, k:k + 1],
                                         scale=gb_col[:, 0, k:k + 1]).then_inc(t_hi, 1)

            def copy_kv(g, n):
                i, m = KV_ORDER[n]
                N = 8 * g + n
                act.wait_ge(kv_mm, N + 1)
                if n < 4 and g:
                    act.wait_ge(a_done, DC * g)
                if n >= 4:
                    act.wait_ge(prod, DC * g + (1, 2, 2, 3)[n - 4])
                bias = b_col[:, i, m:m + 1]
                src = bank[KV_BANKS[n % 4]][:, :]
                nc.scalar.activation(kv[:, KV_SLOT[n], :], src, ACT.Identity, bias=bias).then_inc(kv_copied, 1)
                if N >= 2:
                    act.wait_ge(sq_mm, N - 1)
                nc.scalar.activation(sq[:, n % 2, :], src, ACT.Square, bias=bias).then_inc(sq_ready, 1)

            act.wait_ge(c_in, 16 * B)
            nc.scalar.activation(scT[:, :, :], cT[:, :, :], ACT.Silu).then_inc(sc_ready, 1)
            for n in range(4, 8):
                split_hi(n)
            act.wait_ge(small_in, 16 * 2)
            transposed(0)
            act.wait_ge(bias_in, 16 * 6)
            for g in range(NG):
                for n in range(7):
                    copy_kv(g, n)
                if g + 1 < NG:
                    transposed(g + 1)
                else:
                    for j in range(GT):
                        act.wait_ge(base_out[GT + j], 16 * NG // 2)
                    split_hi(16)
                    split_hi(17)
                copy_kv(g, 7)
            act.wait_ge(base_ready, NT)
            split_hi(18)
            split_hi(19)

            def scaled_q(g):
                b = g // 2
                act.wait_ge(a_ready, b + 1)
                for m in range(DC):
                    act.wait_ge(q_mm, DC * g + m + 1)
                    if g == 0:
                        act.wait_ge(t_lo, NT)
                        act.wait_ge(a_done, NT)
                    else:
                        act.wait_ge(y_mm, GT * g)
                    if g >= 2:
                        act.wait_ge(lg_mm, g - 1)
                        act.wait_ge(t2_lo, DC * (g - 1))
                    src = bank[Q_BANKS[(DC * g + m) % 3]][:, :]
                    col = dict(bias=a_col[:, b, 1, m:m + 1], scale=a_col[:, b, 0, m:m + 1])
                    nc.scalar.activation(tmp[:, m, :], src, ACT.Identity, **col)
                    nc.scalar.activation(qa[:, 0, m, :], src, ACT.Identity, **col).then_inc(qa_hi, 1)

            def transposed2(g):
                for k in range(DC):
                    n = DC * g + k
                    act.wait_ge(t2_mm, n + 1)
                    src = bank[T2_BANKS[k % 2]][:, :]
                    if k == 0:
                        act.wait_ge(qa_lo, DC * (g + 1))
                    nc.scalar.activation(tmp[:, k, :], src, ACT.Copy)
                    nc.scalar.activation(xt[:, g, 0, k, :], src, ACT.Copy).then_inc(t2_hi, 1)

            def s_silu_of(g, m):
                n = NS * g + m
                r = SM[m]
                act.wait_ge(s_gu_mm, n + 1)
                if n >= 3:
                    act.wait_ge(s_lo, n - 2)
                nc.scalar.activation(gbuf[n % 3][0:r, :], bank[GATE_BANKS[m % 2]][0:r, :], ACT.Silu).then_inc(s_silu, 1)

            def s_hi_of(g, m):
                n = NS * g + m
                r = SM[m]
                act.wait_ge(s_mul, n + 1)
                if g:
                    act.wait_ge(s_down_mm, GT * g)
                nc.scalar.activation(gtS[0:r, 0, m, :], gbuf[n % 3][0:r, :], ACT.Copy).then_inc(s_hi, 1)

            def shared(g):
                for m in range(NS):
                    s_silu_of(g, m)
                    if m:
                        s_hi_of(g, m - 1)
                    if g == 0 and m >= 3:
                        split_hi(25 + m)
                s_hi_of(g, NS - 1)

            def expert_hi(w, par, q):
                lo, hi = EW_PART[q]
                slot = (par + q) % 2
                act.wait_ge(ew_in[q], (16 if q < 2 else 32) * (w + 1))
                if not isinstance(w, int):
                    act.wait_ge(down_mm, CT * (w - 1) + 1)
                if q < 2:
                    nc.scalar.activation(ew[par][:, 0, lo:hi], ewst[:, slot, 0:hi - lo], ACT.Copy).then_inc(ew_hi, 1)
                    return
                full = H // P * D
                nc.scalar.activation(ew[par][:, 0, lo:lo + full], ewst[:, slot, 0:full], ACT.Copy)
                nc.scalar.activation(ew[par][0:RM[-1], 0, lo + full:hi], ewst[0:RM[-1], slot, full:NR * D], ACT.Copy)\
                    .then_inc(ew_hi, 1)

            def picked_hi(w, par, steps):
                for s in steps:
                    act.wait_ge(rt_mm, CT * w + s + 1)
                    src = bank[RT_BANKS[(par + s) % 2]]
                    if s < DC:
                        nc.scalar.activation(ht[par][:, 0, s, 0:GN], src[:, :], ACT.Copy).then_inc(rt_hi, 1)
                    else:
                        nc.scalar.activation(ht[par][:, 0, :, GN:CAP], src[:, :].rearrange("p (k t) -> p k t", k=DC),
                                             ACT.Copy).then_inc(rt_hi, 1)

            def select_gb(u, par, j):
                if j == 0:
                    act.wait_ge(wc_ready, u + 1)
                    act.wait_ge(y_ready, CT * u + 1)
                nc.scalar.activation(gsel[:, j, :], bc_gb[:, 1, :], ACT.Copy, scale=wc[:, par, 1, j:j + 1])\
                    .then_inc(gs_ready, 1)

            def r_silu_of(u, par, c):
                half, m = divmod(c, NR)
                r = RM[m]
                act.wait_ge(gu_mm, 2 * NR * u + c + 1)
                act.wait_ge(r_lo, 2 * NR * u + max(c - 2, 0) + 1)
                nc.scalar.activation(gbuf[c % 3][0:r, 0:HALF], bank[GATE_BANKS[c % 2]][0:r, 0:HALF], ACT.Silu)\
                    .then_inc(r_silu, 1)

            def r_hi_of(u, par, c):
                half, m = divmod(c, NR)
                r = RM[m]
                act.wait_ge(r_mul, 2 * NR * u + c + 1 + 1)
                if c == 0:
                    act.wait_ge(down_mm, CT * u + 1)
                nc.scalar.activation(gtR[0:r, 0, m, half * HALF:(half + 1) * HALF], gbuf[c % 3][0:r, 0:HALF],
                                     ACT.Copy)\
                    .then_inc(r_hi, 1)

            act.wait_ge(a_done, NT)
            act.wait_ge(sq_mm, 8 * NG)
            scaled_q(0)
            for g in range(NG):
                for n in range(20 + 2 * g, 22 + 2 * g):
                    split_hi(n)
                if g:
                    transposed2(g - 1)
                if g + 1 < NG:
                    scaled_q(g + 1)
            shared(0)
            transposed2(NG - 1)

            act.wait_ge(lg_ready, 1)
            nc.scalar.activation(sc[:, :, :], sc[:, :, :], ACT.Exp).then_inc(exp_ready, 1)
            shared(1)
            shared(2)
            expert_hi(0, 0, 0)
            expert_hi(0, 0, 1)
            shared(3)
            expert_hi(0, 0, 2)
            for i in range(2):
                act.wait_ge(s_out[i], 16 * NT // 2)
            picked_hi(0, 0, range(CT))
            act.wait_ge(loops_ready, 1)
            n = nc.scalar.value_load(loops[0:1, 0:1], min_val=E // 2, max_val=ROUNDS * E // 2)
            nc.scalar.preload_act_table(ACT.Silu)
            with act.Fori(0, n) as i:
                for par in range(2):
                    u = 2 * i + par
                    for c in range(2 * NR):
                        r_silu_of(u, par, c)
                        if c:
                            r_hi_of(u, par, c - 1)
                        if c in EW_AT:
                            expert_hi(u + 1, 1 - par, EW_AT[c])
                        for j in GB_AT[c]:
                            select_gb(u, par, j)
                        if c and ROWS_AT[c - 1]:
                            picked_hi(u + 1, 1 - par, ROWS_AT[c - 1])
                    r_hi_of(u, par, 2 * NR - 1)
                    picked_hi(u + 1, 1 - par, ROWS_AT[2 * NR - 1])
                    for j in GB_AT[-1]:
                        select_gb(u, par, j)

        @block.vector
        def _(dve):
            steps = [0]

            def link(ins):
                steps[0] += 1
                ins.then_inc(dve_step, 1)
                dve.wait_ge(dve_step, steps[0])

            def split_lo(n):
                i = SPLITS.index(PIECES[n])
                arrived(dve, n)
                dve.wait_ge(hi_done, i + 1)
                his = split_views(n, 0)
                for (dst, src), (hi, _) in zip(split_views(n, 1), his):
                    last = dve.tensor_tensor(dst, src, hi.bitcast(F32), ALU.subtract)
                last.then_inc(lo_done, 1)

            def mod_vector(i):
                w = MODS[i]
                row = mrow[:, :]
                src = bank[W_BANK][0:B, :]
                dve.wait_ge(mod_mm, 2 * i + 2)
                if i:
                    dve.wait_ge(mod_out, 16 * i)
                if w in ("sa", "sb"):
                    dve.tensor_copy(row, src).then_inc(mod_row, 1)
                elif w in ("ca", "cb"):
                    dve.tensor_scalar_add(row, src, 1.0).then_inc(mod_row, 1)
                else:
                    link(dve.tensor_copy(row, src))
                    link(dve.scalar_tensor_tensor(mabs, row, -1.0, row, ALU.mult, ALU.max))
                    dve.tensor_scalar(row, row, 0.0, 2.0, ALU.is_ge, ALU.mult)
                    link(dve.tensor_scalar_max(mabs, mabs, 0.25))
                    dve.scalar_tensor_tensor(row, row, -1.0, mabs, ALU.add, ALU.mult)\
                        .then_inc(mod_row, 1)

            def statistics(src):
                for j in range(GT):
                    last = dve.bn_stats(st6[:, j, :], src[:, j, :])
                link(last)
                for j in range(GT):
                    last = dve.bn_aggr(mv[:, j, :], st6[:, j, :])
                link(last)
                dve.tensor_scalar_add(ve[:, :], mv[:, :, 1], EPS).then_inc(ve_ready, 1)

            def norm_rows(j, dst, src):
                return dve.tensor_scalar(dst[:, j, :], src[:, j, :], mv[:, j, 0:1], rs[:, j:j + 1],
                                         ALU.subtract, ALU.mult)

            def x_statistics(g):
                for j in range(GT):
                    dve.wait_ge(x_in[g % 2 * GT + j], 16 * (g // 2 + 1))
                statistics(a1_rows[g % 2])

            def first_norm(g):
                b = g // (NG // B)
                dve.wait_ge(rs_ready, 2 * g + 1)
                if g:
                    dve.wait_ge(h_read, GT * g)
                for j in range(GT):
                    last = norm_rows(j, hx, a1_rows[g % 2])
                link(last)
                if g == 0:
                    dve.wait_ge(bc_in, 16 * 2)
                for j in range(GT):
                    last = dve.tensor_tensor(hx[:, j, :], hx[:, j, :], bc_c[:, b, :], ALU.mult)
                link(last)
                for j in range(GT):
                    dve.tensor_tensor(hx[:, j, :], hx[:, j, :], bc_s[:, b, :], ALU.add).then_inc(h_ready, 1)
                dve.wait_ge(h_ready, GT * (g + 1))
                statistics(hx)

            def second_norm(g):
                dve.wait_ge(rs_ready, 2 * g + 2)
                if g:
                    dve.wait_ge(t_mm, DC * g)
                for j in range(GT):
                    norm_rows(j, xn, hx).then_inc(xn_ready, 1)

            def transposed_lo(g):
                for k in range(DC):
                    dve.wait_ge(t_hi, DC * g + k + 1)
                    dve.tensor_tensor(xt[:, g, 1, k, :], atmp[:, k % 2, :], xt[:, g, 0, k, :].bitcast(F32),
                                      ALU.subtract).then_inc(t_lo, 1)

            def turn_k(g):
                at = slice((g * GN) % S, (g * GN) % S + GN)
                dve.wait_ge(kv_copied, 8 * g + 2)
                dve.tensor_tensor(rk[:, 0, :], kv[:, 0, :], cos[:, at], ALU.mult)
                link(dve.tensor_tensor(rk[:, 1, :], kv[:, 1, :], sin[:, at], ALU.mult))
                dve.tensor_tensor(kv[:, 0, :], kv[:, 0, :], sin[:, at], ALU.mult)
                link(dve.tensor_tensor(kv[:, 1, :], kv[:, 1, :], cos[:, at], ALU.mult))
                link(dve.tensor_tensor(kv[:, 1, :], kv[:, 0, :], kv[:, 1, :], ALU.add))
                link(dve.tensor_tensor(kv[:, 0, :], rk[:, 0, :], rk[:, 1, :], ALU.subtract))
                dve.wait_ge(v_turned, g + 1)
                dve.tensor_tensor(kv[:, 0, :], kv[:, 0, :], kv[:, 2, :], ALU.mult).then_inc(prod, 1)
                dve.tensor_tensor(kv[:, 1, :], kv[:, 1, :], kv[:, 3, :], ALU.mult).then_inc(prod, 1)

            def product(g, m):
                dve.wait_ge(kv_copied, 8 * g + 2 * m + 2)
                s = (0, 0, 2, 4)[m]
                dve.tensor_tensor(kv[:, s, :], kv[:, s, :], kv[:, 3, :], ALU.mult).then_inc(prod, 1)

            def sum_products(g):
                dve.wait_ge(w_mm, g + 1)
                dve.wait_ge(prod, DC * (g + 1))
                for m in range(DC):
                    weighted = kv[:, (0, 1, 2, 4)[m], :]
                    dve.tensor_tensor_reduce(out=weighted, in0=weighted,
                                             in1=bank[W_BANK][:, :], scale=1.0, scalar=0.0, op0=ALU.mult,
                                             op1=ALU.add, accum_out=a_part[:, g, m:m + 1]).then_inc(a_done, 1)

            def finish_a(b):
                n = NG // B
                dve.wait_ge(a_done, DC * n * (b + 1))
                link(dve.tensor_tensor(a_col[:, b, 0, :], a_part[:, n * b, :], a_part[:, n * b + 1, :], ALU.add))
                link(dve.tensor_scalar(a_col[:, b, 0, :], a_col[:, b, 0, :], 0.5, 0.5, ALU.mult, ALU.add))
                dve.tensor_tensor(a_col[:, b, 1, :], a_col[:, b, 0, :], b_col[:, 2, :], ALU.mult).then_inc(a_ready, 1)

            x_statistics(0)
            mod_vector(0)
            mod_vector(1)
            for n in range(4, 8):
                split_lo(n)
            first_norm(0)
            second_norm(0)
            transposed_lo(0)
            mod_vector(2)
            dve.wait_ge(table_in, 16 * 3)
            for g in range(NG):
                if g + 1 < NG:
                    x_statistics(g + 1)
                if g:
                    sum_products(g - 1)
                if g == 2:
                    finish_a(0)
                if g + 1 < NG:
                    first_norm(g + 1)
                turn_k(g)
                if g + 1 < NG:
                    second_norm(g + 1)
                product(g, 2)
                if g + 1 < NG:
                    transposed_lo(g + 1)
                else:
                    split_lo(16)
                    split_lo(17)
                product(g, 3)
                dve.wait_ge(sq_mm, 8 * (g + 1))
                if g:
                    dve.wait_ge(w_ready, g)
                dve.tensor_copy(nrm[:, :, :], bank[NORM_BANK][:, 0:2 * GT].rearrange("p (t k) -> p t k", k=2))\
                    .then_inc(nrm_ready, 1)
                if g < 3:
                    mod_vector(3 + g)
            sum_products(NG - 1)
            finish_a(1)
            split_lo(18)
            split_lo(19)

            def qa_lo_parts(g):
                for m in range(DC):
                    dve.wait_ge(qa_hi, DC * g + m + 1)
                    dve.tensor_tensor(qa[:, 1, m, :], tmp[:, m, :], qa[:, 0, m, :].bitcast(F32), ALU.subtract)\
                        .then_inc(qa_lo, 1)

            def residual(g):
                for j in range(GT):
                    t = GT * g + j
                    dve.wait_ge(y_mm, t + 1)
                    link(dve.tensor_tensor(ygate[:, j % 2, :], bank[Y_BANKS[t % 2]][:, :], bc_ga[:, g // (NG // B), :],
                                           ALU.mult))
                    dve.wait_ge(base_in[j], 16 * (g + 1))
                    dve.tensor_tensor(rows[:, j, :], rows[:, j, :], ygate[:, j % 2, :], ALU.add).then_inc(x2_ready, 1)
                dve.wait_ge(x2_ready, GT * (g + 1))
                statistics(rows)

            def ffn_norm(g):
                dve.wait_ge(rs_ready, 2 * NG + g + 1)
                if g:
                    dve.wait_ge(t2_mm, DC * g)
                    for j in range(GT):
                        dve.wait_ge(h2_out[j], 16 * g)
                for j in range(GT):
                    last = norm_rows(j, hx, rows)
                link(last)
                for j in range(GT):
                    dve.tensor_tensor(hx[:, j, :], hx[:, j, :], bc_c[:, g // (NG // B), :], ALU.mult)\
                        .then_inc(h2_half, 1)

            def transposed2_lo(g):
                for k in range(DC):
                    dve.wait_ge(t2_hi, DC * g + k + 1)
                    dve.tensor_tensor(xt[:, g, 1, k, :], tmp[:, k, :], xt[:, g, 0, k, :].bitcast(F32),
                                      ALU.subtract).then_inc(t2_lo, 1)

            def s_mul_of(g, m):
                n = NS * g + m
                r = SM[m]
                dve.wait_ge(s_silu, n + 1)
                dve.tensor_tensor(gbuf[n % 3][0:r, :], gbuf[n % 3][0:r, :], bank[UP_BANKS[m % 2]][0:r, :], ALU.mult)\
                    .then_inc(s_mul, 1)

            def s_lo_of(g, m):
                n = NS * g + m
                r = SM[m]
                dve.wait_ge(s_hi, n + 1)
                dve.tensor_tensor(gtS[0:r, 1, m, :], gbuf[n % 3][0:r, :], gtS[0:r, 0, m, :].bitcast(F32), ALU.subtract)\
                    .then_inc(s_lo, 1)

            def shared(g):
                for m in range(NS):
                    s_mul_of(g, m)
                    if m:
                        s_lo_of(g, m - 1)
                    if g == 0 and m >= 3:
                        split_lo(25 + m)
                s_lo_of(g, NS - 1)

            def shared_rows(g):
                b = g // (NG // B)
                for j in range(GT):
                    t = GT * g + j
                    dve.wait_ge(s_down_mm, t + 1)
                    link(dve.tensor_tensor(srow[:, t % 2, :], bank[DOWN_BANKS[t % 2]][:, :], bc_gb[:, b, :], ALU.mult))
                    dve.wait_ge(x2_in[t % 2], 16 * (t // 2 + 1))
                    dve.tensor_tensor(xrow[:, t % 2, :], xrow[:, t % 2, :], srow[:, t % 2, :], ALU.add).then_inc(s_row, 1)

            full_e = [P, NT, E]

            def gate_scores():
                dve.wait_ge(lg_mm, NG)
                link(dve.tensor_copy(lg[:, :, :], bank[LG_BANK][:, 0:NT * E].rearrange("p (t e) -> p t e", e=E)))
                link(dve.tensor_reduce(mx[:, 0, :, 0], lg[:, :, :], AX.X, ALU.max))
                dve.tensor_tensor(sc[:, :, :], lg[:, :, :], mx[:, 0, :, :].to_broadcast(full_e), ALU.subtract)\
                    .then_inc(lg_ready, 1)

            def first():
                dve.wait_ge(exp_ready, 1)
                dve.wait_ge(tab_ready, 1)
                link(dve.tensor_reduce(mx[:, 0, :, 0], sc[:, :, :], AX.X, ALU.add))
                link(dve.reciprocal(mx[:, 1, :, 0], mx[:, 0, :, 0]))
                link(dve.tensor_tensor(sc[:, :, :], sc[:, :, :], mx[:, 1, :, :].to_broadcast(full_e), ALU.mult))
                top(0)
                link(dve.scalar_tensor_tensor(sc[:, :, :], oh[:, 0, :, :], -2.0, sc[:, :, :], ALU.mult, ALU.add))

            def second():
                top(1)
                dve.tensor_tensor(both[:, :, :], oh[:, 0, :, :], oh[:, 1, :, :], ALU.add).then_inc(both_ready, 1)

            def top(k):
                link(dve.tensor_reduce(wt[:, k, :, 0], sc[:, :, :], AX.X, ALU.max))
                link(dve.tensor_tensor(eq[:, :, :], sc[:, :, :], wt[:, k, :, :].to_broadcast(full_e), ALU.is_equal))
                link(dve.tensor_tensor(eq[:, :, :], eq[:, :, :], iota8[:, :, :], ALU.mult))
                link(dve.tensor_reduce(ix[:, k, :, 0], eq[:, :, :], AX.X, ALU.min))
                link(dve.tensor_tensor(oh[:, k, :, :], iota8[:, :, :], ix[:, k, :, :].to_broadcast(full_e), ALU.is_equal))

            def slots():
                dve.wait_ge(rank_mm, 1)
                src = bank[LG_BANK][:, NT * E:3 * NT * E].rearrange("p (i t e) -> p i t e", i=2, e=E)
                dve.tensor_copy(within[:, :, :], src[:, 0, :, :])
                link(dve.tensor_copy(upto[:, 0, :, :], src[:, 1, :, :]))
                dve.tensor_copy(upto[:, 1, :, :], upto[:, 0, :, :]).then_inc(rank_read, 1)
                dve.wait_ge(rank_read, 1)
                at, step = 1, 1
                while step < NT:
                    dve.tensor_copy(upto[:, 3 - at, 0:step, :], upto[:, at, 0:step, :])
                    link(dve.tensor_tensor(upto[:, 3 - at, step:NT, :], upto[:, at, step:NT, :],
                                           upto[:, at, 0:NT - step, :], ALU.add))
                    at, step = 3 - at, 2 * step
                link(dve.tensor_reduce(cntf[:, 0:1], upto[:, at, NT - 1, :], AX.X, ALU.max))
                link(dve.tensor_single_scalar(cntf[:, 1:2], cntf[:, 0:1], float(CAP), ALU.is_gt))
                for r in range(2, ROUNDS):
                    link(dve.scalar_tensor_tensor(cntf[:, 1:2], cntf[:, 0:1], float(CAP * r), cntf[:, 1:2], ALU.is_gt, ALU.add))
                link(dve.tensor_scalar(cntf[:, 1:2], cntf[:, 1:2], E / 2, E / 2, ALU.mult, ALU.add))
                dve.tensor_copy(loops[:, :], cntf[:, 1:2]).then_inc(loops_ready, 1)
                link(dve.tensor_tensor(upto[:, 0, :, :], upto[:, at, :, :], upto[:, 0, :, :], ALU.subtract))
                link(dve.tensor_tensor(within[:, :, :], within[:, :, :], upto[:, 0, :, :], ALU.add))
                for k in range(2):
                    link(dve.tensor_tensor(upto[:, 1 + k, :, :], oh[:, k, :, :], within[:, :, :], ALU.mult))
                    link(dve.tensor_reduce(rr[:, k, :, 0], upto[:, 1 + k, :, :], AX.X, ALU.add))

                def flat(a):
                    return a[:, :, :, :].rearrange("p k t o -> p (k t o)")

                link(dve.tensor_single_scalar(flat(rd), flat(rr), float(CAP), ALU.is_ge))
                for r in range(2, ROUNDS):
                    link(dve.scalar_tensor_tensor(flat(rd), flat(rr), float(CAP * r), flat(rd), ALU.is_ge, ALU.add))
                link(dve.scalar_tensor_tensor(flat(rr), flat(rd), -float(CAP), flat(rr), ALU.mult, ALU.add))
                link(dve.tensor_single_scalar(flat(qq), flat(rr), float(P), ALU.is_ge))
                for r in range(2, CT):
                    link(dve.scalar_tensor_tensor(flat(qq), flat(rr), float(P * r), flat(qq), ALU.is_ge, ALU.add))
                link(dve.scalar_tensor_tensor(flat(rr), flat(qq), -float(P), flat(rr), ALU.mult, ALU.add))
                link(dve.tensor_scalar(flat(sl), flat(ix), float(CT), float(E * CT), ALU.mult, ALU.add))
                link(dve.scalar_tensor_tensor(flat(sl), flat(rd), float(E * CT), flat(sl), ALU.mult, ALU.add))
                link(dve.tensor_tensor(flat(sl), flat(sl), flat(qq), ALU.add))
                link(dve.scalar_tensor_tensor(flat(sl), flat(rr), float(COLS), flat(sl), ALU.mult, ALU.add))
                link(dve.tensor_copy(sidx[:, :], flat(sl)))
                dve.tensor_copy(rec[:, :, :, :].bitcast(F32)[:, :, :, 1], wt[:, :, :, 0]).then_inc(slots_ready, 1)

            def columns():
                dve.wait_ge(tab_in, 16)
                bits = tab[:, :, :].bitcast(F32)[:, :, 1]
                dve.tensor_scalar_min(gidx[:, :], tab[:, :, 0], T - 1)
                dve.scalar_tensor_tensor(w01[:, 0, :], tab[:, :, 0], float(S), bits, ALU.is_lt, ALU.mult)
                link(dve.scalar_tensor_tensor(w01[:, 1, :], tab[:, :, 0], float(S), bits, ALU.is_ge, ALU.mult))
                dve.drain().then_inc(cols_ready, 1)

            def expert_lo(w, par, q):
                lo, hi = EW_PART[q]
                slot = (par + q) % 2
                dve.wait_ge(ew_hi, 3 * w + q + 1)
                parts = [(P, lo, hi, 0)]
                if q == 2:
                    full = H // P * D
                    parts = [(P, lo, lo + full, 0), (RM[-1], lo + full, hi, full)]
                for r, a, z, at in parts:
                    last = dve.tensor_tensor(ew[par][0:r, 1, a:z], ewst[0:r, slot, at:at + z - a],
                                             ew[par][0:r, 0, a:z].bitcast(F32), ALU.subtract)
                last.then_inc(ew_lo, 1)

            def picked_lo(w, par, steps):
                for s in steps:
                    dve.wait_ge(rt_hi, CT * w + s + 1)
                    src = bank[RT_BANKS[(par + s) % 2]][:, :]
                    at = (slice(s, s + 1), slice(0, GN)) if s < DC else (slice(0, DC), slice(GN, CAP))
                    src = src.rearrange("p (k t) -> p k t", k=1 if s < DC else DC)
                    dve.tensor_tensor(ht[par][:, 1, at[0], at[1]], src, ht[par][:, 0, at[0], at[1]].bitcast(F32),
                                      ALU.subtract).then_inc(rt_lo, 1)

            def turn_columns(w, par):
                dve.tensor_copy(wc[:, par, :, :], w01[:, :, bass.ds(w * CT, CT)]).then_inc(wc_ready, 1)

            def select_gb(u, par, j):
                dve.wait_ge(gs_ready, CT * u + j + 1)
                dve.scalar_tensor_tensor(gsel[:, j, :], bc_gb[:, 0, :], wc[:, par, 0, j:j + 1], gsel[:, j, :],
                                         ALU.mult, ALU.add).then_inc(gsel_ready, 1)

            def r_mul_of(u, c):
                half, m = divmod(c, NR)
                r = RM[m]
                dve.wait_ge(r_silu, 2 * NR * u + c + 1)
                dve.tensor_tensor(gbuf[c % 3][0:r, 0:HALF], gbuf[c % 3][0:r, 0:HALF], bank[UP_BANKS[c % 2]][0:r, 0:HALF], ALU.mult)\
                    .then_inc(r_mul, 1)

            def r_lo_of(u, c):
                half, m = divmod(c, NR)
                r, at = RM[m], slice(half * HALF, (half + 1) * HALF)
                dve.wait_ge(r_hi, 2 * NR * u + c + 1)
                dve.tensor_tensor(gtR[0:r, 1, m, at], gbuf[c % 3][0:r, 0:HALF], gtR[0:r, 0, m, at].bitcast(F32), ALU.subtract)\
                    .then_inc(r_lo, 1)

            def expert_rows(u, j, par):
                dve.wait_ge(down_mm, CT * u + j + 1 + 1)
                if j == 0:
                    dve.wait_ge(gsel_ready, CT * u + CT)
                    dve.wait_ge(added, u + 1)
                dve.tensor_tensor(y[:, j, :], bank[DOWN_BANKS[(par + j) % 2]][:, :], gsel[:, j, :], ALU.mult)\
                    .then_inc(y_ready, 1)

            qa_lo_parts(0)
            dve.wait_ge(bc_in, 16 * 5)
            for g in range(NG):
                for n in range(20 + 2 * g, 22 + 2 * g):
                    split_lo(n)
                residual(g)
                if g:
                    transposed2_lo(g - 1)
                ffn_norm(g)
                if g + 1 < NG:
                    qa_lo_parts(g + 1)
            shared(0)
            transposed2_lo(NG - 1)

            gate_scores()
            dve.wait_ge(bc_in, 16 * 6)
            first()
            shared_rows(0)
            second()
            shared(1)
            slots()
            shared_rows(1)
            shared(2)
            shared_rows(2)
            columns()
            expert_lo(0, 0, 0)
            expert_lo(0, 0, 1)
            shared(3)
            expert_lo(0, 0, 2)
            shared_rows(3)
            picked_lo(0, 0, range(CT))
            turn_columns(0, 0)
            for i in range(2):
                dve.wait_ge(s_out[i], 16 * NT // 2)
            dve.wait_ge(loops_ready, 1)
            n = nc.vector.value_load(loops[0:1, 0:1], min_val=E // 2, max_val=ROUNDS * E // 2)
            with dve.Fori(0, n) as i:
                for par in range(2):
                    u = 2 * i + par
                    for c in range(2 * NR):
                        r_mul_of(u, c)
                        if c:
                            r_lo_of(u, c - 1)
                        if c in EW_AT:
                            expert_lo(u + 1, 1 - par, EW_AT[c])
                        for j in GB_AT[c]:
                            select_gb(u, par, j)
                        if c and ROWS_AT[c - 1]:
                            picked_lo(u + 1, 1 - par, ROWS_AT[c - 1])
                    r_lo_of(u, 2 * NR - 1)
                    picked_lo(u + 1, 1 - par, ROWS_AT[2 * NR - 1])
                    for j in GB_AT[-1]:
                        select_gb(u, par, j)
                    turn_columns(u + 1, 1 - par)
                    for j in range(CT):
                        expert_rows(u, j, par)

        @block.tensor
        def _(pe):
            def product3(dst, a, b, first, last):
                nc.tensor.matmul(dst, a[0], b[0], start=first, stop=False)
                nc.tensor.matmul(dst, a[0], b[1], start=False, stop=False)
                return nc.tensor.matmul(dst, a[1], b[0], start=False, stop=last)

            def mod_matmul(i):
                w = MODS[i]
                if i:
                    pe.wait_ge(mod_row, i)
                if i > 3:
                    pe.wait_ge(a_done, DC * (i - 3))
                for h in range(2):
                    n = PIECES.index((w, h))
                    arrived(pe, n)
                    for k in range(2):
                        last = nc.tensor.matmul(bank[W_BANK][0:B, :], scT[:, 2 * h + k, :], piece_slot(n)[:, k * D:(k + 1) * D],
                                                start=h + k == 0, stop=h + k == 2)
                    last.then_inc(mod_mm, 1)

            def transposes(g):
                pe.wait_ge(xn_ready, GT * (g + 1))
                for k in range(DC):
                    n = DC * g + k
                    if n >= 2:
                        pe.wait_ge(t_hi, n - 1)
                    for j in range(GT):
                        last = nc.tensor.transpose(bank[T_BANKS[k % 2]][:, j * P:(j + 1) * P],
                                                   xn[:, j, k * P:(k + 1) * P], ident[:, :])
                    last.then_inc(t_mm, 1)

            def kv_matmul(g, n):
                i, m = KV_ORDER[n]
                N = 8 * g + n
                if N >= 4:
                    pe.wait_ge(sq_ready, N - 3)
                for k in range(DC):
                    if n == 0:
                        pe.wait_ge(t_lo, DC * g + k + 1)
                    last = product3(bank[KV_BANKS[n % 4]][:, :],
                                    [wkv[:, s, i, k, m * P:(m + 1) * P] for s in range(2)],
                                    [xt[:, g, s, k, :] for s in range(2)], k == 0, k == DC - 1)
                last.then_inc(kv_mm, 1)

            def square_sums(g, n):
                i, m = KV_ORDER[n]
                pe.wait_ge(sq_ready, 8 * g + n + 1)
                if n == 0 and g:
                    pe.wait_ge(nrm_ready, g)
                for j in range(GT):
                    last = nc.tensor.matmul(bank[NORM_BANK][:, 2 * j + i:2 * j + i + 1], sq[:, n % 2, j * P:(j + 1) * P],
                                            ones[:, 0:1], start=n == 0 and j == 0, stop=n == 7 and j == GT - 1,
                                            skip_group_check=True)
                last.then_inc(sq_mm, 1)

            def spread_weights(g):
                pe.wait_ge(w_ready, g + 1)
                pe.wait_ge(mod_row, min(4 + g, 6))
                if g:
                    pe.wait_ge(a_done, DC * g)
                for j in range(GT):
                    last = nc.tensor.matmul(bank[W_BANK][:, j * P:(j + 1) * P], wtok[:, j:j + 1].to_broadcast([P, P]),
                                            ident[:, :], start=True, stop=True)
                last.then_inc(w_mm, 1)

            def q_matmul(g, chunks=range(DC)):
                for m in chunks:
                    n = DC * g + m
                    if n >= 3:
                        pe.wait_ge(qa_hi, n - 2)
                    for k in range(DC):
                        last = product3(bank[Q_BANKS[n % 3]][:, :], [wq[:, s, k, m * P:(m + 1) * P] for s in range(2)],
                                        [xt[:, g, s, k, :] for s in range(2)], k == 0, k == DC - 1)
                    last.then_inc(q_mm, 1)

            pe.wait_ge(consts, 4)
            pe.wait_ge(sc_ready, 1)
            mod_matmul(0)
            mod_matmul(1)
            transposes(0)
            mod_matmul(2)
            pe.wait_ge(lo_done, 4)
            for g in range(NG):
                for n in range(8):
                    kv_matmul(g, n)
                    if n == 0 and g:
                        spread_weights(g - 1)
                    if n:
                        square_sums(g, n - 1)
                    if n == 7 and g + 1 < NG:
                        transposes(g + 1)
                if g < 3:
                    mod_matmul(3 + g)
                if g == NG - 1:
                    pe.wait_ge(lo_done, 6)
                    pe.wait_ge(sq_ready, 8 * NG)
                    q_matmul(0, range(3))
                square_sums(g, 7)
            spread_weights(NG - 1)
            q_matmul(0, range(3, DC))
            pe.wait_ge(lo_done, 8)

            def shared_gate_up(g):
                for m in range(NS):
                    n, r = NS * g + m, SM[m]
                    if n >= 2:
                        pe.wait_ge(s_mul, n - 1)
                    for i, to in enumerate((GATE_BANKS, UP_BANKS)):
                        for k in range(DC):
                            last = product3(bank[to[m % 2]][0:r, :], [sgu[:, s, i, k, m * P:m * P + r] for s in range(2)],
                                            [xt[:, g, s, k, :] for s in range(2)], k == 0, k == DC - 1)
                    last.then_inc(s_gu_mm, 1)

            def shared_down(g):
                for pair in range(GT // 2):
                    for chunks in (range(NS - 1), range(NS - 1, NS)):
                        for j in (2 * pair, 2 * pair + 1):
                            t = GT * g + j
                            if chunks[0] == 0 and t >= 2:
                                pe.wait_ge(s_row, t - 1)
                            for m in chunks:
                                if j == 0 or m == NS - 1:
                                    pe.wait_ge(s_lo, NS * g + m + 1)
                                r = SM[m]
                                last = product3(bank[DOWN_BANKS[t % 2]][:, :],
                                                [gtS[0:r, s, m, j * P:(j + 1) * P] for s in range(2)],
                                                [sd[0:r, s, m, :] for s in range(2)], m == 0, m == NS - 1)
                            if chunks[0]:
                                last.then_inc(s_down_mm, 1)

            def turn_rows(w, par, steps):
                for s in steps:
                    if s == 0:
                        pe.wait_ge(picked_in, 16 * CT * (w + 1))
                    if not isinstance(w, int) or s >= 2:
                        pe.wait_ge(rt_lo, CT * w + s - 1)
                    for i in range(DC):
                        j, k = (i, s) if s < DC else (DC, i)
                        last = nc.tensor.transpose(bank[RT_BANKS[(par + s) % 2]][:, i * P:(i + 1) * P],
                                                   picked[:, j, k * P:(k + 1) * P], ident[:, :])
                    last.then_inc(rt_mm, 1)

            def expert_gate_up(u, par):
                for c in range(2 * NR):
                    half, m = divmod(c, NR)
                    r, at = RM[m], slice(half * HALF, (half + 1) * HALF)
                    if c == 0:
                        pe.wait_ge(rt_lo, CT * u + CT)
                        pe.wait_ge(ew_lo, 3 * u + 2)
                    pe.wait_ge(r_mul, 2 * NR * u + max(c - 1, 0) + 1)
                    for i, to in enumerate((GATE_BANKS, UP_BANKS)):
                        for k in range(DC):
                            col = (i * DC + k) * H + m * P
                            last = product3(bank[to[c % 2]][0:r, 0:HALF], [ew[par][:, s, col:col + r] for s in range(2)],
                                            [ht[par][:, s, k, at] for s in range(2)], k == 0, k == DC - 1)
                    last.then_inc(gu_mm, 1)
                    turn_rows(u + 1, 1 - par, ROWS_AT[c])

            def expert_down(u, par):
                pe.wait_ge(ew_lo, 3 * u + 3)
                for j in range(CT):
                    if j == 0:
                        pe.wait_ge(r_lo, 2 * NR * u + NR + 1)
                    if j == 2:
                        pe.wait_ge(r_lo, 2 * NR * (u + 1) + 1)
                    pe.wait_ge(y_ready, CT * u + max(j - 1, 0) + 1)
                    for m in range(NR):
                        r, col = RM[m], 2 * DC * H + m * D
                        last = product3(bank[DOWN_BANKS[(par + j) % 2]][:, :],
                                        [gtR[0:r, s, m, j * P:(j + 1) * P] for s in range(2)],
                                        [ew[par][0:r, s, col:col + D] for s in range(2)], m == 0, m == NR - 1)
                    last.then_inc(down_mm, 1)

            def y_matmul(g):
                for pair in range(GT // 2):
                    for chunks in (range(DC - 1), range(DC - 1, DC)):
                        for j in (2 * pair, 2 * pair + 1):
                            t = GT * g + j
                            if chunks[0] == 0 and t >= 2:
                                pe.wait_ge(x2_ready, t - 1)
                            for m in chunks:
                                if j == 0 or m == DC - 1:
                                    pe.wait_ge(qa_lo, DC * g + m + 1)
                                last = product3(bank[Y_BANKS[t % 2]][:, :], [qa[:, s, m, j * P:(j + 1) * P] for s in range(2)],
                                                [wo[:, s, m, :] for s in range(2)], m == 0, m == DC - 1)
                            if chunks[0]:
                                last.then_inc(y_mm, 1)

            def transposes2(g):
                pe.wait_ge(h2_ready, GT * (g + 1))
                for k in range(DC):
                    n = DC * g + k
                    if n >= 2:
                        pe.wait_ge(t2_hi, n - 1)
                    for j in range(GT):
                        last = nc.tensor.transpose(bank[T2_BANKS[k % 2]][:, j * P:(j + 1) * P],
                                                   hx[:, j, k * P:(k + 1) * P], ident[:, :])
                    last.then_inc(t2_mm, 1)

            def gate_logits(g):
                pe.wait_ge(t2_hi, DC * (g + 1))
                for j in range(GT):
                    t = GT * g + j
                    for k in range(DC):
                        last = nc.tensor.matmul(bank[LG_BANK][:, t * E:(t + 1) * E], tmp[:, k, j * P:(j + 1) * P],
                                                gw[:, k, :], start=k == 0, stop=k == DC - 1)
                last.then_inc(lg_mm, 1)

            for g in range(NG):
                y_matmul(g)
                if g:
                    transposes2(g - 1)
                    gate_logits(g - 1)
                if g + 1 < NG:
                    q_matmul(g + 1)
            pe.wait_ge(lo_done, SPLITS.index(("sup", DC - 1)) + 1)
            shared_gate_up(0)
            pe.wait_ge(s_mul, NS)
            transposes2(NG - 1)
            gate_logits(NG - 1)

            pe.wait_ge(lo_done, len(SPLITS))
            for g in range(NG):
                if g:
                    if g == NG - 1:
                        pe.wait_ge(t2_lo, NT)
                    shared_gate_up(g)
                if g == 1:
                    pe.wait_ge(both_ready, 1)
                    for i, lhs in enumerate((upper, ones)):
                        last = nc.tensor.matmul(bank[LG_BANK][:, (1 + i) * NT * E:(2 + i) * NT * E], lhs[:, :],
                                                both[:, :, :].rearrange("p t e -> p (t e)"), start=True, stop=True)
                    last.then_inc(rank_mm, 1)
                shared_down(g)
            pe.wait_ge(rank_read, 1)
            turn_rows(0, 0, range(CT))
            pe.wait_ge(loops_ready, 1)
            n = nc.tensor.value_load(loops[0:1, 0:1], min_val=E // 2, max_val=ROUNDS * E // 2)
            with pe.Fori(0, n) as i:
                for par in range(2):
                    u = 2 * i + par
                    expert_gate_up(u, par)
                    expert_down(u, par)


_INS = ['L0_attn_X', 'L0_attn_W_in', 'L0_attn_b_in', 'L0_attn_W_out', 'L0_attn_b_out', 'L0_attn_gamma',
        'L0_attn_beta', 'L0_ffn_gate_w', 'L0_ffn_w_gate', 'L0_ffn_w_up', 'L0_ffn_w_down', 'L0_ffn_sw_gate',
        'L0_ffn_sw_up', 'L0_ffn_sw_down', 'L0_c', 'L0_wmod']


def rotary_tables():
    inv = np.float32(1.0) / np.float32(10000.0) ** (np.arange(0, ROT, 2, dtype=np.float32) / np.float32(ROT))
    angle = (np.arange(S, dtype=np.float32)[:, None] * inv[None, :].astype(np.float32)).T
    return np.ascontiguousarray(np.cos(angle)), np.ascontiguousarray(np.sin(angle))


def kernel(**inputs):
    import concourse.bacc as bacc
    from concourse.bass_utils import run_bass_kernel_spmd as run

    nc = bacc.Bacc("TRN2", target_bir_lowering=False, num_devices=1)
    arrays, args = {}, []

    def give(name, a):
        a = np.ascontiguousarray(a)
        arrays[name] = a
        args.append(nc.dram_tensor(name, a.shape, mybir.dt.from_np(a.dtype), kind="ExternalInput").ap())

    for name in _INS:
        a = np.asarray(inputs[name])
        give("in_" + name, a.reshape(T, D) if name == 'L0_attn_X' else a)
    for name, a in zip(("cos_table", "sin_table"), rotary_tables()):
        give(name, a)
    args.append(nc.dram_tensor("out_rows", (T + CAP, D), F32, kind="ExternalOutput").ap())
    build(nc, *args)
    r = run(nc, [arrays], core_ids=[0])
    return r.results[0]["out_rows"][:T].reshape(B, S, D)
```

```python
import numpy as np
import concourse.bass as bass
from concourse import mybir
from contextlib import ExitStack

F32, F32R, I32 = mybir.dt.float32, mybir.dt.float32r, mybir.dt.int32
ALU, ACT, AX = mybir.AluOpType, mybir.ActivationFunctionType, mybir.AxisListType

P = 128
B, S, D = 2, 1024, 512
T = B * S
NT = T // P
GT = 4
GN = GT * P
NG = T // GN
DC = D // P
ROT = D // 2
EPS = 1e-5
E, H, HS = 8, 352, 704
SM = [min(P, HS - P * m) for m in range(-(-HS // P))]
RM = [min(P, H - P * m) for m in range(-(-H // P))]
NS, NR = len(SM), len(RM)
CT = 5
CAP = CT * P
ROUNDS = -(-T // CAP)
COLS = ROUNDS * E * CT
TCOLS = COLS + 2 * CT
HALF = CAP // 2
EW = 2 * DC * H + NR * D

MOD = ["sa", "ca", "ga", "sb", "cb", "gb"]
WEIGHTS = ["sa", "ca", "K", "V", "ga", "sb", "cb", "gb", "Q", "O"]
PIECES = [(w, h) for w in WEIGHTS for h in range(2)]
PIECES += [(w, k) for k in range(DC) for w in ("sgate", "sup")]
PIECES += [("sdown", k) for k in range(NS // 2)]
MODS = [w for w in WEIGHTS if w in MOD]
EARLY = 8
SPLITS = [p for p in PIECES if p[0] not in MOD]


def build(nc, X, W_in, b_in, W_out, b_out, gamma, beta, gate_w, w_gate, w_up, w_down,
          sw_gate, sw_up, sw_down, c, wmod, cos_t, sin_t, out):
    def dram(name, shape, dt=F32):
        return nc.dram_tensor(name, shape, dt, kind="Internal").ap()

    mod_d = dram("mod_d", [B, 6 * D])
    base_d = dram("base_d", [T, D])
    x2_d = dram("x2_d", [T, D])
    h2_d = dram("h2_d", [T, D])
    slot_d = dram("slot_d", [P * COLS, 2], I32)

    ctx = ExitStack()
    with ctx:
        ctx.enter_context(nc.allow_non_contiguous_dma(reason="vectors of a few hundred values"))

        def sem(name):
            return ctx.enter_context(nc.semaphore(name))

        def region(stack):
            return lambda name, shape, dt=F32: stack.enter_context(nc.sbuf_tensor(name, shape, dt))

        sb = region(ctx)

        with ExitStack() as r_phase:
            al = region(r_phase)
            ew0 = al("ew0", [P, 2, EW], F32R)
            ht0 = al("ht0", [P, 2, DC, CAP], F32R)
            picked = al("picked", [P, CT, D])
        with ExitStack() as start:
            al = region(start)
            al("xt_head", [P, NG // 2, 2 * DC * GN])
            early = al("early", [P, EARLY, 2 * D])
        xt = sb("xt", [P, NG, 2, DC, GN], F32R)
        with ExitStack() as a1_phase:
            al = region(a1_phase)
            wkv = al("wkv", [P, 2, 2, DC, D], F32R)
            cos = al("cos", [P, S])
            sin = al("sin", [P, S])
            sq = al("sq", [P, 2, GN])
        with ExitStack() as r_phase:
            ew1 = region(r_phase)("ew1", [P, 2, EW], F32R)
        sgu = sb("sgu", [P, 2, DC, 2 * HS], F32R)
        UP_LAST, UP_COL = HS, HS + SM[-1]
        bc_s = sb("bc_s", [P, B, D])
        bc_c = sb("bc_c", [P, B, D])
        bc_ga = sb("bc_ga", [P, B, D])
        bc_gb = sb("bc_gb", [P, B, D])
        bout, mabs = bc_gb[:, 0, :], bc_gb[0:B, 1, :]
        ident = sb("ident", [P, P])
        ones = sb("ones", [P, P])
        upper = sb("upper", [P, P])
        nhalf = sb("nhalf", [P, 2 * GT])
        cT = sb("cT", [P, DC, B])
        scT = sb("scT", [P, DC, B])
        gb_col = sb("gb_col", [P, 2, DC])
        b_col = sb("b_col", [P, 3, DC])
        a_part = sb("a_part", [P, NG, DC])
        a_col = sb("a_col", [P, B, 2, DC])
        st6 = sb("st6", [P, GT, 6])
        mv = sb("mv", [P, GT, 2])
        ve = sb("ve", [P, GT])
        rs = sb("rs", [P, GT])
        nrm = sb("nrm", [P, GT, 2])
        rnm = sb("rnm", [P, GT, 2])
        wtok = sb("wtok", [P, GT])
        gw = sb("gw", [P, DC, E])
        lg = sb("lg", [P, NT, E])
        cntf = sb("cntf", [P, 2])
        loops = sb("loops", [P, 1], I32)
        gi = sb("gi", [P, 2, CT], I32)
        si = sb("si", [P, 2, CT], I32)
        wc = sb("wc", [P, 2, 2, CT])
        begin = sb("begin", [P, 5])
        with ExitStack() as a_phase:
            al = region(a_phase)
            with ExitStack() as a1_phase:
                al1 = region(a1_phase)
                rows1 = al1("rows1", [P, GT, D])
                rk = al1("rk", [P, 2, GN])
                rv = al1("rv", [P, 2, GN])
            wq = al("wq", [P, 2, DC, D], F32R)
            with ExitStack() as a1_phase:
                al1 = region(a1_phase)
                xn = al1("xn", [P, GT, D])
                hb = al1("hb", [P, 2, D])
                v12 = al1("v12", [P, 2, GN])
            wo = al("wo", [P, 2, DC, D], F32R)
            with ExitStack() as a1_phase:
                al1 = region(a1_phase)
                atmp = al1("atmp", [P, 2, GN])
                kt = al1("kt", [P, 2, DC, GN])
                v03 = al1("v03", [P, GN])
                mrow = al1("mrow", [B, D])
            qa = al("qa", [P, 2, DC, GN], F32R)
            tmp = al("tmp", [P, DC, GN])
            stage = al("stage", [P, 2, 2 * D])
            rows = al("rows", [P, GT, D])
            hx = al("hx", [P, GT, D])
        with ExitStack() as s_phase:
            al = region(s_phase)
            with ExitStack() as r_phase:
                al2 = region(r_phase)
                gtR = al2("gtR", [P, 2, NR, CAP], F32R)
                y = al2("y", [P, CT, D])
                gsel = al2("gsel", [P, CT, D])
                ht1 = al2("ht1", [P, 2, DC, CAP], F32R)
            sd = al("sd", [P, 2, NS, D], F32R)
            gtS = al("gtS", [P, 2, NS, GN], F32R)
            xrow = al("xrow", [P, 2, D])
            srow = al("srow", [P, 2, D])
            with ExitStack() as routing:
                al2 = region(routing)
                iota8 = al2("iota8", [P, NT, E])
                sc = al2("sc", [P, NT, E])
                eq = al2("eq", [P, NT, E])
                oh = al2("oh", [P, 2, NT, E])
                both = al2("both", [P, NT, E])
                within = al2("within", [P, NT, E])
                upto = al2("upto", [P, 3, NT, E])
                mx = al2("mx", [P, 2, NT, 1])
                wt = al2("wt", [P, 2, NT, 1])
                ix = al2("ix", [P, 2, NT, 1])
                rr = al2("rr", [P, 2, NT, 1])
                rd = al2("rd", [P, 2, NT, 1])
                qq = al2("qq", [P, 2, NT, 1])
                sl = al2("sl", [P, 2, NT, 1])
                sidx = al2("sidx", [P, 2 * NT], I32)
                rec = al2("rec", [P, 2, NT, 2], I32)
            ewst = al("ewst", [P, 2, NR * D])
            tab = al("tab", [P, TCOLS, 2], I32)
            w01 = al("w01", [P, 2, TCOLS])
            gidx = al("gidx", [P, TCOLS], I32)
        gbuf = [a[:, 0, :] for a in (bc_s, bc_c, bc_ga)]

        a1_rows = (rows, rows1)
        ygate = bc_gb

        bank = [ctx.enter_context(nc.psum_tensor(f"bank{i}", [P, GN], F32)) for i in range(8)]
        T_BANKS, KV_BANKS, NORM_BANK, W_BANK = (0, 1), (2, 3, 4, 5), 6, 7
        GATE_BANKS, UP_BANKS, DOWN_BANKS, RT_BANKS = (2, 4), (3, 5), (6, 7), (0, 1)
        Q_BANKS, Y_BANKS, LG_BANK, FIRST_BANKS = (2, 3, 4), (6, 7, 0, 5), 1, (2, 3, 4, 5)

        def t2_bank(g, k):
            if g == NG - 1:
                return bank[Y_BANKS[k]]
            return bank[Q_BANKS[(DC * (g + 2) + 1 + k) % 3] if k < 2 else Y_BANKS[k]]

        def s_down_bank(t):
            return bank[(6, 7, 0)[t % 3] if t < NT - GT else (6, 7)[t % 2]]

        consts = sem("consts")
        small_in, bias_in, table_in = sem("small_in"), sem("bias_in"), sem("table_in")
        c_in = sem("c_in")
        sc_ready = sem("sc_ready")
        early_in = [sem(f"early_in{i}") for i in range(EARLY)]
        piece_in = [sem(f"piece_in{i}") for i in range(2)]
        mod_mm, mod_row, mod_out = sem("mod_mm"), sem("mod_row"), sem("mod_out")
        first_mm, first_read = sem("first_mm"), sem("first_read")
        bc_in = [sem(f"bc_in{i}") for i in range(len(MODS))]
        bout_in = sem("bout_in")
        hi_done, lo_done = sem("hi_done"), sem("lo_done")
        x_in = [sem(f"x_in{j}") for j in range(2 * GT)]
        dve_step, pool_step = sem("dve_step"), sem("pool_step")
        ve_ready, rs_ready = sem("ve_ready"), sem("rs_ready")
        h_ready, h_read, base_ready = sem("h_ready"), sem("h_read"), sem("base_ready")
        base_out = [sem(f"base_out{j}") for j in range(2 * GT)]
        xn_ready, t_mm, t_hi, t_lo = sem("xn_ready"), sem("t_mm"), sem("t_hi"), sem("t_lo")
        kv_mm, kv_copied, sq_ready, sq_mm = sem("kv_mm"), sem("kv_copied"), sem("sq_ready"), sem("sq_mm")
        v_turned, prod, nrm_ready, w_ready = sem("v_turned"), sem("prod"), sem("nrm_ready"), sem("w_ready")
        w_mm, a_done, a_ready = sem("w_mm"), sem("a_done"), sem("a_ready")
        q_mm, qa_hi, qa_lo, y_mm = sem("q_mm"), sem("qa_hi"), sem("qa_lo"), sem("y_mm")
        base_in = [sem(f"base_in{j}") for j in range(GT)]
        x2_ready, h2_half, h2_ready = sem("x2_ready"), sem("h2_half"), sem("h2_ready")
        x2_out = [sem(f"x2_out{j}") for j in range(GT)]
        h2_out = [sem(f"h2_out{j}") for j in range(GT)]
        t2_mm, t2_hi, t2_lo, lg_mm = sem("t2_mm"), sem("t2_hi"), sem("t2_lo"), sem("lg_mm")

        slot0_out, slot_out, tab_in = sem("slot0_out"), sem("slot_out"), sem("tab_in")
        pad_in, tab_ready = sem("pad_in"), sem("tab_ready")
        lg_ready, exp_ready = sem("lg_ready"), sem("exp_ready")
        both_ready, rank_mm, rank_read = sem("both_ready"), sem("rank_mm"), sem("rank_read")
        slots_ready, loops_ready, cols_ready = sem("slots_ready"), sem("loops_ready"), sem("cols_ready")
        s_gu_mm, s_silu, s_mul, s_hi, s_lo = sem("s_gu_mm"), sem("s_silu"), sem("s_mul"), sem("s_hi"), sem("s_lo")
        s_down_mm, s_row = sem("s_down_mm"), sem("s_row")
        x2_in = [sem(f"x2_in{i}") for i in range(2)]
        s_out = [sem(f"s_out{i}") for i in range(2)]
        ew_in = [sem(f"ew_in{q}") for q in range(3)]
        ew_hi, ew_lo = sem("ew_hi"), sem("ew_lo")
        gi_ready, si_ready, picked_in = sem("gi_ready"), sem("si_ready"), sem("picked_in")
        wc_ready, gs_ready, gsel_ready = sem("wc_ready"), sem("gs_ready"), sem("gsel_ready")
        rt_mm, rt_hi, rt_lo = sem("rt_mm"), sem("rt_hi"), sem("rt_lo")
        gu_mm, r_silu, r_mul, r_hi, r_lo = sem("gu_mm"), sem("r_silu"), sem("r_mul"), sem("r_hi"), sem("r_lo")
        down_mm, y_ready, y_out, added = sem("down_mm"), sem("y_ready"), sem("y_out"), sem("added")

        ew, ht = (ew0, ew1), (ht0, ht1)
        EW_AT = {0: 0, 1: 1, 3: 2}
        ROWS_AT = [(), (0, 1), (), (2, 3), (), (4,)]
        GB_AT = [(), (), (0,), (), (1, 2), (3,), (4,)]
        EW_PART = [(0, DC * H), (DC * H, 2 * DC * H), (2 * DC * H, EW)]

        def arrived(eng, n):
            if n < EARLY:
                return eng.wait_ge(early_in[n], 16)
            n -= EARLY
            eng.wait_ge(piece_in[n % 2], 16 * (n // 2 + 1 + (n == len(PIECES) - EARLY - 1)))

        def piece_slot(n):
            return early[:, n, :] if n < EARLY else stage[:, n % 2, :]

        def tile_rows(ap, t):
            return ap[t * P:(t + 1) * P, :]

        KV_ORDER = [(0, 0), (0, 1), (1, 0), (1, 1), (0, 2), (1, 2), (0, 3), (1, 3)]

        def kv_slot(g, i, m):
            if i == 0:
                return kt[:, g % 2, m, :]
            return v12[:, m - 1, :] if m in (1, 2) else v03[:, :]

        def split_views(n, part):
            w, h = PIECES[n]
            src = piece_slot(n)
            if w in ("sgate", "sup"):
                if w == "sgate":
                    return [(sgu[:, part, h, 0:HS], src[:, 0:HS])]
                full = HS - SM[-1]
                return [(sgu[:, part, h, UP_LAST:UP_COL], src[:, full:HS]), (sgu[:, part, h, UP_COL:], src[:, 0:full])]
            if w == "sdown":
                return [(sd[0:SM[m], part, m, :], src[0:SM[m], (m % 2) * D:(m % 2 + 1) * D]) for m in (2 * h, 2 * h + 1)]
            ks = slice(2 * h, 2 * h + 2)
            src = src.rearrange("p (k n) -> p k n", k=2)
            if w == "O":
                return [(wo[:, part, ks, :], src)]
            dst = wq[:, part, ks, :] if w == "Q" else wkv[:, part, w == "V", ks, :]
            return [(dst[:, :, 0:ROT].rearrange("p k (two f) -> p k two f", two=2),
                     src[:, :, 0:ROT].rearrange("p k (f two) -> p k two f", two=2)),
                    (dst[:, :, ROT:D], src[:, :, ROT:D])]

        block = ctx.enter_context(nc.Block())

        @block.sync
        def _(sp):
            def load_piece(n):
                if n >= EARLY + 2:
                    w, h = PIECES[n - 2]
                    if w in MOD:
                        sp.wait_ge(mod_mm, 2 * (MODS.index(w) - 2) + h + 1)
                    else:
                        sp.wait_ge(lo_done, SPLITS.index(PIECES[n - 2]) + 1)
                w, h = PIECES[n]
                dst = piece_slot(n)
                arrives = early_in[n] if n < EARLY else piece_in[n % 2]
                half = slice(2 * h * P, 2 * (h + 1) * P)
                if w in ("sgate", "sup"):
                    src = (sw_gate if w == "sgate" else sw_up)[h * P:(h + 1) * P, :]
                    sp.dma_start(dst[:, 0:HS], src).then_inc(piece_in[n % 2], 16)
                    return
                if w == "sdown":
                    at = 2 * h * P
                    dst = dst.rearrange("p (k n) -> p k n", k=2)
                    if n < len(PIECES) - 1:
                        sp.dma_start(dst, sw_down[at:at + 2 * P, :].rearrange("(k p) n -> p k n", k=2))\
                            .then_inc(piece_in[n % 2], 16)
                    else:
                        sp.dma_start(dst[:, 0, :], sw_down[at:at + P, :]).then_inc(piece_in[n % 2], 16)
                        sp.dma_start(dst[0:SM[-1], 1, :], sw_down[at + P:HS, :]).then_inc(piece_in[n % 2], 16)
                    return
                dst = dst.rearrange("p (k n) -> p k n", k=2)
                if w == "O" and h == 0:
                    src = W_out[0:ROT, :].rearrange("(p k) n -> p k n", k=2)
                elif w == "O":
                    src = W_out[half, :].rearrange("(k p) n -> p k n", k=2)
                else:
                    col = D * ("Q", "K", "V").index(w) if w in "QKV" else D * MOD.index(w)
                    src = (W_in if w in "QKV" else wmod)[half, col:col + D].rearrange("(k p) n -> p k n", k=2)
                sp.dma_start(dst, src).then_inc(arrives, 16)

            def load_x(t):
                slot, g = t % (2 * GT), t // GT
                if g >= 2:
                    sp.wait_ge(base_out[slot], 16 * (g // 2))
                sp.dma_start(a1_rows[g % 2][:, t % GT, :], tile_rows(X, t)).then_inc(x_in[slot], 16)

            def store_base(t):
                slot, g = t % (2 * GT), t // GT
                sp.wait_ge(base_ready, t + 1)
                sp.dma_start(tile_rows(base_d, t), a1_rows[g % 2][:, t % GT, :]).then_inc(base_out[slot], 16)

            def store_mod(i):
                col = D * MOD.index(MODS[i])
                sp.wait_ge(mod_row, i - 1)
                sp.dma_start(mod_d[:, col:col + D], mrow[:, :]).then_inc(mod_out, 16)

            def spread_mod(i):
                w = MODS[i]
                col = D * MOD.index(w)
                sp.wait_ge(mod_out, 16 * (i - 1))
                dst = {"ga": bc_ga, "sb": bc_s, "cb": bc_c, "gb": bc_gb}[w]
                if w in ("sb", "cb"):
                    sp.wait_ge(h_ready, NT)
                if w == "gb":
                    sp.wait_ge(h_read, NT)
                    sp.wait_ge(x2_ready, NT)
                sp.dma_start(dst[:, :, :], mod_d[:, col:col + D].partition_broadcast(P)).then_inc(bc_in[i], 16)

            for b in range(B):
                sp.dma_start(cT[:, :, b], c[b, :].rearrange("(k p) -> p k", p=P)).then_inc(c_in, 16)
            for n in range(4):
                load_piece(n)
            for t in range(GT):
                load_x(t)
            for n in range(4, EARLY):
                load_piece(n)
            sp.dma_start(gb_col[:, 0, :], gamma.rearrange("(k p) -> p k", p=P)).then_inc(small_in, 16)
            sp.dma_start(gb_col[:, 1, :], beta.rearrange("(k p) -> p k", p=P)).then_inc(small_in, 16)
            load_piece(8)
            load_piece(9)
            sp.dma_start(bout, b_out.partition_broadcast(P)).then_inc(bout_in, 16)
            for i, part in enumerate((1, 2, 0)):
                seg = b_in[part * D:(part + 1) * D]
                sp.dma_start(b_col[:, i, 0:2], seg[0:ROT].rearrange("(p k) -> p k", k=2)).then_inc(bias_in, 16)
                sp.dma_start(b_col[:, i, 2:4], seg[ROT:D].rearrange("(k p) -> p k", p=P)).then_inc(bias_in, 16)
            for t in range(GT, 2 * GT):
                load_x(t)
            sp.dma_start(cos[:, :], cos_t).then_inc(table_in, 16)
            sp.dma_start(sin[:, :], sin_t).then_inc(table_in, 16)
            sp.dma_start(gw[:, :, :], gate_w.rearrange("(k p) e -> p k e", p=P)).then_inc(table_in, 16)
            store_mod(2)
            spread_mod(2)
            load_piece(10)
            load_piece(11)
            for t in range(GT):
                store_base(t)
                load_x(2 * GT + t)
            store_mod(3)
            load_piece(12)
            load_piece(13)
            for t in range(GT, 2 * GT):
                store_base(t)
                load_x(2 * GT + t)
            store_mod(4)
            load_piece(14)
            load_piece(15)
            for t in range(2 * GT, NT):
                store_base(t)
            store_mod(5)
            load_piece(16)
            load_piece(17)
            spread_mod(3)
            spread_mod(4)
            load_piece(18)
            load_piece(19)

            def load_base(t):
                j = t % GT
                for slot in (j, GT + j):
                    sp.wait_ge(base_out[slot], 16 * NG // 2)
                if t >= GT:
                    sp.wait_ge(x2_out[j], 16 * (t // GT))
                    sp.wait_ge(h2_half, t - GT + 1)
                sp.dma_start(rows[:, j, :], tile_rows(base_d, t)).then_inc(base_in[j], 16)

            for t in range(GT):
                load_base(t)
            load_piece(20)
            load_piece(21)
            for g in range(NG):
                for j in range(GT):
                    t = g * GT + j
                    sp.wait_ge(x2_ready, t + 1)
                    sp.dma_start(tile_rows(x2_d, t), rows[:, j, :]).then_inc(x2_out[j], 16)
                load_piece(22 + 2 * g)
                load_piece(23 + 2 * g)
                for j in range(GT):
                    t = g * GT + j
                    if g + 1 < NG:
                        load_base(t + GT)
                    sp.wait_ge(h2_ready, t + 1)
                    sp.dma_start(tile_rows(h2_d, t), hx[:, j, :]).then_inc(h2_out[j], 16)
                if g == 0:
                    sp.dma_start(out[T:T + CAP, :], X[0:CAP, :]).then_inc(pad_in, 16)
            load_piece(30)
            spread_mod(5)
            sp.wait_ge(tab_ready, 1)
            sp.dma_start(slot_d.rearrange("(p c) two -> p c two", p=P), tab[:, 0:COLS, :]).then_inc(slot0_out, 16)

            def load_x2(t):
                if t >= 2:
                    sp.wait_ge(s_out[t % 2], 16 * (t // 2))
                sp.wait_ge(x2_out[t % GT], 16 * (t // GT + 1))
                sp.dma_start(xrow[:, t % 2, :], tile_rows(x2_d, t)).then_inc(x2_in[t % 2], 16)

            def store_s(t):
                sp.wait_ge(s_row, t + 1)
                sp.dma_start(tile_rows(out, t), xrow[:, t % 2, :]).then_inc(s_out[t % 2], 16)
                if t + 2 < NT:
                    load_x2(t + 2)

            def load_expert(w, par, pieces=range(3)):
                e = w % E if isinstance(w, int) else sp.snap(w % E)
                before = None if isinstance(w, int) else [sp.snap(3 * w + q - 1) for q in range(3)]
                for q in pieces:
                    slot = (par + q) % 2
                    if before:
                        sp.wait_ge(ew_lo, before[q])
                    elif q == 2:
                        sp.wait_ge(ew_lo, 1)
                    if q < 2:
                        src = (w_gate, w_up)[q][bass.ds(e, 1), :, :].rearrange("e (k p) n -> p (e k) n", p=P)
                        dst = ewst[:, slot, 0:DC * H].rearrange("p (k n) -> p k n", k=DC)
                        sp.dma_start(dst, src).then_inc(ew_in[q], 16)
                    else:
                        full = H // P
                        dst = ewst[:, slot, 0:full * D].rearrange("p (k n) -> p k n", k=full)
                        src = w_down[bass.ds(e, 1), 0:full * P, :].rearrange("e (k p) n -> p (e k) n", p=P)
                        sp.dma_start(dst, src).then_inc(ew_in[q], 16)
                        sp.dma_start(ewst[0:RM[-1], slot, full * D:NR * D],
                                     w_down[bass.ds(e, 1), full * P:H, :].rearrange("e p n -> p (e n)"))\
                            .then_inc(ew_in[q], 16)

            sp.wait_ge(t2_lo, NT)
            sp.wait_ge(lg_mm, NG)
            load_x2(0)
            load_x2(1)
            for t in range(NT):
                if t == 2 * GT:
                    sp.wait_ge(slot_out, 16 * 2 * NT)
                    sp.dma_start(tab[:, 0:COLS, :], slot_d.rearrange("(p c) two -> p c two", p=P)).then_inc(tab_in, 16)
                    sp.wait_ge(lo_done, len(SPLITS))
                    load_expert(0, 0, (0, 1))
                if t == 3 * GT:
                    load_expert(0, 0, (2,))
                store_s(t)
            sp.wait_ge(loops_ready, 1)
            n = nc.sync.value_load(loops[0:1, 0:1], min_val=E // 2, max_val=ROUNDS * E // 2)
            with sp.Fori(0, n) as i:
                for par in range(2):
                    load_expert(2 * i + par + 1, 1 - par)

        @block.gpsimd
        def _(pool):
            steps = [0]

            def link(ins):
                steps[0] += 1
                ins.then_inc(pool_step, 1)
                pool.wait_ge(pool_step, steps[0])

            for i, begun in enumerate((added, y_ready, down_mm, r_lo, r_mul)):
                pool.memset(begin[:, i:i + 1], 0.0).then_inc(begun, 1)
            pool.memset(ones[:, :], 1.0).then_inc(consts, 1)
            pool.memset(nhalf[:, :], -0.5).then_inc(consts, 1)
            link(pool.memset(ident[:, :], 0.0))
            pool.affine_select(out=ident[:, :], in_=ident[:, :], compare_op=ALU.not_equal, fill=1.0,
                               base=0, pattern=[[-1, P]], channel_multiplier=1).then_inc(consts, 1)
            pool.wait_ge(consts, 3)
            pool.affine_select(out=upper[:, :], in_=ones[:, :], compare_op=ALU.is_gt, fill=0.0,
                               base=0, pattern=[[1, P]], channel_multiplier=-1).then_inc(consts, 1)

            def norm_power(n):
                pool.wait_ge(ve_ready, n + 1)
                pool.tensor_tensor(rs[:, :], ve[:, :], nhalf[:, 0:GT], ALU.pow).then_inc(rs_ready, 1)

            def hb_slot(g, j):
                return (rv if g == 0 and j >= 2 else hb)[:, j % 2, :]

            def add_bias(g, j):
                pool.wait_ge(h_ready, GT * g + j + 1)
                if g:
                    pool.wait_ge(base_ready, GT * g + j - 1)
                pool.tensor_tensor(hb_slot(g, j), hx[:, j, :], bout, ALU.add).then_inc(h_read, 1)

            def finish_base(g, j):
                row = a1_rows[g % 2][:, j, :]
                pool.wait_ge(h_read, GT * g + j + 1)
                link(pool.tensor_tensor(hb_slot(g, j), hb_slot(g, j), bc_ga[:, g // (NG // B), :], ALU.mult))
                pool.tensor_tensor(row, row, hb_slot(g, j), ALU.add).then_inc(base_ready, 1)

            def base_start(g):
                for j in range(GT if g == 0 else 2):
                    add_bias(g, j)
                norm_power(2 * g + 1)

            def base_rest(g):
                finish_base(g, 0)
                if g:
                    add_bias(g, 2)
                finish_base(g, 1)
                if g:
                    add_bias(g, 3)
                finish_base(g, 2)
                finish_base(g, 3)

            def turn_v(g):
                at = slice((g * GN) % S, (g * GN) % S + GN)
                even, odd = kv_slot(g, 1, 0), kv_slot(g, 1, 1)
                pool.wait_ge(kv_copied, 8 * g + 4)
                if g == 0:
                    pool.wait_ge(base_ready, GT)
                pool.tensor_tensor(rv[:, 0, :], even, cos[:, at], ALU.mult)
                link(pool.tensor_tensor(rv[:, 1, :], odd, sin[:, at], ALU.mult))
                pool.tensor_tensor(even, even, sin[:, at], ALU.mult)
                link(pool.tensor_tensor(odd, odd, cos[:, at], ALU.mult))
                link(pool.tensor_tensor(odd, even, odd, ALU.add))
                pool.tensor_tensor(even, rv[:, 0, :], rv[:, 1, :], ALU.subtract).then_inc(v_turned, 1)

            def token_weights(g):
                pool.wait_ge(nrm_ready, g + 1)
                if g:
                    pool.wait_ge(w_mm, g)
                link(pool.tensor_tensor(rnm[:, :, :], nrm[:, :, :], nhalf[:, :].rearrange("p (t k) -> p t k", k=2), ALU.pow))
                pool.tensor_tensor(wtok[:, :], rnm[:, :, 0], rnm[:, :, 1], ALU.mult).then_inc(w_ready, 1)

            def split_kv_lo(n):
                arrived(pool, n)
                pool.wait_ge(hi_done, SPLITS.index(PIECES[n]) + 1)
                for (dst, src), (hi, _) in zip(split_views(n, 1), split_views(n, 0)):
                    last = pool.tensor_tensor(dst, src, hi.bitcast(F32), ALU.subtract)
                last.then_inc(lo_done, 1)

            norm_power(0)
            split_kv_lo(4)
            split_kv_lo(5)
            pool.wait_ge(bout_in, 16)
            base_start(0)
            split_kv_lo(6)
            split_kv_lo(7)
            norm_power(2)
            pool.wait_ge(bc_in[2], 16)
            base_rest(0)
            pool.wait_ge(table_in, 16 * 3)
            for g in range(NG):
                if g + 1 < NG:
                    if g:
                        norm_power(2 * g + 2)
                    base_start(g + 1)
                turn_v(g)
                if g + 1 < NG:
                    base_rest(g + 1)
                token_weights(g)

            pool.wait_ge(bc_in[3], 16)
            pool.wait_ge(bc_in[4], 16)
            for g in range(NG):
                norm_power(2 * NG + g)
                for j in range(GT):
                    pool.wait_ge(h2_half, GT * g + j + 1)
                    pool.tensor_tensor(hx[:, j, :], hx[:, j, :], bc_s[:, g // 2, :], ALU.add).then_inc(h2_ready, 1)

            for j in range(GT):
                pool.wait_ge(x2_out[j], 16 * NG)
            pool.wait_ge(lo_done, len(SPLITS))
            pool.iota(tab[:, :, 0], pattern=[[0, TCOLS // CT], [P, CT]], base=T, channel_multiplier=1)
            pool.memset(tab[:, :, 1], 0)
            pool.iota(rec[:, :, :, 0], pattern=[[0, 2], [P, NT]], base=0, channel_multiplier=1)
            pool.iota(iota8[:, :, :], pattern=[[0, NT], [1, E]], base=-E, channel_multiplier=0,
                      allow_small_or_imprecise_dtypes=True)
            pool.drain().then_inc(tab_ready, 1)

            pool.wait_ge(slots_ready, 1)
            pool.wait_ge(slot0_out, 16)
            for n in range(2 * NT):
                pool.indirect_dma_start(out=slot_d, out_offset=bass.IndirectOffsetOnAxis(ap=sidx[:, n:n + 1], axis=0),
                                        in_=rec[:, n // NT, n % NT, :], in_offset=None).then_inc(slot_out, 16)

            def gather(w, par):
                pool.tensor_copy(gi[:, par, :], gidx[:, bass.ds(w * CT, CT)]).then_inc(gi_ready, 1)
                pool.wait_ge(gi_ready, w + 1)
                if not isinstance(w, int) or w:
                    pool.wait_ge(rt_mm, CT * w)
                pool.nop(nofuse=True)
                for j in range(CT):
                    pool.indirect_dma_start(out=picked[:, j, :], out_offset=None, in_=h2_d,
                                            in_offset=bass.IndirectOffsetOnAxis(ap=gi[:, par, j:j + 1], axis=0))\
                        .then_inc(picked_in, 16)

            def scatter(u, par):
                pool.tensor_copy(si[:, par, :], tab[:, bass.ds(u * CT, CT), 0]).then_inc(si_ready, 1)
                pool.wait_ge(si_ready, u + 1)
                for j in range(CT):
                    pool.wait_ge(y_ready, CT * u + j + 1 + 1)
                    pool.nop(nofuse=True)
                    pool.indirect_dma_start(out=out, out_offset=bass.IndirectOffsetOnAxis(ap=si[:, par, j:j + 1], axis=0),
                                            in_=y[:, j, :], in_offset=None, compute_op=ALU.add).then_inc(y_out, 16)
                pool.wait_ge(y_out, 16 * CT * (u + 1))
                pool.nop(nofuse=True).then_inc(added, 1)

            pool.wait_ge(cols_ready, 1)
            pool.wait_ge(s_gu_mm, NS * NG)
            for j in range(GT):
                pool.wait_ge(h2_out[j], 16 * NG)
            gather(0, 0)
            gather(1, 1)
            pool.wait_ge(pad_in, 16)
            for i in range(2):
                pool.wait_ge(s_out[i], 16 * NT // 2)
            pool.wait_ge(loops_ready, 1)
            n = nc.gpsimd.value_load(loops[0:1, 0:1], min_val=E // 2, max_val=ROUNDS * E // 2)
            with pool.Fori(0, n) as i:
                for par in range(2):
                    gather(2 * i + par + 2, par)
                    scatter(2 * i + par, par)

        @block.scalar
        def _(act):
            def split_hi(n):
                w, h = PIECES[n]
                arrived(act, n)
                for dst, src in split_views(n, 0):
                    last = nc.scalar.activation(dst, src, ACT.Copy)
                last.then_inc(hi_done, 1)

            def transposed(g):
                for k in range(DC):
                    n = DC * g + k
                    act.wait_ge(t_mm, n + 1)
                    if n >= 2:
                        act.wait_ge(t_lo, n - 1)
                    src = bank[T_BANKS[k % 2]][:, :]
                    nc.scalar.activation(atmp[:, k % 2, :], src, ACT.Identity,
                                         bias=gb_col[:, 1, k:k + 1], scale=gb_col[:, 0, k:k + 1])
                    nc.scalar.activation(xt[:, g, 0, k, :], src, ACT.Identity, bias=gb_col[:, 1, k:k + 1],
                                         scale=gb_col[:, 0, k:k + 1]).then_inc(t_hi, 1)

            def copy_kv(g, n):
                i, m = KV_ORDER[n]
                N = 8 * g + n
                act.wait_ge(kv_mm, N + 1)
                if i == 0 and g >= 2:
                    act.wait_ge(a_done, DC * (g - 1))
                if i and (g or m == 3):
                    act.wait_ge(prod, DC * g + (0, -2, -1, 1)[m])
                bias = b_col[:, i, m:m + 1]
                src = bank[KV_BANKS[n % 4]][:, :]
                nc.scalar.activation(kv_slot(g, i, m), src, ACT.Identity, bias=bias).then_inc(kv_copied, 1)
                if N >= 2:
                    act.wait_ge(sq_mm, N - 1)
                nc.scalar.activation(sq[:, n % 2, :], src, ACT.Square, bias=bias).then_inc(sq_ready, 1)

            act.wait_ge(c_in, 16 * B)
            nc.scalar.activation(scT[:, :, :], cT[:, :, :], ACT.Silu).then_inc(sc_ready, 1)
            for n in range(4, 8):
                split_hi(n)
            act.wait_ge(small_in, 16 * 2)
            transposed(0)
            act.wait_ge(bias_in, 16 * 6)
            for g in range(NG):
                for n in range(7):
                    copy_kv(g, n)
                if g + 1 < NG:
                    transposed(g + 1)
                else:
                    for j in range(GT):
                        act.wait_ge(base_out[GT + j], 16 * NG // 2)
                    split_hi(16)
                    split_hi(17)
                copy_kv(g, 7)
            act.wait_ge(base_ready, NT)
            split_hi(18)
            split_hi(19)

            def scaled_q(g):
                b = g // 2
                act.wait_ge(a_ready, b + 1)
                for m in range(DC):
                    act.wait_ge(q_mm, DC * g + m + 1)
                    if g == 0:
                        act.wait_ge(t_lo, NT)
                        act.wait_ge(a_done, NT)
                    else:
                        act.wait_ge(y_mm, GT * g)
                    if g >= 2:
                        act.wait_ge(lg_mm, g - 1)
                        act.wait_ge(t2_lo, DC * (g - 1))
                    src = bank[Q_BANKS[(DC * g + m) % 3]][:, :]
                    col = dict(bias=a_col[:, b, 1, m:m + 1], scale=a_col[:, b, 0, m:m + 1])
                    nc.scalar.activation(tmp[:, m, :], src, ACT.Identity, **col)
                    nc.scalar.activation(qa[:, 0, m, :], src, ACT.Identity, **col).then_inc(qa_hi, 1)

            def transposed2(g):
                for k in range(DC):
                    n = DC * g + k
                    act.wait_ge(t2_mm, n + 1)
                    src = t2_bank(g, k)[:, :]
                    if k == 0:
                        act.wait_ge(qa_lo, DC * (g + 1))
                    nc.scalar.activation(tmp[:, k, :], src, ACT.Copy)
                    nc.scalar.activation(xt[:, g, 0, k, :], src, ACT.Copy).then_inc(t2_hi, 1)

            def s_silu_of(g, m):
                n = NS * g + m
                r = SM[m]
                act.wait_ge(s_gu_mm, n + 1)
                if n >= 3:
                    act.wait_ge(s_lo, n - 2)
                nc.scalar.activation(gbuf[n % 3][0:r, :], bank[GATE_BANKS[m % 2]][0:r, :], ACT.Silu).then_inc(s_silu, 1)

            def s_hi_of(g, m):
                n = NS * g + m
                r = SM[m]
                act.wait_ge(s_mul, n + 1)
                if g:
                    act.wait_ge(s_down_mm, GT * g)
                nc.scalar.activation(gtS[0:r, 0, m, :], gbuf[n % 3][0:r, :], ACT.Copy).then_inc(s_hi, 1)

            def shared(g):
                for m in range(NS):
                    if g == 0 and m == 4:
                        act.wait_ge(lg_mm, NG - 1)
                        act.wait_ge(t2_lo, DC * (NG - 1))
                        transposed2(NG - 1)
                    s_silu_of(g, m)
                    if m:
                        s_hi_of(g, m - 1)
                    if g == 0 and m >= 3:
                        split_hi(25 + m)
                s_hi_of(g, NS - 1)

            def expert_hi(w, par, q):
                lo, hi = EW_PART[q]
                slot = (par + q) % 2
                act.wait_ge(ew_in[q], (16 if q < 2 else 32) * (w + 1))
                if not isinstance(w, int):
                    act.wait_ge(down_mm, CT * (w - 1) + 1)
                if q < 2:
                    nc.scalar.activation(ew[par][:, 0, lo:hi], ewst[:, slot, 0:hi - lo], ACT.Copy).then_inc(ew_hi, 1)
                    return
                full = H // P * D
                nc.scalar.activation(ew[par][:, 0, lo:lo + full], ewst[:, slot, 0:full], ACT.Copy)
                nc.scalar.activation(ew[par][0:RM[-1], 0, lo + full:hi], ewst[0:RM[-1], slot, full:NR * D], ACT.Copy)\
                    .then_inc(ew_hi, 1)

            def picked_hi(w, par, steps):
                for s in steps:
                    act.wait_ge(rt_mm, CT * w + s + 1)
                    src = bank[RT_BANKS[(par + s) % 2]]
                    if s < DC:
                        nc.scalar.activation(ht[par][:, 0, s, 0:GN], src[:, :], ACT.Copy).then_inc(rt_hi, 1)
                    else:
                        nc.scalar.activation(ht[par][:, 0, :, GN:CAP], src[:, :].rearrange("p (k t) -> p k t", k=DC),
                                             ACT.Copy).then_inc(rt_hi, 1)

            def select_gb(u, par, j):
                if j == 0:
                    act.wait_ge(wc_ready, u + 1)
                    act.wait_ge(y_ready, CT * u + 1)
                nc.scalar.activation(gsel[:, j, :], bc_gb[:, 1, :], ACT.Copy, scale=wc[:, par, 1, j:j + 1])\
                    .then_inc(gs_ready, 1)

            def r_silu_of(u, par, c):
                half, m = divmod(c, NR)
                r = RM[m]
                act.wait_ge(gu_mm, 2 * NR * u + c + 1)
                act.wait_ge(r_lo, 2 * NR * u + max(c - 2, 0) + 1)
                nc.scalar.activation(gbuf[c % 3][0:r, 0:HALF], bank[GATE_BANKS[c % 2]][0:r, 0:HALF], ACT.Silu)\
                    .then_inc(r_silu, 1)

            def r_hi_of(u, par, c):
                half, m = divmod(c, NR)
                r = RM[m]
                act.wait_ge(r_mul, 2 * NR * u + c + 1 + 1)
                if c == 0:
                    act.wait_ge(down_mm, CT * u + 1)
                nc.scalar.activation(gtR[0:r, 0, m, half * HALF:(half + 1) * HALF], gbuf[c % 3][0:r, 0:HALF],
                                     ACT.Copy)\
                    .then_inc(r_hi, 1)

            act.wait_ge(a_done, NT)
            act.wait_ge(sq_mm, 8 * NG)
            scaled_q(0)
            for g in range(NG):
                for n in range(20 + 2 * g, 22 + 2 * g):
                    split_hi(n)
                if g:
                    transposed2(g - 1)
                if g + 1 < NG:
                    scaled_q(g + 1)
            shared(0)

            act.wait_ge(lg_ready, 1)
            nc.scalar.activation(sc[:, :, :], sc[:, :, :], ACT.Exp).then_inc(exp_ready, 1)
            shared(1)
            shared(2)
            expert_hi(0, 0, 0)
            expert_hi(0, 0, 1)
            shared(3)
            expert_hi(0, 0, 2)
            picked_hi(0, 0, range(CT))
            for i in range(2):
                act.wait_ge(s_out[i], 16 * NT // 2)
            act.wait_ge(loops_ready, 1)
            n = nc.scalar.value_load(loops[0:1, 0:1], min_val=E // 2, max_val=ROUNDS * E // 2)
            nc.scalar.preload_act_table(ACT.Silu)
            with act.Fori(0, n) as i:
                for par in range(2):
                    u = 2 * i + par
                    for c in range(2 * NR):
                        r_silu_of(u, par, c)
                        if c:
                            r_hi_of(u, par, c - 1)
                        if c in EW_AT:
                            expert_hi(u + 1, 1 - par, EW_AT[c])
                        for j in GB_AT[c]:
                            select_gb(u, par, j)
                        if c and ROWS_AT[c - 1]:
                            picked_hi(u + 1, 1 - par, ROWS_AT[c - 1])
                    r_hi_of(u, par, 2 * NR - 1)
                    picked_hi(u + 1, 1 - par, ROWS_AT[2 * NR - 1])
                    for j in GB_AT[-1]:
                        select_gb(u, par, j)

        @block.vector
        def _(dve):
            steps = [0]

            def link(ins):
                steps[0] += 1
                ins.then_inc(dve_step, 1)
                dve.wait_ge(dve_step, steps[0])

            def split_lo(n):
                i = SPLITS.index(PIECES[n])
                arrived(dve, n)
                dve.wait_ge(hi_done, i + 1)
                his = split_views(n, 0)
                for (dst, src), (hi, _) in zip(split_views(n, 1), his):
                    last = dve.tensor_tensor(dst, src, hi.bitcast(F32), ALU.subtract)
                last.then_inc(lo_done, 1)

            def mod_vector(i):
                w = MODS[i]
                row = mrow[:, :]
                src = bank[W_BANK][0:B, :]
                dve.wait_ge(mod_mm, 2 * (i - 2) + 2)
                if i > 2:
                    dve.wait_ge(mod_out, 16 * (i - 2))
                if w == "sb":
                    dve.tensor_copy(row, src).then_inc(mod_row, 1)
                elif w == "cb":
                    dve.tensor_scalar_add(row, src, 1.0).then_inc(mod_row, 1)
                else:
                    link(dve.tensor_copy(row, src))
                    link(dve.scalar_tensor_tensor(mabs, row, -1.0, row, ALU.mult, ALU.max))
                    dve.tensor_scalar(row, row, 0.0, 2.0, ALU.is_ge, ALU.mult)
                    link(dve.tensor_scalar_max(mabs, mabs, 0.25))
                    dve.scalar_tensor_tensor(row, row, -1.0, mabs, ALU.add, ALU.mult)\
                        .then_inc(mod_row, 1)

            def statistics(src):
                for j in range(GT):
                    last = dve.bn_stats(st6[:, j, :], src[:, j, :])
                link(last)
                for j in range(GT):
                    last = dve.bn_aggr(mv[:, j, :], st6[:, j, :])
                link(last)
                dve.tensor_scalar_add(ve[:, :], mv[:, :, 1], EPS).then_inc(ve_ready, 1)

            def norm_rows(j, dst, src):
                return dve.tensor_scalar(dst[:, j, :], src[:, j, :], mv[:, j, 0:1], rs[:, j:j + 1],
                                         ALU.subtract, ALU.mult)

            def x_statistics(g):
                for j in range(GT):
                    dve.wait_ge(x_in[g % 2 * GT + j], 16 * (g // 2 + 1))
                statistics(a1_rows[g % 2])

            def first_norm(g):
                b = g // (NG // B)
                dve.wait_ge(rs_ready, 2 * g + 1)
                if g:
                    dve.wait_ge(h_read, GT * g)
                for j in range(GT):
                    last = norm_rows(j, hx, a1_rows[g % 2])
                link(last)
                if g == 0:
                    dve.wait_ge(first_read, 2)
                if g == NG // B:
                    dve.wait_ge(first_read, 4)
                for j in range(GT):
                    last = dve.tensor_tensor(hx[:, j, :], hx[:, j, :], bc_c[:, b, :], ALU.mult)
                link(last)
                for j in range(GT):
                    dve.tensor_tensor(hx[:, j, :], hx[:, j, :], bc_s[:, b, :], ALU.add).then_inc(h_ready, 1)
                dve.wait_ge(h_ready, GT * (g + 1))
                statistics(hx)

            def second_norm(g):
                dve.wait_ge(rs_ready, 2 * g + 2)
                if g:
                    dve.wait_ge(t_mm, DC * g)
                for j in range(GT):
                    norm_rows(j, xn, hx).then_inc(xn_ready, 1)

            def transposed_lo(g):
                for k in range(DC):
                    dve.wait_ge(t_hi, DC * g + k + 1)
                    dve.tensor_tensor(xt[:, g, 1, k, :], atmp[:, k % 2, :], xt[:, g, 0, k, :].bitcast(F32),
                                      ALU.subtract).then_inc(t_lo, 1)

            def turn_k(g):
                at = slice((g * GN) % S, (g * GN) % S + GN)
                even, odd = kv_slot(g, 0, 0), kv_slot(g, 0, 1)
                dve.wait_ge(kv_copied, 8 * g + 2)
                dve.tensor_tensor(rk[:, 0, :], even, cos[:, at], ALU.mult)
                link(dve.tensor_tensor(rk[:, 1, :], odd, sin[:, at], ALU.mult))
                dve.tensor_tensor(even, even, sin[:, at], ALU.mult)
                link(dve.tensor_tensor(odd, odd, cos[:, at], ALU.mult))
                link(dve.tensor_tensor(odd, even, odd, ALU.add))
                link(dve.tensor_tensor(even, rk[:, 0, :], rk[:, 1, :], ALU.subtract))

            def product(g, m):
                if m < 2:
                    dve.wait_ge(v_turned, g + 1)
                else:
                    dve.wait_ge(kv_copied, 8 * g + 2 * m + 2)
                k = kv_slot(g, 0, m)
                dve.tensor_tensor(k, k, kv_slot(g, 1, m), ALU.mult).then_inc(prod, 1)

            def sum_products(g):
                dve.wait_ge(w_mm, g + 1)
                dve.wait_ge(prod, DC * (g + 1))
                for m in range(DC):
                    weighted = kv_slot(g, 0, m)
                    dve.tensor_tensor_reduce(out=weighted, in0=weighted,
                                             in1=bank[W_BANK][:, :], scale=1.0, scalar=0.0, op0=ALU.mult,
                                             op1=ALU.add, accum_out=a_part[:, g, m:m + 1]).then_inc(a_done, 1)

            def finish_a(b):
                n = NG // B
                dve.wait_ge(a_done, DC * n * (b + 1))
                link(dve.tensor_tensor(a_col[:, b, 0, :], a_part[:, n * b, :], a_part[:, n * b + 1, :], ALU.add))
                link(dve.tensor_scalar(a_col[:, b, 0, :], a_col[:, b, 0, :], 0.5, 0.5, ALU.mult, ALU.add))
                dve.tensor_tensor(a_col[:, b, 1, :], a_col[:, b, 0, :], b_col[:, 2, :], ALU.mult).then_inc(a_ready, 1)

            def first_vectors(b):
                dve.wait_ge(first_mm, 2 * b + 1)
                dve.tensor_copy(bc_s[:, b, :], bank[FIRST_BANKS[2 * b]][:, :]).then_inc(first_read, 1)
                dve.wait_ge(first_mm, 2 * b + 2)
                dve.tensor_scalar_add(bc_c[:, b, :], bank[FIRST_BANKS[2 * b + 1]][:, :], 1.0).then_inc(first_read, 1)

            x_statistics(0)
            first_vectors(0)
            first_norm(0)
            first_vectors(1)
            second_norm(0)
            x_statistics(1)
            transposed_lo(0)
            mod_vector(2)
            dve.wait_ge(lo_done, 4)
            dve.wait_ge(table_in, 16 * 3)
            for g in range(NG):
                if 0 < g < NG - 1:
                    x_statistics(g + 1)
                if g + 1 < NG:
                    first_norm(g + 1)
                if g:
                    sum_products(g - 1)
                if g == 2:
                    finish_a(0)
                turn_k(g)
                if g + 1 < NG:
                    second_norm(g + 1)
                product(g, 0)
                product(g, 1)
                product(g, 2)
                if g + 1 < NG:
                    transposed_lo(g + 1)
                else:
                    split_lo(16)
                    split_lo(17)
                product(g, 3)
                dve.wait_ge(sq_mm, 8 * (g + 1))
                if g:
                    dve.wait_ge(w_ready, g)
                dve.tensor_copy(nrm[:, :, :], bank[NORM_BANK][:, 0:2 * GT].rearrange("p (t k) -> p t k", k=2))\
                    .then_inc(nrm_ready, 1)
                if g < 3:
                    mod_vector(3 + g)
            sum_products(NG - 1)
            finish_a(1)
            split_lo(18)
            split_lo(19)

            def qa_lo_parts(g):
                for m in range(DC):
                    dve.wait_ge(qa_hi, DC * g + m + 1)
                    dve.tensor_tensor(qa[:, 1, m, :], tmp[:, m, :], qa[:, 0, m, :].bitcast(F32), ALU.subtract)\
                        .then_inc(qa_lo, 1)

            def residual(g):
                for j in range(GT):
                    t = GT * g + j
                    dve.wait_ge(y_mm, t + 1)
                    link(dve.tensor_tensor(ygate[:, j % 2, :], bank[Y_BANKS[t % GT]][:, :], bc_ga[:, g // (NG // B), :],
                                           ALU.mult))
                    dve.wait_ge(base_in[j], 16 * (g + 1))
                    dve.tensor_tensor(rows[:, j, :], rows[:, j, :], ygate[:, j % 2, :], ALU.add).then_inc(x2_ready, 1)
                dve.wait_ge(x2_ready, GT * (g + 1))
                statistics(rows)

            def ffn_norm(g):
                dve.wait_ge(rs_ready, 2 * NG + g + 1)
                if g:
                    dve.wait_ge(t2_mm, DC * g)
                    for j in range(GT):
                        dve.wait_ge(h2_out[j], 16 * g)
                for j in range(GT):
                    last = norm_rows(j, hx, rows)
                link(last)
                for j in range(GT):
                    dve.tensor_tensor(hx[:, j, :], hx[:, j, :], bc_c[:, g // (NG // B), :], ALU.mult)\
                        .then_inc(h2_half, 1)

            def transposed2_lo(g):
                for k in range(DC):
                    dve.wait_ge(t2_hi, DC * g + k + 1)
                    dve.tensor_tensor(xt[:, g, 1, k, :], tmp[:, k, :], xt[:, g, 0, k, :].bitcast(F32),
                                      ALU.subtract).then_inc(t2_lo, 1)

            def s_mul_of(g, m):
                n = NS * g + m
                r = SM[m]
                dve.wait_ge(s_silu, n + 1)
                up = bank[GATE_BANKS[m % 2]][r:P, :] if r == P // 2 else bank[UP_BANKS[m % 2]][0:r, :]
                dve.tensor_tensor(gbuf[n % 3][0:r, :], gbuf[n % 3][0:r, :], up, ALU.mult)\
                    .then_inc(s_mul, 1)

            def s_lo_of(g, m):
                n = NS * g + m
                r = SM[m]
                dve.wait_ge(s_hi, n + 1)
                dve.tensor_tensor(gtS[0:r, 1, m, :], gbuf[n % 3][0:r, :], gtS[0:r, 0, m, :].bitcast(F32), ALU.subtract)\
                    .then_inc(s_lo, 1)

            def shared(g):
                for m in range(NS):
                    if g == 0 and m == 4:
                        transposed2_lo(NG - 1)
                    s_mul_of(g, m)
                    if m:
                        s_lo_of(g, m - 1)
                    if g == 0 and m >= 3:
                        split_lo(25 + m)
                s_lo_of(g, NS - 1)

            def shared_rows(g, tiles=range(GT)):
                b = g // (NG // B)
                for j in tiles:
                    t = GT * g + j
                    dve.wait_ge(s_down_mm, t + 1)
                    link(dve.tensor_tensor(srow[:, t % 2, :], s_down_bank(t)[:, :], bc_gb[:, b, :], ALU.mult))
                    dve.wait_ge(x2_in[t % 2], 16 * (t // 2 + 1))
                    dve.tensor_tensor(xrow[:, t % 2, :], xrow[:, t % 2, :], srow[:, t % 2, :], ALU.add).then_inc(s_row, 1)

            full_e = [P, NT, E]

            def gate_scores():
                dve.wait_ge(lg_mm, NG)
                link(dve.tensor_copy(lg[:, :, :], bank[LG_BANK][:, 0:NT * E].rearrange("p (t e) -> p t e", e=E)))
                link(dve.tensor_reduce(mx[:, 0, :, 0], lg[:, :, :], AX.X, ALU.max))
                dve.tensor_tensor(sc[:, :, :], lg[:, :, :], mx[:, 0, :, :].to_broadcast(full_e), ALU.subtract)\
                    .then_inc(lg_ready, 1)

            def highest_score():
                dve.wait_ge(exp_ready, 1)
                dve.wait_ge(tab_ready, 1)
                link(dve.tensor_reduce(mx[:, 0, :, 0], sc[:, :, :], AX.X, ALU.add))
                link(dve.reciprocal(mx[:, 1, :, 0], mx[:, 0, :, 0]))
                link(dve.tensor_tensor(sc[:, :, :], sc[:, :, :], mx[:, 1, :, :].to_broadcast(full_e), ALU.mult))
                top(0)
                link(dve.scalar_tensor_tensor(sc[:, :, :], oh[:, 0, :, :], -2.0, sc[:, :, :], ALU.mult, ALU.add))

            def second_score():
                top(1)
                dve.tensor_tensor(both[:, :, :], oh[:, 0, :, :], oh[:, 1, :, :], ALU.add).then_inc(both_ready, 1)

            def top(k):
                link(dve.tensor_reduce(wt[:, k, :, 0], sc[:, :, :], AX.X, ALU.max))
                link(dve.tensor_tensor(eq[:, :, :], sc[:, :, :], wt[:, k, :, :].to_broadcast(full_e), ALU.is_equal))
                link(dve.tensor_tensor(eq[:, :, :], eq[:, :, :], iota8[:, :, :], ALU.mult))
                link(dve.tensor_reduce(ix[:, k, :, 0], eq[:, :, :], AX.X, ALU.min))
                link(dve.tensor_tensor(oh[:, k, :, :], iota8[:, :, :], ix[:, k, :, :].to_broadcast(full_e), ALU.is_equal))

            def slots():
                dve.wait_ge(rank_mm, 1)
                src = bank[LG_BANK][:, NT * E:3 * NT * E].rearrange("p (i t e) -> p i t e", i=2, e=E)
                dve.tensor_copy(within[:, :, :], src[:, 0, :, :])
                link(dve.tensor_copy(upto[:, 0, :, :], src[:, 1, :, :]))
                dve.tensor_copy(upto[:, 1, :, :], upto[:, 0, :, :]).then_inc(rank_read, 1)
                dve.wait_ge(rank_read, 1)
                at, step = 1, 1
                while step < NT:
                    dve.tensor_copy(upto[:, 3 - at, 0:step, :], upto[:, at, 0:step, :])
                    link(dve.tensor_tensor(upto[:, 3 - at, step:NT, :], upto[:, at, step:NT, :],
                                           upto[:, at, 0:NT - step, :], ALU.add))
                    at, step = 3 - at, 2 * step
                link(dve.tensor_reduce(cntf[:, 0:1], upto[:, at, NT - 1, :], AX.X, ALU.max))
                link(dve.tensor_single_scalar(cntf[:, 1:2], cntf[:, 0:1], float(CAP), ALU.is_gt))
                for r in range(2, ROUNDS):
                    link(dve.scalar_tensor_tensor(cntf[:, 1:2], cntf[:, 0:1], float(CAP * r), cntf[:, 1:2], ALU.is_gt, ALU.add))
                link(dve.tensor_scalar(cntf[:, 1:2], cntf[:, 1:2], E / 2, E / 2, ALU.mult, ALU.add))
                dve.tensor_copy(loops[:, :], cntf[:, 1:2]).then_inc(loops_ready, 1)
                link(dve.tensor_tensor(upto[:, 0, :, :], upto[:, at, :, :], upto[:, 0, :, :], ALU.subtract))
                link(dve.tensor_tensor(within[:, :, :], within[:, :, :], upto[:, 0, :, :], ALU.add))
                for k in range(2):
                    link(dve.tensor_tensor(upto[:, 1 + k, :, :], oh[:, k, :, :], within[:, :, :], ALU.mult))
                    link(dve.tensor_reduce(rr[:, k, :, 0], upto[:, 1 + k, :, :], AX.X, ALU.add))

                def flat(a):
                    return a[:, :, :, :].rearrange("p k t o -> p (k t o)")

                link(dve.tensor_single_scalar(flat(rd), flat(rr), float(CAP), ALU.is_ge))
                for r in range(2, ROUNDS):
                    link(dve.scalar_tensor_tensor(flat(rd), flat(rr), float(CAP * r), flat(rd), ALU.is_ge, ALU.add))
                link(dve.scalar_tensor_tensor(flat(rr), flat(rd), -float(CAP), flat(rr), ALU.mult, ALU.add))
                link(dve.tensor_single_scalar(flat(qq), flat(rr), float(P), ALU.is_ge))
                for r in range(2, CT):
                    link(dve.scalar_tensor_tensor(flat(qq), flat(rr), float(P * r), flat(qq), ALU.is_ge, ALU.add))
                link(dve.scalar_tensor_tensor(flat(rr), flat(qq), -float(P), flat(rr), ALU.mult, ALU.add))
                link(dve.tensor_scalar(flat(sl), flat(ix), float(CT), float(E * CT), ALU.mult, ALU.add))
                link(dve.scalar_tensor_tensor(flat(sl), flat(rd), float(E * CT), flat(sl), ALU.mult, ALU.add))
                link(dve.tensor_tensor(flat(sl), flat(sl), flat(qq), ALU.add))
                link(dve.scalar_tensor_tensor(flat(sl), flat(rr), float(COLS), flat(sl), ALU.mult, ALU.add))
                link(dve.tensor_copy(sidx[:, :], flat(sl)))
                dve.tensor_copy(rec[:, :, :, :].bitcast(F32)[:, :, :, 1], wt[:, :, :, 0]).then_inc(slots_ready, 1)

            def columns():
                dve.wait_ge(tab_in, 16)
                bits = tab[:, :, :].bitcast(F32)[:, :, 1]
                dve.tensor_scalar_min(gidx[:, :], tab[:, :, 0], T - 1)
                dve.scalar_tensor_tensor(w01[:, 0, :], tab[:, :, 0], float(S), bits, ALU.is_lt, ALU.mult)
                link(dve.scalar_tensor_tensor(w01[:, 1, :], tab[:, :, 0], float(S), bits, ALU.is_ge, ALU.mult))
                dve.drain().then_inc(cols_ready, 1)

            def expert_lo(w, par, q):
                lo, hi = EW_PART[q]
                slot = (par + q) % 2
                dve.wait_ge(ew_hi, 3 * w + q + 1)
                parts = [(P, lo, hi, 0)]
                if q == 2:
                    full = H // P * D
                    parts = [(P, lo, lo + full, 0), (RM[-1], lo + full, hi, full)]
                for r, a, z, at in parts:
                    last = dve.tensor_tensor(ew[par][0:r, 1, a:z], ewst[0:r, slot, at:at + z - a],
                                             ew[par][0:r, 0, a:z].bitcast(F32), ALU.subtract)
                last.then_inc(ew_lo, 1)

            def picked_lo(w, par, steps):
                for s in steps:
                    dve.wait_ge(rt_hi, CT * w + s + 1)
                    src = bank[RT_BANKS[(par + s) % 2]][:, :]
                    at = (slice(s, s + 1), slice(0, GN)) if s < DC else (slice(0, DC), slice(GN, CAP))
                    src = src.rearrange("p (k t) -> p k t", k=1 if s < DC else DC)
                    dve.tensor_tensor(ht[par][:, 1, at[0], at[1]], src, ht[par][:, 0, at[0], at[1]].bitcast(F32),
                                      ALU.subtract).then_inc(rt_lo, 1)

            def turn_columns(w, par):
                dve.tensor_copy(wc[:, par, :, :], w01[:, :, bass.ds(w * CT, CT)]).then_inc(wc_ready, 1)

            def select_gb(u, par, j):
                dve.wait_ge(gs_ready, CT * u + j + 1)
                dve.scalar_tensor_tensor(gsel[:, j, :], bc_gb[:, 0, :], wc[:, par, 0, j:j + 1], gsel[:, j, :],
                                         ALU.mult, ALU.add).then_inc(gsel_ready, 1)

            def r_mul_of(u, c):
                half, m = divmod(c, NR)
                r = RM[m]
                dve.wait_ge(r_silu, 2 * NR * u + c + 1)
                dve.tensor_tensor(gbuf[c % 3][0:r, 0:HALF], gbuf[c % 3][0:r, 0:HALF], bank[UP_BANKS[c % 2]][0:r, 0:HALF], ALU.mult)\
                    .then_inc(r_mul, 1)

            def r_lo_of(u, c):
                half, m = divmod(c, NR)
                r, at = RM[m], slice(half * HALF, (half + 1) * HALF)
                dve.wait_ge(r_hi, 2 * NR * u + c + 1)
                dve.tensor_tensor(gtR[0:r, 1, m, at], gbuf[c % 3][0:r, 0:HALF], gtR[0:r, 0, m, at].bitcast(F32), ALU.subtract)\
                    .then_inc(r_lo, 1)

            def expert_rows(u, j, par):
                dve.wait_ge(down_mm, CT * u + j + 1 + 1)
                dve.wait_ge(gsel_ready, CT * u + j + 1)
                if j == 0:
                    dve.wait_ge(added, u + 1)
                dve.tensor_tensor(y[:, j, :], bank[DOWN_BANKS[(par + j) % 2]][:, :], gsel[:, j, :], ALU.mult)\
                    .then_inc(y_ready, 1)

            qa_lo_parts(0)
            dve.wait_ge(bc_in[3], 16)
            dve.wait_ge(bc_in[4], 16)
            for g in range(NG):
                for n in range(20 + 2 * g, 22 + 2 * g):
                    split_lo(n)
                residual(g)
                if g:
                    transposed2_lo(g - 1)
                ffn_norm(g)
                if g + 1 < NG:
                    qa_lo_parts(g + 1)
            shared(0)

            gate_scores()
            dve.wait_ge(bc_in[5], 16)
            highest_score()
            shared_rows(0)
            second_score()
            shared(1)
            slots()
            shared_rows(1)
            shared(2)
            shared_rows(2)
            columns()
            expert_lo(0, 0, 0)
            expert_lo(0, 0, 1)
            shared(3)
            expert_lo(0, 0, 2)
            shared_rows(3, (0, 1))
            picked_lo(0, 0, range(CT))
            shared_rows(3, (2, 3))
            turn_columns(0, 0)
            for i in range(2):
                dve.wait_ge(s_out[i], 16 * NT // 2)
            dve.wait_ge(loops_ready, 1)
            n = nc.vector.value_load(loops[0:1, 0:1], min_val=E // 2, max_val=ROUNDS * E // 2)
            with dve.Fori(0, n) as i:
                for par in range(2):
                    u = 2 * i + par
                    for c in range(2 * NR):
                        r_mul_of(u, c)
                        if c:
                            r_lo_of(u, c - 1)
                        if c in EW_AT:
                            expert_lo(u + 1, 1 - par, EW_AT[c])
                        for j in GB_AT[c]:
                            select_gb(u, par, j)
                        if c and ROWS_AT[c - 1]:
                            picked_lo(u + 1, 1 - par, ROWS_AT[c - 1])
                    r_lo_of(u, 2 * NR - 1)
                    picked_lo(u + 1, 1 - par, ROWS_AT[2 * NR - 1])
                    for j in GB_AT[-1]:
                        select_gb(u, par, j)
                    turn_columns(u + 1, 1 - par)
                    for j in range(CT):
                        expert_rows(u, j, par)

        @block.tensor
        def _(pe):
            def product3(dst, a, b, first, last):
                nc.tensor.matmul(dst, a[0], b[0], start=first, stop=False)
                nc.tensor.matmul(dst, a[0], b[1], start=False, stop=False)
                return nc.tensor.matmul(dst, a[1], b[0], start=False, stop=last)

            def spread_matmul(b, i):
                for h in range(2):
                    n = PIECES.index((MODS[i], h))
                    arrived(pe, n)
                    for k in range(2):
                        last = nc.tensor.matmul(bank[FIRST_BANKS[2 * b + i]][:, :],
                                                scT[:, 2 * h + k, b:b + 1].to_broadcast([P, P]),
                                                piece_slot(n)[:, k * D:(k + 1) * D],
                                                start=h + k == 0, stop=h + k == 2)
                last.then_inc(first_mm, 1)

            def mod_matmul(i):
                w = MODS[i]
                if i > 2:
                    pe.wait_ge(mod_row, i - 2)
                if i > 3:
                    pe.wait_ge(a_done, DC * (i - 3))
                for h in range(2):
                    n = PIECES.index((w, h))
                    arrived(pe, n)
                    for k in range(2):
                        last = nc.tensor.matmul(bank[W_BANK][0:B, :], scT[:, 2 * h + k, :], piece_slot(n)[:, k * D:(k + 1) * D],
                                                start=h + k == 0, stop=h + k == 2)
                    last.then_inc(mod_mm, 1)

            def transposes(g, chunks=range(DC)):
                pe.wait_ge(xn_ready, GT * (g + 1))
                for k in chunks:
                    n = DC * g + k
                    if n >= 2:
                        pe.wait_ge(t_hi, n - 1)
                    for j in range(GT):
                        last = nc.tensor.transpose(bank[T_BANKS[k % 2]][:, j * P:(j + 1) * P],
                                                   xn[:, j, k * P:(k + 1) * P], ident[:, :])
                    last.then_inc(t_mm, 1)

            def kv_matmul(g, n):
                i, m = KV_ORDER[n]
                N = 8 * g + n
                if N >= 4:
                    pe.wait_ge(sq_ready, N - 3)
                for k in range(DC):
                    if n == 0:
                        pe.wait_ge(t_lo, DC * g + k + 1)
                    last = product3(bank[KV_BANKS[n % 4]][:, :],
                                    [wkv[:, s, i, k, m * P:(m + 1) * P] for s in range(2)],
                                    [xt[:, g, s, k, :] for s in range(2)], k == 0, k == DC - 1)
                last.then_inc(kv_mm, 1)

            def square_sums(g, n):
                i, m = KV_ORDER[n]
                pe.wait_ge(sq_ready, 8 * g + n + 1)
                if n == 0 and g:
                    pe.wait_ge(nrm_ready, g)
                for j in range(GT):
                    last = nc.tensor.matmul(bank[NORM_BANK][:, 2 * j + i:2 * j + i + 1], sq[:, n % 2, j * P:(j + 1) * P],
                                            ones[:, 0:1], start=n == 0 and j == 0, stop=n == 7 and j == GT - 1,
                                            skip_group_check=True)
                last.then_inc(sq_mm, 1)

            def spread_weights(g):
                pe.wait_ge(w_ready, g + 1)
                pe.wait_ge(mod_row, min(2 + g, 4))
                if g:
                    pe.wait_ge(a_done, DC * g)
                for j in range(GT):
                    last = nc.tensor.matmul(bank[W_BANK][:, j * P:(j + 1) * P], wtok[:, j:j + 1].to_broadcast([P, P]),
                                            ident[:, :], start=True, stop=True)
                last.then_inc(w_mm, 1)

            def q_matmul(g, chunks=range(DC)):
                for m in chunks:
                    n = DC * g + m
                    if n >= 3:
                        pe.wait_ge(qa_hi, n - 2)
                    for k in range(DC):
                        last = product3(bank[Q_BANKS[n % 3]][:, :], [wq[:, s, k, m * P:(m + 1) * P] for s in range(2)],
                                        [xt[:, g, s, k, :] for s in range(2)], k == 0, k == DC - 1)
                    last.then_inc(q_mm, 1)

            pe.wait_ge(consts, 4)
            pe.wait_ge(sc_ready, 1)
            for b in range(B):
                for i in range(2):
                    spread_matmul(b, i)
            mod_matmul(2)
            pe.wait_ge(first_read, 4)
            transposes(0)
            pe.wait_ge(lo_done, 4)
            for g in range(NG):
                for n in range(8):
                    kv_matmul(g, n)
                    if n == 1 and g:
                        spread_weights(g - 1)
                    if n == 7 and g + 1 < NG:
                        transposes(g + 1, (0, 1))
                    if n:
                        square_sums(g, n - 1)
                    if n == 7 and g + 1 < NG:
                        transposes(g + 1, (2, 3))
                if g < 3:
                    mod_matmul(3 + g)
                if g == NG - 1:
                    pe.wait_ge(lo_done, 6)
                    pe.wait_ge(sq_ready, 8 * NG)
                    q_matmul(0, range(3))
                square_sums(g, 7)
            spread_weights(NG - 1)
            q_matmul(0, range(3, DC))
            pe.wait_ge(lo_done, 8)

            def shared_gate_up(g, chunks=range(NS)):
                for m in chunks:
                    n, r = NS * g + m, SM[m]
                    if g == 0:
                        pe.wait_ge(t2_hi, (DC * (NG - 1) - 2 if m == 0 else DC * (NG - 1)) if m < NS - 1 else DC * NG)
                    if n >= 2:
                        pe.wait_ge(s_mul, n - 1)
                    if r == P // 2:
                        for k in range(DC):
                            last = product3(bank[GATE_BANKS[m % 2]][:, :], [sgu[:, s, k, m * P:UP_COL] for s in range(2)],
                                            [xt[:, g, s, k, :] for s in range(2)], k == 0, k == DC - 1)
                        last.then_inc(s_gu_mm, 1)
                        continue
                    for i, to in enumerate((GATE_BANKS, UP_BANKS)):
                        for k in range(DC):
                            last = product3(bank[to[m % 2]][0:r, :], [sgu[:, s, k, i * UP_COL + m * P:i * UP_COL + m * P + r]
                                                                for s in range(2)],
                                            [xt[:, g, s, k, :] for s in range(2)], k == 0, k == DC - 1)
                    last.then_inc(s_gu_mm, 1)

            def shared_down(g, pairs=range(GT // 2)):
                for pair in pairs:
                    for chunks in (range(NS - 1), range(NS - 1, NS)):
                        for j in (2 * pair, 2 * pair + 1):
                            t = GT * g + j
                            if chunks[0] == 0 and t >= 3:
                                pe.wait_ge(s_row, t - 2 if t < NT - GT else t - 1)
                            for m in chunks:
                                if j == 0 or m == NS - 1:
                                    pe.wait_ge(s_lo, NS * g + m + 1)
                                r = SM[m]
                                last = product3(s_down_bank(t)[:, :],
                                                [gtS[0:r, s, m, j * P:(j + 1) * P] for s in range(2)],
                                                [sd[0:r, s, m, :] for s in range(2)], m == 0, m == NS - 1)
                            if chunks[0]:
                                last.then_inc(s_down_mm, 1)

            def turn_rows(w, par, steps):
                for s in steps:
                    if s == 0:
                        pe.wait_ge(picked_in, 16 * CT * (w + 1))
                    if not isinstance(w, int) or s >= 2:
                        pe.wait_ge(rt_lo, CT * w + s - 1)
                    for i in range(DC):
                        j, k = (i, s) if s < DC else (DC, i)
                        last = nc.tensor.transpose(bank[RT_BANKS[(par + s) % 2]][:, i * P:(i + 1) * P],
                                                   picked[:, j, k * P:(k + 1) * P], ident[:, :])
                    last.then_inc(rt_mm, 1)

            def expert_gate_up(u, par):
                for c in range(2 * NR):
                    half, m = divmod(c, NR)
                    r, at = RM[m], slice(half * HALF, (half + 1) * HALF)
                    if c == 0:
                        pe.wait_ge(rt_lo, CT * u + CT)
                        pe.wait_ge(ew_lo, 3 * u + 2)
                    pe.wait_ge(r_mul, 2 * NR * u + max(c - 1, 0) + 1)
                    for i, to in enumerate((GATE_BANKS, UP_BANKS)):
                        for k in range(DC):
                            col = (i * DC + k) * H + m * P
                            last = product3(bank[to[c % 2]][0:r, 0:HALF], [ew[par][:, s, col:col + r] for s in range(2)],
                                            [ht[par][:, s, k, at] for s in range(2)], k == 0, k == DC - 1)
                    last.then_inc(gu_mm, 1)
                    turn_rows(u + 1, 1 - par, ROWS_AT[c])

            def expert_down(u, par):
                pe.wait_ge(ew_lo, 3 * u + 3)
                for j in range(CT):
                    if j == 0:
                        pe.wait_ge(r_lo, 2 * NR * u + NR + 1)
                    if j == 2:
                        pe.wait_ge(r_lo, 2 * NR * (u + 1) + 1)
                    pe.wait_ge(y_ready, CT * u + max(j - 1, 0) + 1)
                    for m in range(NR):
                        r, col = RM[m], 2 * DC * H + m * D
                        last = product3(bank[DOWN_BANKS[(par + j) % 2]][:, :],
                                        [gtR[0:r, s, m, j * P:(j + 1) * P] for s in range(2)],
                                        [ew[par][0:r, s, col:col + D] for s in range(2)], m == 0, m == NR - 1)
                    last.then_inc(down_mm, 1)

            def y_matmul(g):
                for pair in range(GT // 2):
                    for chunks in (range(DC - 1), range(DC - 1, DC)):
                        for j in (2 * pair, 2 * pair + 1):
                            t = GT * g + j
                            if chunks[0] == 0 and t >= GT:
                                pe.wait_ge(x2_ready, t - GT + 1)
                            if chunks[0] == 0 and g >= 2 and j >= 2:
                                pe.wait_ge(t2_hi, DC * (g - 2) + j + 1)
                            for m in chunks:
                                if j == 0 or m == DC - 1:
                                    pe.wait_ge(qa_lo, DC * g + m + 1)
                                last = product3(bank[Y_BANKS[t % GT]][:, :], [qa[:, s, m, j * P:(j + 1) * P] for s in range(2)],
                                                [wo[:, s, m, :] for s in range(2)], m == 0, m == DC - 1)
                            if chunks[0]:
                                last.then_inc(y_mm, 1)

            def transposes2(g):
                pe.wait_ge(h2_ready, GT * (g + 1))
                for k in range(DC):
                    if k >= 2 and g + 1 < NG:
                        pe.wait_ge(x2_ready, GT * (g + 1) + k + 1)
                    if g + 1 == NG:
                        pe.wait_ge(x2_ready, NT)
                        if k == DC - 1:
                            pe.wait_ge(s_mul, 4)
                    for j in range(GT):
                        last = nc.tensor.transpose(t2_bank(g, k)[:, j * P:(j + 1) * P],
                                                   hx[:, j, k * P:(k + 1) * P], ident[:, :])
                    last.then_inc(t2_mm, 1)

            def gate_logits(g):
                pe.wait_ge(t2_hi, DC * (g + 1))
                for j in range(GT):
                    t = GT * g + j
                    for k in range(DC):
                        last = nc.tensor.matmul(bank[LG_BANK][:, t * E:(t + 1) * E], tmp[:, k, j * P:(j + 1) * P],
                                                gw[:, k, :], start=k == 0, stop=k == DC - 1)
                last.then_inc(lg_mm, 1)

            for g in range(NG):
                y_matmul(g)
                if g:
                    transposes2(g - 1)
                if g + 1 < NG:
                    q_matmul(g + 1, (0,))
                else:
                    pe.wait_ge(lo_done, SPLITS.index(("sup", DC - 1)) + 1)
                    shared_gate_up(0, (0,))
                if g:
                    gate_logits(g - 1)
                if g + 1 < NG:
                    q_matmul(g + 1, range(1, DC))
            shared_gate_up(0, range(1, 4))
            transposes2(NG - 1)
            shared_gate_up(0, range(4, NS))
            gate_logits(NG - 1)

            pe.wait_ge(lo_done, len(SPLITS))
            for g in range(NG):
                if g:
                    if g == NG - 1:
                        pe.wait_ge(t2_lo, NT)
                    shared_gate_up(g)
                if g == 1:
                    pe.wait_ge(both_ready, 1)
                    for i, lhs in enumerate((upper, ones)):
                        last = nc.tensor.matmul(bank[LG_BANK][:, (1 + i) * NT * E:(2 + i) * NT * E], lhs[:, :],
                                                both[:, :, :].rearrange("p t e -> p (t e)"), start=True, stop=True)
                    last.then_inc(rank_mm, 1)
                if g + 1 < NG:
                    shared_down(g)
            shared_down(NG - 1, (0,))
            pe.wait_ge(rank_read, 1)
            turn_rows(0, 0, range(CT))
            shared_down(NG - 1, (1,))
            pe.wait_ge(loops_ready, 1)
            n = nc.tensor.value_load(loops[0:1, 0:1], min_val=E // 2, max_val=ROUNDS * E // 2)
            with pe.Fori(0, n) as i:
                for par in range(2):
                    u = 2 * i + par
                    expert_gate_up(u, par)
                    expert_down(u, par)


_INS = ['L0_attn_X', 'L0_attn_W_in', 'L0_attn_b_in', 'L0_attn_W_out', 'L0_attn_b_out', 'L0_attn_gamma',
        'L0_attn_beta', 'L0_ffn_gate_w', 'L0_ffn_w_gate', 'L0_ffn_w_up', 'L0_ffn_w_down', 'L0_ffn_sw_gate',
        'L0_ffn_sw_up', 'L0_ffn_sw_down', 'L0_c', 'L0_wmod']


def rotary_tables():
    inv = np.float32(1.0) / np.float32(10000.0) ** (np.arange(0, ROT, 2, dtype=np.float32) / np.float32(ROT))
    angle = (np.arange(S, dtype=np.float32)[:, None] * inv[None, :].astype(np.float32)).T
    return np.ascontiguousarray(np.cos(angle)), np.ascontiguousarray(np.sin(angle))


def kernel(**inputs):
    import concourse.bacc as bacc
    from concourse.bass_utils import run_bass_kernel_spmd as run

    nc = bacc.Bacc("TRN2", target_bir_lowering=False, num_devices=1)
    arrays, args = {}, []

    def give(name, a):
        a = np.ascontiguousarray(a)
        arrays[name] = a
        args.append(nc.dram_tensor(name, a.shape, mybir.dt.from_np(a.dtype), kind="ExternalInput").ap())

    for name in _INS:
        a = np.asarray(inputs[name])
        give("in_" + name, a.reshape(T, D) if name == 'L0_attn_X' else a)
    for name, a in zip(("cos_table", "sin_table"), rotary_tables()):
        give(name, a)
    args.append(nc.dram_tensor("out_rows", (T + CAP, D), F32, kind="ExternalOutput").ap())
    build(nc, *args)
    r = run(nc, [arrays], core_ids=[0])
    return r.results[0]["out_rows"][:T].reshape(B, S, D)
```
